# Optimizing a Trainium2 kernel written in Bass

```python
import numpy as np
import jax
import jax.numpy as jnp

def _softmax(x, axis=-1):
    return jax.nn.softmax(x, axis=axis)

def _gelu(x):
    return jax.nn.gelu(x, approximate=True)

def _silu(x):
    return jax.nn.silu(x)

def _sigmoid(x):
    return jax.nn.sigmoid(x)

def _layernorm(x, axis=-1, eps=1e-05):
    m = jnp.mean(x, axis=axis, keepdims=True)
    v = jnp.var(x, axis=axis, keepdims=True)
    return (x - m) / jnp.sqrt(v + eps)

def _scatter_add(tgt, idx, src, axis=0):
    return tgt.at[idx].add(src)

def _segment_sum(src, seg, n):
    return jax.ops.segment_sum(src, seg, n)
kernel_name = 'mk_adaln_d1_jaxref_r4_9c84b6'

def setup_inputs(seed: int=0):
    np.random.seed(seed)
    _w = jnp.asarray

    def _L0_attn_setup():
        import jax, jax.numpy as jnp
        import numpy as np
        ROPE_THETA = 10000.0

        def rope(t, rot_dim):
            S = t.shape[-2]
            half = rot_dim // 2
            inv_freq = 1.0 / ROPE_THETA ** (jnp.arange(0, rot_dim, 2, dtype=jnp.float32) / rot_dim)
            freqs = jnp.arange(S, dtype=jnp.float32)[:, None] * inv_freq[None, :]
            freqs = jnp.repeat(freqs, 2, axis=-1)
            cos, sin = (jnp.cos(freqs), jnp.sin(freqs))
            t_rot, t_pass = (t[..., :rot_dim], t[..., rot_dim:])
            x = t_rot.reshape(*t_rot.shape[:-1], half, 2)
            rh = jnp.stack([-x[..., 1], x[..., 0]], axis=-1).reshape(t_rot.shape)
            t_rot = t_rot * cos + rh * sin
            return jnp.concatenate([t_rot, t_pass], axis=-1)

        def feature_map(x):
            norm = jnp.sqrt(jnp.sum(x * x, axis=-1, keepdims=True))
            return x / jnp.maximum(norm, 1e-12)
        key = jax.random.key(seed)
        kx, kwi, kwo = jax.random.split(key, 3)
        B, S, D = (8, 1024, 512)
        scale = 0.02
        return {'X': jax.random.normal(kx, (B, S, D), dtype=jnp.float32), 'W_in': jax.random.normal(kwi, (3 * D, D), dtype=jnp.float32) * scale, 'b_in': jnp.zeros((3 * D,), dtype=jnp.float32), 'W_out': jax.random.normal(kwo, (D, D), dtype=jnp.float32) * scale, 'b_out': jnp.zeros((D,), dtype=jnp.float32)}
    _L0_attn_in = _L0_attn_setup()

    def _L0_ffn_setup():
        import jax, jax.numpy as jnp
        import numpy as np
        H = 512
        E = 64
        I = 128
        SI = 128
        TOP_K = 8
        B, T = (2, 128)
        key = jax.random.key(seed)
        ks = jax.random.split(key, 8)
        s = 0.02
        return {'h': jax.random.normal(ks[0], (B, T, H), jnp.float32), 'gate_w': jax.random.normal(ks[1], (E, H), jnp.float32) * s, 'gu_w': jax.random.normal(ks[2], (E, 2 * I, H), jnp.float32) * s, 'dp_w': jax.random.normal(ks[3], (E, H, I), jnp.float32) * s, 'sh_gate_w': jax.random.normal(ks[4], (SI, H), jnp.float32) * s, 'sh_up_w': jax.random.normal(ks[5], (SI, H), jnp.float32) * s, 'sh_down_w': jax.random.normal(ks[6], (H, SI), jnp.float32) * s, 'sh_gate1_w': jax.random.normal(ks[7], (1, H), jnp.float32) * s}
    _L0_ffn_in = _L0_ffn_setup()
    _L0_c = _w((lambda *s: np.random.randn(*s).astype(np.float32) * 0.05)(4, 512))
    _L0_wmod = _w((lambda *s: np.random.randn(*s).astype(np.float32) * 0.05)(512, 6 * 512) * 512 ** (-0.5))
    _d = {'L0_attn_X': _L0_attn_in['X'], 'L0_attn_W_in': _L0_attn_in['W_in'], 'L0_attn_b_in': _L0_attn_in['b_in'], 'L0_attn_W_out': _L0_attn_in['W_out'], 'L0_attn_b_out': _L0_attn_in['b_out'], 'L0_ffn_gate_w': _L0_ffn_in['gate_w'], 'L0_ffn_gu_w': _L0_ffn_in['gu_w'], 'L0_ffn_dp_w': _L0_ffn_in['dp_w'], 'L0_ffn_sh_gate_w': _L0_ffn_in['sh_gate_w'], 'L0_ffn_sh_up_w': _L0_ffn_in['sh_up_w'], 'L0_ffn_sh_down_w': _L0_ffn_in['sh_down_w'], 'L0_ffn_sh_gate1_w': _L0_ffn_in['sh_gate1_w'], 'L0_c': _L0_c, 'L0_wmod': _L0_wmod}
    _x0 = _d['L0_attn_X']
    _d['L0_attn_X'] = jax.random.normal(jax.random.fold_in(jax.random.key(seed), 1), (4, 512, 512), dtype=_x0.dtype)
    del _x0
    return _d

def reference(L0_attn_X, L0_attn_W_in, L0_attn_b_in, L0_attn_W_out, L0_attn_b_out, L0_ffn_gate_w, L0_ffn_gu_w, L0_ffn_dp_w, L0_ffn_sh_gate_w, L0_ffn_sh_up_w, L0_ffn_sh_down_w, L0_ffn_sh_gate1_w, L0_c, L0_wmod):

    def _L0_attn_ref(X, W_in, b_in, W_out, b_out):
        import jax, jax.numpy as jnp
        import numpy as np
        ROPE_THETA = 10000.0

        def rope(t, rot_dim):
            S = t.shape[-2]
            half = rot_dim // 2
            inv_freq = 1.0 / ROPE_THETA ** (jnp.arange(0, rot_dim, 2, dtype=jnp.float32) / rot_dim)
            freqs = jnp.arange(S, dtype=jnp.float32)[:, None] * inv_freq[None, :]
            freqs = jnp.repeat(freqs, 2, axis=-1)
            cos, sin = (jnp.cos(freqs), jnp.sin(freqs))
            t_rot, t_pass = (t[..., :rot_dim], t[..., rot_dim:])
            x = t_rot.reshape(*t_rot.shape[:-1], half, 2)
            rh = jnp.stack([-x[..., 1], x[..., 0]], axis=-1).reshape(t_rot.shape)
            t_rot = t_rot * cos + rh * sin
            return jnp.concatenate([t_rot, t_pass], axis=-1)

        def feature_map(x):
            norm = jnp.sqrt(jnp.sum(x * x, axis=-1, keepdims=True))
            return x / jnp.maximum(norm, 1e-12)
        D = X.shape[-1]
        QKV = jnp.einsum('bsd,ed->bse', X, W_in) + b_in
        Q, K, V = jnp.split(QKV, 3, axis=-1)
        rot_dim = D // 2
        Q = rope(Q, rot_dim)
        K = rope(K, rot_dim)
        A = jnp.sum(feature_map(K) * V, axis=-2)
        Y = A[:, None, :] * Q
        Y = jnp.einsum('bsd,ed->bse', Y, W_out) + b_out
        return Y + X

    def _L0_ffn_ref(h, gate_w, gu_w, dp_w, sh_gate_w, sh_up_w, sh_down_w, sh_gate1_w):
        import jax, jax.numpy as jnp
        import numpy as np
        H = 512
        E = 64
        I = 128
        SI = 128
        TOP_K = 8
        B, T = (2, 128)
        Bb, Tt, Hh = h.shape
        x = h.reshape(Bb * Tt, Hh)
        N = x.shape[0]
        logits = x @ gate_w.T
        topv, topi = jax.lax.top_k(logits, TOP_K)
        rw = jax.nn.softmax(topv.astype(jnp.float32), axis=-1).astype(x.dtype)
        W = jnp.zeros((N, E), x.dtype).at[jnp.arange(N)[:, None], topi].set(rw)
        gu = jnp.einsum('nh,eih->nei', x, gu_w)
        gate, up = (gu[..., :I], gu[..., I:])
        inter = jax.nn.silu(gate) * up
        inter_w = inter * W[:, :, None]
        out = jnp.einsum('nei,ehi->nh', inter_w, dp_w)
        sh_inter = jax.nn.silu(x @ sh_gate_w.T) * (x @ sh_up_w.T)
        sh_out = sh_inter @ sh_down_w.T
        sh_g = jax.nn.sigmoid(x @ sh_gate1_w.T)
        out = out + sh_g * sh_out
        return out.reshape(Bb, Tt, Hh)
    x = L0_attn_X
    mod = (_silu(L0_c) @ L0_wmod).reshape(L0_c.shape[0], 6, 1, -1)
    sa, ca, ga, sb, cb, gb = (mod[:, 0], mod[:, 1], mod[:, 2], mod[:, 3], mod[:, 4], mod[:, 5])
    ga = (2 * (ga >= 0) - 1) * jnp.maximum(jnp.abs(ga), 0.25)
    gb = (2 * (gb >= 0) - 1) * jnp.maximum(jnp.abs(gb), 0.25)
    h = _layernorm(x, axis=-1) * (1 + ca) + sa
    x = x + ga * _L0_attn_ref(h, L0_attn_W_in, L0_attn_b_in, L0_attn_W_out, L0_attn_b_out)
    h = _layernorm(x, axis=-1) * (1 + cb) + sb
    x = x + gb * _L0_ffn_ref(h, L0_ffn_gate_w, L0_ffn_gu_w, L0_ffn_dp_w, L0_ffn_sh_gate_w, L0_ffn_sh_up_w, L0_ffn_sh_down_w, L0_ffn_sh_gate1_w)
    return x

_drawn_inputs = setup_inputs


def setup_inputs(seed=0):
    import zlib

    import numpy as np

    out = dict(_drawn_inputs(seed))
    spreads = {'L0_attn_b_in': (0.0, 0.312), 'L0_attn_b_out': (0.0, 0.35)}
    factors = {'L0_ffn_gate_w': 8.0,
     'L0_ffn_gu_w': 8.0,
     'L0_ffn_dp_w': 8.0,
     'L0_ffn_sh_gate_w': 8.0,
     'L0_ffn_sh_up_w': 8.0,
     'L0_ffn_sh_down_w': 8.0,
     'L0_ffn_sh_gate1_w': 8.0}
    for name, (base, spread) in spreads.items():
        noise = np.random.default_rng([zlib.crc32(name.encode()), seed]).standard_normal(out[name].shape)
        drawn = base * np.exp(spread * noise) if base else spread * noise
        out[name] = jnp.asarray(drawn.astype(out[name].dtype))
    for name, factor in factors.items():
        out[name] = (out[name] * factor).astype(out[name].dtype)
    return out
```

```python
from contextlib import ExitStack

import numpy as np

import concourse.bass as bass
from concourse import mybir

ALU = mybir.AluOpType
ACT = mybir.ActivationFunctionType
F32 = mybir.dt.float32
BF16 = mybir.dt.bfloat16
I32 = mybir.dt.int32
U32 = mybir.dt.uint32

P = 128
BATCH = 4
SEQ = 512
D = 512
KC = D // P
TPB = SEQ // P
TOKENS = BATCH * SEQ
TILES = TOKENS // P
ROT = D // 2
HALF = ROT // 2
EXPERTS = 64
TOPK = 8
INNER = 128
EV = EXPERTS + 1
GU = 2 * INNER
WROW = KC * GU + D
WSLOTS = 4
SLOT_COLS = TOKENS // P
PAD_ID = TOKENS
ROWS = TOKENS + P
EXPERT_TILES = TOKENS * TOPK // P + EXPERTS
FLAT = TILES + EXPERT_TILES
ROUND = 4
SHARED_ROUNDS = TILES // ROUND
ROUNDS = FLAT // ROUND
DUMMY_COL = EV * SLOT_COLS
NMOD = 6
MODC = NMOD * KC
LN_EPS = 1e-5
NEG = -3.0e38

C_ID, C_TRI, C_TRI65, C_IOTA, C_FLAT = 0, 128, 256, 256 + EV, 256 + EV + EXPERTS
C_TOK = C_FLAT + FLAT
CONSTS = C_TOK + TILES


class Tally:

    def __init__(self, sem, start=0):
        self.sem, self.start, self.n = sem, start, 0

    def mark(self, ins):
        ins.then_inc(self.sem, 1)
        self.n += 1
        return self.start + self.n


def build(nc, x_in, w_in, b_col, b_row, w_out, bout_col, gates, experts, c_t, w_mod, tables, rope_rows,
          rope_cols, out):
    slots = nc.dram_tensor("slot_table", [P * EXPERTS * SLOT_COLS, 2], I32)
    h2_rows = nc.dram_tensor("h2_rows", [ROWS, D], F32)
    acc = [nc.dram_tensor(f"ffn_sum{i}", [ROWS, D], F32) for i in range(2)]
    mod_rows = nc.dram_tensor("mod_rows", [MODC * BATCH, P], F32)

    ctx = ExitStack()
    with ctx:
        def sb(name, shape, dt=F32):
            return ctx.enter_context(nc.sbuf_tensor(name, shape, dt))

        def sem(name):
            return ctx.enter_context(nc.semaphore(name))

        x = sb("x", [P, TILES * D])
        front = sb("front", [P, KC * NMOD * D])
        wmod = front[:, :].rearrange("p (k m) -> p k m", k=KC)
        region = [front[:, i * 2048:(i + 1) * 2048] for i in range(6)]
        hT = region[0].rearrange("p (k s) -> p k s", k=KC)
        qT = region[1].rearrange("p (k s) -> p k s", k=KC)
        woa = region[2].rearrange("p (k s) -> p k s", k=KC)
        kv = region[3].rearrange("p (i d) -> p i d", i=TPB)
        kb, vb, rope_t, pool_t = (region[4][:, i * D:(i + 1) * D] for i in range(4))
        square_junk = region[5][:, 0:D]
        rope_q = [region[5][:, D:2 * D], region[5][:, 2 * D:3 * D]]
        h2_t = region[5][:, 3 * D:4 * D]
        wqkv = sb("wqkv", [P, KC * 3 * D])
        win = wqkv[:, :].rearrange("p (k e) -> p k e", k=KC)
        wo = sb("wo", [P, KC, D])
        kcos = sb("kcos", [P, TPB, ROT])
        ksin = sb("ksin", [P, TPB, ROT])
        qcos = sb("qcos", [P, SEQ])
        qsin = sb("qsin", [P, SEQ])
        bias_kv = sb("bias_kv", [P, 2, D])
        xn = sb("xn", [P, TPB, D])
        h2 = sb("h2", [P, TPB, D])
        h2T = sb("h2T", [P, KC, SEQ])
        rows_a = sb("rows_a", [P, 3, D])
        rows_b = sb("rows_b", [P, 2, D])
        rows_g = sb("rows_g", [P, BATCH, D])
        gate_w = sb("gate_w", [P, KC, EV])
        const = sb("const", [P, CONSTS])
        ident = const[:, C_ID:C_ID + P]
        tri_bf = sb("tri_bf", [P, P], BF16)
        ones_bf = sb("ones_bf", [P, P], BF16)
        ones1 = sb("ones1", [P, 1])
        tbl = sb("tbl", [P, DUMMY_COL + 1, 2], I32)
        bqc = sb("bqc", [P, KC])
        boc = sb("boc", [P, KC * BATCH])
        cT = sb("cT", [P, KC * BATCH])
        silu_c = sb("silu_c", [P, KC * BATCH])
        modc = sb("modc", [P, MODC * BATCH])
        modf = sb("modf", [P, MODC * BATCH])
        modr = sb("modr", [MODC * BATCH, P])
        scale_a = sb("scale_a", [P, KC * BATCH])
        mod_t = sb("mod_t", [P, 3, KC * BATCH])
        stats = sb("stats", [P, TPB, 6])
        mean_var = sb("mean_var", [P, TPB, 2])
        rstd = sb("rstd", [P, TPB])
        shift = sb("shift", [P, TPB])
        stats2 = sb("stats2", [P, TPB, 6])
        mean_var2 = sb("mean_var2", [P, TPB, 2])
        rstd2 = sb("rstd2", [P, TPB])
        shift2 = sb("shift2", [P, TPB])
        ksq = sb("ksq", [P, TPB])
        krn = sb("krn", [P, TPB])
        var = sb("var", [P, 3, TPB])
        root = sb("root", [P, 3, TPB])
        corr = sb("corr", [P, 3, TPB])
        asum = sb("asum", [P, KC])
        logit = sb("logit", [P, TPB, EV])
        topv = sb("topv", [P, TPB, TOPK])
        topi = sb("topi", [P, TPB, TOPK], U32)
        topif = sb("topif", [P, TPB, TOPK])
        ntop = sb("ntop", [P, TPB])
        replaced = sb("replaced", [P, TPB, EXPERTS])
        mask = sb("mask", [P, TPB, EV], BF16)
        seen = sb("seen", [P, TPB + 1, EV], BF16)
        etop = sb("etop", [P, TPB, TOPK])
        esum = sb("esum", [P, TPB])
        esh = sb("esh", [P, TPB])
        rsum = sb("rsum", [P, TPB])
        sh1 = sb("sh1", [P, TPB])
        gate_sh = sb("gate_sh", [P, TILES])
        rank_all = sb("rank_all", [P, TPB, EV])
        pick = sb("pick", [P, TOPK, EXPERTS])
        rank_f = sb("rank_f", [P, TPB, TOPK])
        rank_i = sb("rank_i", [P, TPB, TOPK], I32)
        idx_i = sb("idx_i", [P, TPB, TOPK], I32)
        place_r = sb("place_r", [P, TPB, TOPK], I32)
        place_q = sb("place_q", [P, TPB, TOPK], I32)
        place_e = sb("place_e", [P, TPB, TOPK], I32)
        place = sb("place", [P, TPB, TOPK], I32)
        pay = sb("pay", [P, TPB, TOPK, 2], I32)
        zero8 = sb("zero8", [P, TOPK])
        zrow = sb("zrow", [P, D])
        count_f = sb("count_f", [EV, 1])
        count_i = sb("count_i", [EV, 1], I32)
        tiles_i = sb("tiles_i", [EV, 1], I32)
        tiles_f = sb("tiles_f", [EV, 1])
        col_step = sb("col_step", [EV, 1])
        cum = sb("cum", [EV, 1])
        past = sb("past", [EV, FLAT])
        plan_f = sb("plan_f", [1, 3, FLAT])
        plan_w = sb("plan_w", [1, 2, FLAT], I32)
        plan = sb("plan", [1, 3, FLAT], I32)
        cum_i = sb("cum_i", [1, EV], I32)
        xg = [xn[:, i, :] for i in range(4)]
        ids = [sb(f"ids{i}", [P, 2], I32) for i in range(4)]
        xT = [h2T[:, 2 + i, :].rearrange("p (k t) -> p k t", k=KC) for i in range(2)]
        act = [sb(f"act{i}", [P, INNER]) for i in range(2)]
        inter = [sb(f"inter{i}", [P, INNER]) for i in range(2)]
        iT = [sb(f"iT{i}", [P, P]) for i in range(2)]
        yb = [h2T[:, i, :] for i in range(2)]
        fa = [region[0].rearrange("p (i d) -> p i d", i=TPB), region[1].rearrange("p (i d) -> p i d", i=TPB)]
        fb = [region[2].rearrange("p (i d) -> p i d", i=TPB), region[3].rearrange("p (i d) -> p i d", i=TPB)]

        bank = [ctx.enter_context(nc.psum_tensor(f"bank{i}", [P, 512], F32)) for i in range(8)]

        s_const = sem("s_const")
        s_small = sem("s_small")
        s_wmod = sem("s_wmod")
        s_x0 = sem("s_x0")
        s_xrest = sem("s_xrest")
        s_win = sem("s_win")
        s_att = sem("s_att")
        s_modw = sem("s_modw")
        s_rows_a = sem("s_rows_a")
        s_rows_b = sem("s_rows_b")
        s_rows_g = sem("s_rows_g")
        s_zero = sem("s_zero")
        s_prefill = sem("s_prefill")
        s_h2w = sem("s_h2w")
        s_scat = sem("s_scat")
        s_tbl = sem("s_tbl")
        s_fill = sem("s_fill")
        s_silu = sem("s_silu")
        s_mod = sem("s_mod")
        s_modv = sem("s_modv")
        s_modT = sem("s_modT")
        s_modr = sem("s_modr")
        s_cst = sem("s_cst")
        s_v = sem("s_v")
        s_vl = sem("s_vl")
        s_va = sem("s_va")
        s_vb = sem("s_vb")
        s_vc = sem("s_vc")
        s_mv = sem("s_mv")
        s_var = [sem(f"s_var{i}") for i in range(3)]
        s_root = [sem(f"s_root{i}") for i in range(3)]
        s_xn = sem("s_xn")
        s_pres = sem("s_pres")
        s_res = sem("s_res")
        s_tpA = sem("s_tpA")
        s_hT = sem("s_hT")
        s_kv = sem("s_kv")
        s_kvr = sem("s_kvr")
        s_kro = sem("s_kro")
        s_ksq = sem("s_ksq")
        s_kvp = sem("s_kvp")
        s_rn = sem("s_rn")
        s_q = sem("s_q")
        s_qT = sem("s_qT")
        s_qro = sem("s_qro")
        s_as = sem("s_as")
        s_woa = sem("s_woa")
        s_o = sem("s_o")
        s_or = sem("s_or")
        s_mv2 = sem("s_mv2")
        s_xn2 = sem("s_xn2")
        s_h2m = sem("s_h2m")
        s_h2 = sem("s_h2")
        s_tpC = sem("s_tpC")
        s_h2T = sem("s_h2T")
        s_g = sem("s_g")
        s_gr = sem("s_gr")
        s_top = sem("s_top")
        s_ex = sem("s_ex")
        s_mask = sem("s_mask")
        s_rk = sem("s_rk")
        s_place = sem("s_place")
        s_cnt = sem("s_cnt")
        s_ntile = sem("s_ntile")
        s_cum = sem("s_cum")
        s_past = sem("s_past")
        s_flat = sem("s_flat")
        s_plan = sem("s_plan")
        s_w = sem("s_w")
        s_xs = [sem(f"s_xs{i}") for i in range(4)]
        s_xg = [sem(f"s_xg{i}") for i in range(4)]
        s_ids = sem("s_ids")
        s_T = sem("s_T")
        s_xT = sem("s_xT")
        s_G = sem("s_G")
        s_sl = sem("s_sl")
        s_in = sem("s_in")
        s_I = sem("s_I")
        s_iT = sem("s_iT")
        s_d = sem("s_d")
        s_y = sem("s_y")
        s_ss = [sem("s_ss0"), sem("s_ss1")]
        s_sc = [sem("s_sc0"), sem("s_sc1")]
        s_fl = [sem("s_fl0"), sem("s_fl1")]
        s_fs = sem("s_fs")
        s_fm = sem("s_fm")
        s_fo = sem("s_fo")
        s_out = sem("s_out")

        x_view = x_in.rearrange("(b i p) d -> b p i d", i=TPB, p=P)
        out_view = out.rearrange("(b i p) d -> b p i d", i=TPB, p=P)
        x_tiles = x[:, :].rearrange("p (g d) -> p g d", g=TILES)
        h2_view = h2_rows[0:TOKENS, :].rearrange("(b i p) d -> b p i d", i=TPB, p=P)
        h2_tile = h2_rows[0:TOKENS, :].rearrange("(g p) d -> g p d", p=P)
        acc_tile = [a[0:TOKENS, :].rearrange("(g p) d -> g p d", p=P) for a in acc]
        acc_view = [a[0:TOKENS, :].rearrange("(b i p) d -> b p i d", i=TPB, p=P) for a in acc]
        mod_view = mod_rows[:, :].rearrange("(m c b) f -> m b c f", m=NMOD, b=BATCH)
        ex_view = experts

        def x_at(g):
            return x[:, bass.ds(g * D, D)]

        def mod_row(m, b):
            v = mod_view[m, bass.ds(b, 1), :, :].rearrange("o c f -> (o c) f")
            return v.unsqueeze(0).to_broadcast([P, KC, P])

        def apart(eng):
            eng.nop(nofuse=True)

        block = ctx.enter_context(nc.Block())

        @block.sync
        def _(sp):
            sp.dma_start(cT[:, :], c_t).then_inc(s_small, 16)
            sp.dma_start(bqc[:, :], b_col).then_inc(s_small, 16)
            sp.dma_start(boc[:, :], bout_col).then_inc(s_small, 16)
            for m in range(NMOD):
                sp.dma_start(wmod[:, :, m * D:(m + 1) * D], w_mod[:, :, m * D:(m + 1) * D]).then_inc(s_wmod, 16)
            sp.dma_start(x_tiles[:, 0:TPB, :], x_view[0]).then_inc(s_x0, 16)
            sp.dma_start(const[:, :], tables).then_inc(s_const, 16)
            sp.dma_start(win, w_in).then_inc(s_win, 16)
            sp.dma_start(bias_kv[:, :, :], b_row.unsqueeze(0).to_broadcast([P, 2, D])).then_inc(s_att, 16)
            sp.dma_start(kcos[:, :, :], rope_rows[0]).then_inc(s_att, 16)
            sp.dma_start(ksin[:, :, :], rope_rows[1]).then_inc(s_att, 16)
            sp.dma_start(qcos[:, :], rope_cols[0]).then_inc(s_att, 16)
            sp.dma_start(qsin[:, :], rope_cols[1]).then_inc(s_att, 16)
            sp.dma_start(wo[:, :, :], w_out).then_inc(s_att, 16)
            sp.dma_start(gate_w[:, :, :], gates).then_inc(s_att, 16)
            for b in range(1, BATCH):
                sp.dma_start(x_tiles[:, b * TPB:(b + 1) * TPB, :], x_view[b]).then_inc(s_xrest, 16)

            sp.wait_ge(s_modr, 1)
            sp.dma_start(mod_rows[:, :], modr[:, :]).then_inc(s_modw, 16)
            sp.wait_ge(s_modw, 16)

            def load_rows_a(b):
                for m in range(3):
                    sp.dma_start(rows_a[:, m, :].rearrange("p (c f) -> p c f", c=KC), mod_row(m, b)).then_inc(s_rows_a, 16)

            def load_rows_b(b):
                for m in range(2):
                    sp.dma_start(rows_b[:, m, :].rearrange("p (c f) -> p c f", c=KC), mod_row(3 + m, b)).then_inc(s_rows_b, 16)

            load_rows_a(0)
            load_rows_b(0)
            for b in range(BATCH):
                sp.dma_start(rows_g[:, b, :].rearrange("p (c f) -> p c f", c=KC), mod_row(5, b)).then_inc(s_rows_g, 16)
            sp.wait_ge(s_fill, 3)
            sp.dma_start(slots[:, :].rearrange("(p c) w -> p c w", p=P), tbl[:, 0:EXPERTS * SLOT_COLS, :]).then_inc(s_prefill, 16)
            sp.dma_start(h2_rows[TOKENS:ROWS, :], zrow[:, :]).then_inc(s_zero, 16)
            sp.dma_start(acc[0][TOKENS:ROWS, :], zrow[:, :]).then_inc(s_zero, 16)
            sp.dma_start(acc[1][:, :].rearrange("(g p) d -> p g d", p=P),
                         zrow[:, :].unsqueeze(1).to_broadcast([P, ROWS // P, D])).then_inc(s_zero, 16)
            sp.wait_ge(s_woa, KC)
            sp.wait_ge(s_res, TPB)
            load_rows_a(1)

            def round_sp(b, last):
                sp.wait_ge(s_h2, TPB * (b + 1))
                apart(sp)
                sp.dma_start(h2_view[bass.ds(b, 1)].rearrange("o p i d -> (o p) i d"), h2[:, :, :]).then_inc(s_h2w, 16)
                if not last:
                    load_rows_b(b + 1)

            for b in range(BATCH):
                round_sp(b, b == BATCH - 1)
                if b + 2 < BATCH:
                    sp.wait_ge(s_woa, KC * (b + 2))
                    sp.wait_ge(s_res, TPB * (b + 2))
                    load_rows_a(b + 2)

            def load_w(e):
                slot = wqkv[:, bass.ds((e & (WSLOTS - 1)) * WROW, WROW)] if not isinstance(e, int) else \
                    wqkv[:, (e % WSLOTS) * WROW:(e % WSLOTS + 1) * WROW]
                sp.dma_start(slot, ex_view[bass.ds(e, 1)].rearrange("o p w -> (o p) w")).then_inc(s_w, 16)

            sp.wait_ge(s_q, KC * BATCH)
            sp.wait_ge(s_kv, 2 * TPB * BATCH)
            for e in range(WSLOTS):
                if e:
                    sp.wait_ge(s_w, 16 * e)
                load_w(e)

            sp.wait_ge(s_h2w, 16 * BATCH)
            sp.wait_ge(s_zero, 48)

            def load_shared(t, s):
                if not (isinstance(t, int) and t < 4):
                    sp.wait_ge(s_T, t - 3)
                    apart(sp)
                sp.dma_start(xg[s], h2_tile[bass.ds(t, 1)].rearrange("o p d -> (o p) d")).then_inc(s_xs[s], 16)

            def store_shared(t, s):
                sp.wait_ge(s_y, t + 1)
                apart(sp)
                sp.dma_start(acc_tile[0][bass.ds(t, 1)].rearrange("o p d -> (o p) d"), yb[s % 2]).then_inc(s_ss[s % 2], 16)

            load_shared(0, 0)
            load_shared(1, 1)
            load_shared(2, 2)
            load_shared(3, 3)
            with sp.Fori(0, SHARED_ROUNDS - 1) as r:
                for s in range(ROUND):
                    store_shared(r * ROUND + s, s)
                    load_shared(r * ROUND + s + 4, s)
            for s in range(ROUND):
                store_shared(TILES - ROUND + s, s)

            sp.wait_ge(s_plan, 2)
            with sp.Fori(WSLOTS, EV) as e:
                done = sp.value_load(cum_i[0:1, bass.ds(e - WSLOTS, 1)], min_val=0, max_val=FLAT)
                sp.wait_ge(s_d, done)
                apart(sp)
                sp.wait_ge(s_w, 16 * e)
                apart(sp)
                load_w(e)

            def load_sums(b):
                if b >= 2:
                    sp.wait_ge(s_fo, TPB * (b - 1))
                sp.dma_start(fa[b % 2], acc_view[0][b]).then_inc(s_fl[b % 2], 16)
                sp.dma_start(fb[b % 2], acc_view[1][b]).then_inc(s_fl[b % 2], 16)

            sp.wait_ge(s_sc[0], 16 * (EXPERT_TILES // 2))
            sp.wait_ge(s_sc[1], 16 * (EXPERT_TILES // 2))
            load_sums(0)
            load_sums(1)
            for b in range(BATCH):
                sp.wait_ge(s_fo, TPB * (b + 1))
                sp.dma_start(out_view[b], x_tiles[:, b * TPB:(b + 1) * TPB, :]).then_inc(s_out, 16)
                if b + 2 < BATCH:
                    load_sums(b + 2)
            sp.wait_ge(s_out, 16 * BATCH)

        @block.gpsimd
        def _(pool):
            pool.memset(tbl[:, :, :], 0).then_inc(s_pres, 1)
            pool.memset(zrow[:, :], 0.0).then_inc(s_fill, 1)
            pool.memset(zero8[:, :], 0.0).then_inc(s_fill, 1)
            pool.wait_ge(s_pres, 1)
            pool.iota(tbl[:, :, 0], pattern=[[0, DUMMY_COL + 1]], base=PAD_ID, channel_multiplier=1).then_inc(s_fill, 1)

            PRES = 2 * TPB

            def residual(b):
                t = Tally(s_pres, PRES * b + 1)
                for i in range(TPB):
                    g = x_at(b * TPB + i)
                    pool.wait_ge(s_rows_a, 48 * (b + 1))
                    pool.wait_ge(s_xn, TPB * b + i + 1)
                    if i:
                        pool.wait_ge(s_res, TPB * b + i)
                    elif not (isinstance(b, int) and b == 0):
                        pool.wait_ge(s_res, TPB * b)
                    apart(pool)
                    a = t.mark(pool.tensor_tensor(pool_t, xn[:, i, :], rows_a[:, 1, :], ALU.mult))
                    c = t.mark(pool.tensor_tensor(g, g, rows_a[:, 2, :], ALU.add))
                    pool.wait_ge(s_pres, c)
                    apart(pool)
                    pool.tensor_tensor(g, g, pool_t, ALU.add).then_inc(s_res, 1)

            def finish_h2(b):
                for i in range(TPB):
                    pool.wait_ge(s_h2m, TPB * b + i + 1)
                    pool.tensor_tensor(h2[:, i, :], h2[:, i, :], rows_b[:, 1, :], ALU.add).then_inc(s_h2, 1)

            def scatter(b):
                for i in range(TPB):
                    pool.wait_ge(s_place, TPB * b + i + 1)
                    apart(pool)
                    for k in range(TOPK):
                        pool.indirect_dma_start(
                            out=slots[:, :], out_offset=bass.IndirectOffsetOnAxis(ap=place[:, i, k:k + 1], axis=0),
                            in_=pay[:, i, k, :], in_offset=None).then_inc(s_scat, 16)

            residual(0)
            pool.wait_ge(s_prefill, 16)
            residual(1)
            finish_h2(0)
            scatter(0)
            with pool.Fori(1, BATCH - 1) as b:
                residual(b + 1)
                finish_h2(b)
                scatter(b)
            finish_h2(BATCH - 1)
            scatter(BATCH - 1)
            pool.wait_ge(s_scat, 16 * TOPK * TILES)
            pool.dma_start(tbl[:, SLOT_COLS:EV * SLOT_COLS, :], slots[:, :].rearrange("(p c) w -> p c w", p=P)).then_inc(s_tbl, 16)
            pool.wait_ge(s_tbl, 16)
            pool.wait_ge(s_plan, 2)

            def gather(t, r, s):
                col = pool.value_load(plan[0:1, 0, bass.ds(t, 1)], min_val=0, max_val=DUMMY_COL)
                if not (isinstance(t, int) and t < TILES + 4):
                    pool.wait_ge(s_sc[s % 2], 32 * (r - SHARED_ROUNDS) + 16 * (s // 2) - 16)
                pool.tensor_copy(ids[s][:, :], tbl[:, bass.ds(col, 1), :].rearrange("p o w -> p (o w)")).then_inc(s_ids, 1)
                pool.wait_ge(s_ids, t - TILES + 1)
                pool.wait_ge(s_T, t - 3)
                apart(pool)
                pool.indirect_dma_start(
                    out=xg[s], out_offset=None, in_=h2_rows[:, :],
                    in_offset=bass.IndirectOffsetOnAxis(ap=ids[s][:, 0:1], axis=0)).then_inc(s_xg[s], 16)

            def add_rows(t, r, s):
                pool.wait_ge(s_y, t + 1)
                if not (isinstance(t, int) and t < TILES + 2):
                    pool.wait_ge(s_sc[s % 2], 32 * (r - SHARED_ROUNDS) + 16 * (s // 2))
                apart(pool)
                pool.indirect_dma_start(
                    out=acc[s % 2][:, :], out_offset=bass.IndirectOffsetOnAxis(ap=ids[s][:, 0:1], axis=0),
                    in_=yb[s % 2], in_offset=None, compute_op=ALU.add).then_inc(s_sc[s % 2], 16)

            gather(TILES, SHARED_ROUNDS, 0)
            gather(TILES + 1, SHARED_ROUNDS, 1)
            pool.wait_ge(s_ss[0], 16 * (TILES // 2))
            pool.wait_ge(s_ss[1], 16 * (TILES // 2))
            def round_pool(r, last=False):
                for s in range(ROUND):
                    n = s + 2
                    if not (last and n >= ROUND):
                        gather(r * ROUND + n, r + n // ROUND, n % ROUND)
                    add_rows(r * ROUND + s, r, s)

            round_pool(SHARED_ROUNDS)
            with pool.Fori(SHARED_ROUNDS + 1, ROUNDS - 1) as r:
                round_pool(r)
            round_pool(ROUNDS - 1, last=True)

            for g in range(TILES):
                b, i = divmod(g, TPB)
                pool.wait_ge(s_fl[b % 2], 32 * (b // 2 + 1))
                pool.tensor_tensor(fa[b % 2][:, i, :], fa[b % 2][:, i, :], fb[b % 2][:, i, :], ALU.add).then_inc(s_fs, 1)

        @block.scalar
        def _(sc):
            sc.wait_ge(s_small, 48)
            sc.activation(silu_c[:, :], cT[:, :], ACT.Silu).then_inc(s_silu, 1)

            def take_root(b, n):
                sc.wait_ge(s_var[n], b + 1)
                sc.activation(root[:, n, :], var[:, n, :], ACT.Sqrt).then_inc(s_root[n], 1)

            def norm1(b):
                take_root(b, 0)
                sc.wait_ge(s_mv, b + 1)
                if not (isinstance(b, int) and b == 0):
                    sc.wait_ge(s_tpA, KC * b)
                    sc.wait_ge(s_res, TPB * b)
                for i in range(TPB):
                    sc.activation(xn[:, i, :], x_at(b * TPB + i), ACT.Identity, bias=shift[:, i:i + 1],
                                  scale=rstd[:, i:i + 1]).then_inc(s_xn, 1)

            def attend(b):
                sc.wait_ge(s_modv, 3)
                if not (isinstance(b, int) and b == 0):
                    sc.wait_ge(s_q, KC * b)
                    sc.wait_ge(s_kv, 2 * TPB * b)
                for c in range(KC):
                    sc.wait_ge(s_tpA, KC * b + c + 1)
                    sc.activation(hT[:, c, :], bank[c % 2][:, :], ACT.Identity,
                                  bias=modc[:, bass.ds(c * BATCH + b, 1)],
                                  scale=scale_a[:, bass.ds(c * BATCH + b, 1)]).then_inc(s_hT, 1)
                for i in range(TPB):
                    sc.wait_ge(s_kro, TPB * b + i + 1)
                    if i == 0 and not (isinstance(b, int) and b == 0):
                        sc.wait_ge(s_rn, b)
                    if i or not (isinstance(b, int) and b == 0):
                        sc.wait_ge(s_ksq, TPB * b + i)
                    sc.activation(square_junk, kb, ACT.Square, accum_out=ksq[:, i:i + 1]).then_inc(s_ksq, 1)
                take_root(b, 2)
                if not (isinstance(b, int) and b == 0):
                    sc.wait_ge(s_o, TPB * b)
                for c in range(KC):
                    sc.wait_ge(s_q, KC * b + c + 1)
                    sc.activation(qT[:, c, :], bank[4 + c % 2][:, :], ACT.Identity,
                                  bias=bqc[:, c:c + 1]).then_inc(s_qT, 1)

            def norm2(b):
                if not (isinstance(b, int) and b == 0):
                    sc.wait_ge(s_tpC, KC * b)
                    sc.wait_ge(s_h2w, 16 * b)
                take_root(b, 1)
                sc.wait_ge(s_mv2, b + 1)
                for i in range(TPB):
                    sc.activation(h2[:, i, :], x_at(b * TPB + i), ACT.Identity, bias=shift2[:, i:i + 1],
                                  scale=rstd2[:, i:i + 1]).then_inc(s_xn2, 1)

            def route(b):
                if not (isinstance(b, int) and b == 0):
                    sc.wait_ge(s_g, TPB * b)
                for c in range(KC):
                    sc.wait_ge(s_tpC, KC * b + c + 1)
                    sc.activation(h2T[:, c, :], bank[c % 2][:, :], ACT.Copy).then_inc(s_h2T, 1)
                if not (isinstance(b, int) and b == 0):
                    sc.wait_ge(s_place, TPB * b)
                for i in range(TPB):
                    sc.wait_ge(s_top, TPB * b + i + 1)
                    sc.activation(etop[:, i, :], topv[:, i, :], ACT.Exp, bias=ntop[:, i:i + 1],
                                  accum_out=esum[:, i:i + 1]).then_inc(s_ex, 1)
                    sc.activation(esh[:, i:i + 1], logit[:, i, 0:1], ACT.Exp, scale=-1.0).then_inc(s_ex, 1)

            norm1(0)
            attend(0)
            norm1(1)
            norm2(0)
            attend(1)
            route(0)
            with sc.Fori(1, BATCH - 1) as b:
                norm1(b + 1)
                norm2(b)
                attend(b + 1)
                route(b)
            norm2(BATCH - 1)
            route(BATCH - 1)

            def take_x(t, s):
                sc.wait_ge(s_T, t + 1)
                if not (isinstance(t, int) and t < 2):
                    sc.wait_ge(s_G, t - 1)
                sc.activation(h2T[:, 2 + s % 2, :], bank[s % 2][:, :], ACT.Copy).then_inc(s_xT, 1)

            def silu(t, s):
                sc.wait_ge(s_G, t + 1)
                if not (isinstance(t, int) and t < 2):
                    sc.wait_ge(s_in, t - 1)
                sc.activation(act[s % 2][:, :], bank[2 + s % 2][:, 0:INNER], ACT.Silu).then_inc(s_sl, 1)

            def round_act(r, last=False):
                for s in range(ROUND):
                    if not (last and s == ROUND - 1):
                        take_x(r * ROUND + s + 1, s + 1)
                    silu(r * ROUND + s, s)

            take_x(0, 0)
            round_act(0)
            with sc.Fori(1, ROUNDS - 1) as r:
                round_act(r)
            round_act(ROUNDS - 1, last=True)

        @block.vector
        def _(ve):
            def step(t, ins):
                ve.wait_ge(t.sem, t.mark(ins))

            t0 = Tally(s_v)
            ve.memset(ones_bf[:, :], 1.0).then_inc(s_cst, 1)
            ve.memset(ones1[:, :], 1.0).then_inc(s_cst, 1)
            ve.memset(mask[:, :, 0:1], 1.0).then_inc(s_cst, 1)
            ve.memset(seen[:, TPB, :], 0.0).then_inc(s_cst, 1)
            ve.wait_ge(s_const, 16)
            ve.tensor_copy(tri_bf[:, :], const[:, C_TRI:C_TRI + P]).then_inc(s_cst, 1)

            def one_over_root(t, n, to):
                step(t, ve.reciprocal(to, root[:, n, :]))
                step(t, ve.tensor_tensor(corr[:, n, :], to, to, ALU.mult))
                step(t, ve.tensor_tensor(corr[:, n, :], corr[:, n, :], var[:, n, :], ALU.mult))
                step(t, ve.tensor_scalar(corr[:, n, :], corr[:, n, :], -0.5, 1.5, ALU.mult, ALU.add))

            def stats1(b):
                t = Tally(s_vl, (2 * TPB + 5) * b)
                if not (isinstance(b, int) and b == 0):
                    ve.wait_ge(s_xn, TPB * b)
                    ve.wait_ge(s_mv, b)
                for i in range(TPB):
                    a = t.mark(ve.bn_stats(stats[:, i, :], x_at(b * TPB + i)))
                for i in range(TPB):
                    ve.wait_ge(s_vl, a - TPB + 1 + i)
                    apart(ve)
                    c = t.mark(ve.bn_aggr(mean_var[:, i, :], stats[:, i, :]))
                ve.wait_ge(s_vl, c)
                ve.tensor_scalar(var[:, 0, :], mean_var[:, :, 1], LN_EPS, None, ALU.add).then_inc(s_var[0], 1)
                ve.wait_ge(s_root[0], b + 1)
                one_over_root(t, 0, rstd[:, :])
                step(t, ve.tensor_tensor(rstd[:, :], rstd[:, :], corr[:, 0, :], ALU.mult))
                ve.scalar_tensor_tensor(out=shift[:, :], in0=mean_var[:, :, 0], scalar=-1.0, in1=rstd[:, :],
                                        op0=ALU.mult, op1=ALU.mult).then_inc(s_mv, 1)

            ve.wait_ge(s_x0, 16)
            stats1(0)

            ve.wait_ge(s_mod, 1)
            step(t0, ve.tensor_copy(modc[:, :], bank[0][:, 0:MODC * BATCH]))
            n = KC * BATCH
            sa, ca, ga, sbm, cb, gb = (modc[:, m * n:(m + 1) * n] for m in range(NMOD))
            row = [modf[:, m * n:(m + 1) * n] for m in range(NMOD)]
            for g, to in ((ga, row[0]), (gb, row[5])):
                t0.mark(ve.tensor_scalar(mod_t[:, 0, :], g, 0.0, 2.0, ALU.is_ge, ALU.mult))
                step(t0, ve.tensor_scalar(mod_t[:, 2, :], g, -1.0, 0.25, ALU.mult, ALU.max))
                step(t0, ve.tensor_tensor(mod_t[:, 1, :], g, mod_t[:, 2, :], ALU.max))
                step(t0, ve.tensor_scalar(mod_t[:, 2, :], mod_t[:, 0, :], -1.0, None, ALU.add))
                step(t0, ve.tensor_tensor(to, mod_t[:, 2, :], mod_t[:, 1, :], ALU.mult))
            ve.tensor_scalar(scale_a[:, :], ca, 1.0, None, ALU.add).then_inc(s_modv, 1)
            step(t0, ve.tensor_tensor(mod_t[:, 0, :], boc[:, :], sa, ALU.add))
            ve.wait_ge(s_modv, 1)
            t0.mark(ve.tensor_tensor(row[1], row[0], scale_a[:, :], ALU.mult))
            t0.mark(ve.tensor_tensor(row[2], row[0], mod_t[:, 0, :], ALU.mult))
            t0.mark(ve.tensor_scalar(row[3], cb, 1.0, None, ALU.add))
            step(t0, ve.tensor_copy(row[4], sbm))
            ve.tensor_copy(mod_t[:, 1, :], sbm).then_inc(s_modv, 1)
            ve.tensor_copy(mod_t[:, 2, :], sbm).then_inc(s_modv, 1)
            ve.wait_ge(s_modT, 1)
            ve.tensor_copy(modr[:, :], bank[1][0:MODC * BATCH, 0:P]).then_inc(s_modr, 1)

            VA = TPB * 6 + 4 + 5
            def attend(b):
                t = Tally(s_va, VA * b)
                for i in range(TPB):
                    ve.wait_ge(s_kv, 2 * TPB * b + 2 * i + 1)
                    if i or not (isinstance(b, int) and b == 0):
                        ve.wait_ge(s_ksq, TPB * b + i)
                        ve.wait_ge(s_kvp, TPB * b + i)
                    t.mark(ve.tensor_tensor(kb, bank[2][:, :], bias_kv[:, 0, :], ALU.add))
                    ve.wait_ge(s_va, t.start + t.n)
                    ve.nop().then_inc(s_kvr, 1)
                    t.mark(ve.tensor_tensor(rope_t[:, 0:HALF], kb[:, HALF:ROT], ksin[:, i, 0:HALF], ALU.mult))
                    c = t.mark(ve.tensor_tensor(rope_t[:, HALF:ROT], kb[:, 0:HALF], ksin[:, i, HALF:ROT], ALU.mult))
                    ve.wait_ge(s_va, c)
                    step(t, ve.tensor_tensor(kb[:, 0:ROT], kb[:, 0:ROT], kcos[:, i, :], ALU.mult))
                    step(t, ve.tensor_tensor(kb[:, 0:ROT], kb[:, 0:ROT], rope_t[:, 0:ROT], ALU.add))
                    ve.nop().then_inc(s_kro, 1)
                    ve.wait_ge(s_kv, 2 * TPB * b + 2 * i + 2)
                    step(t, ve.tensor_tensor(vb, bank[3][:, :], bias_kv[:, 1, :], ALU.add))
                    ve.nop().then_inc(s_kvr, 1)
                    if i == 0 and not (isinstance(b, int) and b == 0):
                        ve.wait_ge(s_as, b)
                    ve.tensor_tensor(kv[:, i, :], kb, vb, ALU.mult).then_inc(s_kvp, 1)
                ve.wait_ge(s_ksq, TPB * (b + 1))
                ve.tensor_scalar(var[:, 2, :], ksq[:, :], 1e-24, None, ALU.max).then_inc(s_var[2], 1)
                ve.wait_ge(s_root[2], b + 1)
                if not (isinstance(b, int) and b == 0):
                    ve.wait_ge(s_rn, b)
                    ve.wait_ge(s_as, b)
                one_over_root(t, 2, krn[:, :])
                ve.tensor_tensor(krn[:, :], krn[:, :], corr[:, 2, :], ALU.mult).then_inc(s_rn, 1)
                ve.wait_ge(s_qT, KC * b + 2)
                if not (isinstance(b, int) and b == 0):
                    ve.wait_ge(s_qro, 2 * b)
                t.mark(ve.tensor_tensor(rope_q[0], qT[:, 1, :], qsin[:, :], ALU.mult))
                c = t.mark(ve.tensor_tensor(rope_q[1], qT[:, 0, :], qsin[:, :], ALU.mult))
                ve.wait_ge(s_va, c)
                t.mark(ve.tensor_tensor(qT[:, 0, :], qT[:, 0, :], qcos[:, :], ALU.mult))
                c = t.mark(ve.tensor_tensor(qT[:, 1, :], qT[:, 1, :], qcos[:, :], ALU.mult))
                ve.wait_ge(s_va, c)
                ve.tensor_tensor(qT[:, 0, :], qT[:, 0, :], rope_q[0], ALU.subtract).then_inc(s_qro, 1)
                ve.tensor_tensor(qT[:, 1, :], qT[:, 1, :], rope_q[1], ALU.add).then_inc(s_qro, 1)
                ve.wait_ge(s_as, b + 1)
                ve.wait_ge(s_rows_a, 48 * (b + 1))
                if not (isinstance(b, int) and b == 0):
                    ve.wait_ge(s_woa, KC * b)
                step(t, ve.tensor_copy(asum[:, :], bank[6][:, 0:KC]))
                if not (isinstance(b, int) and b == 0):
                    ve.wait_ge(s_o, TPB * b)
                for k in range(KC):
                    ve.scalar_tensor_tensor(out=woa[:, k, :], in0=wo[:, k, :], scalar=asum[:, k:k + 1],
                                            in1=rows_a[:, 0, :], op0=ALU.mult, op1=ALU.mult).then_inc(s_woa, 1)
                assert t.n == VA, t.n

            VB = 3 * TPB + 5
            def finish(b):
                t = Tally(s_vb, VB * b)
                if not (isinstance(b, int) and b == 0):
                    ve.wait_ge(s_mv2, b)
                    ve.wait_ge(s_xn2, TPB * b)
                for i in range(TPB):
                    g = x_at(b * TPB + i)
                    ve.wait_ge(s_o, TPB * b + i + 1)
                    ve.wait_ge(s_res, TPB * b + i + 1)
                    step(t, ve.tensor_tensor(g, bank[4 + i % 2][:, :], g, ALU.add))
                    ve.nop().then_inc(s_or, 1)
                    step(t, ve.bn_stats(stats2[:, i, :], g))
                    apart(ve)
                    step(t, ve.bn_aggr(mean_var2[:, i, :], stats2[:, i, :]))
                ve.tensor_scalar(var[:, 1, :], mean_var2[:, :, 1], LN_EPS, None, ALU.add).then_inc(s_var[1], 1)
                ve.wait_ge(s_root[1], b + 1)
                one_over_root(t, 1, rstd2[:, :])
                step(t, ve.tensor_tensor(rstd2[:, :], rstd2[:, :], corr[:, 1, :], ALU.mult))
                ve.scalar_tensor_tensor(out=shift2[:, :], in0=mean_var2[:, :, 0], scalar=-1.0,
                                        in1=rstd2[:, :], op0=ALU.mult, op1=ALU.mult).then_inc(s_mv2, 1)
                for i in range(TPB):
                    ve.wait_ge(s_rows_b, 32 * (b + 1))
                    ve.wait_ge(s_xn2, TPB * b + i + 1)
                    ve.tensor_tensor(h2[:, i, :], h2[:, i, :], rows_b[:, 0, :], ALU.mult).then_inc(s_h2m, 1)
                assert t.n == VB

            VC = 7 * TPB + 17 * TPB + 2
            def route(b):
                t = Tally(s_vc, (VC + 1) * b)
                if not (isinstance(b, int) and b == 0):
                    ve.wait_ge(s_rk, TPB * b)
                step(t, ve.tensor_copy(seen[:, 0, :], seen[:, TPB, :]))
                if not (isinstance(b, int) and b == 0):
                    ve.wait_ge(s_scat, 16 * TOPK * TPB * b)
                ve.wait_ge(s_g, TPB * (b + 1))
                c = t.mark(ve.tensor_copy(logit[:, :, :].rearrange("p i e -> p (i e)"), bank[7][:, 0:TPB * EV]))
                ve.wait_ge(s_vc, c)
                for i in range(TPB):
                    apart(ve)
                    step(t, ve.max(topv[:, i, :], logit[:, i, 1:EV]))
                    ve.tensor_scalar(ntop[:, i:i + 1], topv[:, i, 0:1], -1.0, None, ALU.mult).then_inc(s_top, 1)
                    t.mark(ve.max_index(topi[:, i, :], topv[:, i, :], logit[:, i, 1:EV]))
                    step(t, ve.match_replace(replaced[:, i, :], topv[:, i, :], logit[:, i, 1:EV], NEG))
                    step(t, ve.tensor_tensor(mask[:, i, 1:EV], replaced[:, i, :], logit[:, i, 1:EV], ALU.not_equal))
                    step(t, ve.tensor_tensor(seen[:, i + 1, :], seen[:, i, :], mask[:, i, :], ALU.add))
                    ve.nop().then_inc(s_mask, 1)
                    t.mark(ve.tensor_copy(topif[:, i, :], topi[:, i, :]))
                    step(t, ve.tensor_copy(idx_i[:, i, :], topi[:, i, :]))
                ve.wait_ge(s_rk, TPB * (b + 1))
                step(t, ve.tensor_copy(rank_all[:, :, :].rearrange("p i e -> p (i e)"), bank[6][:, 8:8 + TPB * EV]))
                for i in range(TPB):
                    g = b * TPB + i
                    for k in range(TOPK):
                        c = t.mark(ve.scalar_tensor_tensor(
                            out=pick[:, k, :], in0=const[:, C_IOTA:C_IOTA + EXPERTS], scalar=topif[:, i, k:k + 1],
                            in1=rank_all[:, i, 1:EV], op0=ALU.is_equal, op1=ALU.mult,
                            accum_out=rank_f[:, i, k:k + 1]))
                    ve.wait_ge(s_vc, c)
                    step(t, ve.tensor_copy(rank_i[:, i, :], rank_f[:, i, :]))
                    t.mark(ve.tensor_scalar(place_r[:, i, :], rank_i[:, i, :], P - 1, 10, ALU.bitwise_and, ALU.logical_shift_left))
                    t.mark(ve.tensor_scalar(place_q[:, i, :], rank_i[:, i, :], 7, None, ALU.logical_shift_right))
                    step(t, ve.tensor_scalar(place_e[:, i, :], idx_i[:, i, :], 4, None, ALU.logical_shift_left))
                    step(t, ve.tensor_tensor(place_q[:, i, :], place_q[:, i, :], place_e[:, i, :], ALU.bitwise_or))
                    t.mark(ve.tensor_tensor(place[:, i, :], place_q[:, i, :], place_r[:, i, :], ALU.bitwise_or))
                    ve.wait_ge(s_ex, 2 * TPB * b + 2 * i + 2)
                    t.mark(ve.tensor_scalar(sh1[:, i:i + 1], esh[:, i:i + 1], 1.0, None, ALU.add))
                    step(t, ve.reciprocal(rsum[:, i:i + 1], esum[:, i:i + 1]))
                    t.mark(ve.tensor_scalar(pay[:, i, :, 0], zero8[:, :], const[:, bass.ds(C_TOK + g, 1)], None, ALU.add))
                    ve.tensor_scalar(pay[:, i, :, 1].bitcast(F32), etop[:, i, :], rsum[:, i:i + 1], None, ALU.mult).then_inc(s_gr, 1)
                    ve.wait_ge(s_gr, TPB * b + i + 1)
                    ve.reciprocal(gate_sh[:, bass.ds(g, 1)], sh1[:, i:i + 1]).then_inc(s_place, 1)
                assert t.n == VC + 1, t.n

            ve.wait_ge(s_att, 16 * 7)
            ve.wait_ge(s_fill, 3)
            attend(0)
            ve.wait_ge(s_xrest, 16 * (BATCH - 1))
            stats1(1)
            finish(0)
            attend(1)
            route(0)
            with ve.Fori(1, BATCH - 1) as b:
                stats1(b + 1)
                finish(b)
                attend(b + 1)
                route(b)
            finish(BATCH - 1)
            route(BATCH - 1)

            ve.wait_ge(s_cnt, 1)
            step(t0, ve.tensor_copy(count_i[:, :], bank[6][0:EV, 0:1]))
            step(t0, ve.tensor_scalar(count_f[:, :], count_i[:, :], float(P - 1), None, ALU.add))
            step(t0, ve.tensor_copy(count_i[:, :], count_f[:, :]))
            step(t0, ve.tensor_scalar(tiles_i[:, :], count_i[:, :], 7, None, ALU.logical_shift_right))
            step(t0, ve.tensor_copy(tiles_f[:, :], tiles_i[:, :]))
            step(t0, ve.tensor_scalar(tiles_f[:, :], tiles_f[:, :], 1.0, None, ALU.max))
            step(t0, ve.tensor_scalar(col_step[:, :], tiles_f[:, :], -1.0, float(SLOT_COLS), ALU.mult, ALU.add))
            ve.tensor_copy(tiles_f[:, :], tiles_f[:, :]).then_inc(s_ntile, 1)
            ve.wait_ge(s_cum, 1)
            step(t0, ve.tensor_copy(cum[:, :], bank[6][0:EV, 1:2]))
            t0.mark(ve.tensor_copy(cum_i[:, :], bank[6][0:1, 8:8 + EV]))
            ve.tensor_scalar(past[:, :], const[0:EV, C_FLAT:C_FLAT + FLAT], cum[:, 0:1], None, ALU.is_ge).then_inc(s_past, 1)
            ve.wait_ge(s_flat, 1)
            t0.mark(ve.tensor_tensor(plan_f[:, 0, :], bank[7][0:1, 0:FLAT], const[0:1, C_FLAT:C_FLAT + FLAT], ALU.add))
            step(t0, ve.tensor_scalar(plan_f[:, 1, :], bank[7][0:1, 256:256 + FLAT], float(EV - 1), None, ALU.min))
            step(t0, ve.tensor_scalar(plan_f[:, 0, :], plan_f[:, 0, :], float(DUMMY_COL), None, ALU.min))
            t0.mark(ve.tensor_copy(plan[:, 0, :], plan_f[:, 0, :]))
            t0.mark(ve.tensor_copy(plan_w[:, 0, :], plan_f[:, 1, :]))
            step(t0, ve.tensor_scalar(plan_f[:, 2, :], plan_f[:, 1, :], 1.0, 16.0, ALU.add, ALU.mult))
            step(t0, ve.tensor_scalar(plan_w[:, 1, :], plan_w[:, 0, :], WSLOTS - 1, None, ALU.bitwise_and))
            step(t0, ve.tensor_copy(plan_f[:, 1, :], plan_w[:, 1, :]))
            step(t0, ve.tensor_scalar(plan_f[:, 1, :], plan_f[:, 1, :], float(WROW), None, ALU.mult))
            ve.tensor_copy(plan[:, 1, :], plan_f[:, 1, :]).then_inc(s_plan, 1)
            ve.tensor_copy(plan[:, 2, :], plan_f[:, 2, :]).then_inc(s_plan, 1)

            def gated(t, r, s, shared):
                ve.wait_ge(s_sl, t + 1)
                if not (isinstance(t, int) and t < 2):
                    ve.wait_ge(s_I, t - 1)
                w = gate_sh[:, bass.ds(t, 1)] if shared else ids[s][:, 1:2].bitcast(F32)
                ve.scalar_tensor_tensor(out=inter[s % 2][:, :], in0=bank[2 + s % 2][:, INNER:GU], scalar=w,
                                        in1=act[s % 2][:, :], op0=ALU.mult, op1=ALU.mult).then_inc(s_in, 1)

            def take_y(t, r, s, shared):
                ve.wait_ge(s_d, t + 1)
                if shared or (isinstance(t, int) and t < TILES + 2):
                    if not (isinstance(t, int) and t < 2):
                        ve.wait_ge(s_ss[s % 2], 32 * r + 16 * (s // 2))
                else:
                    ve.wait_ge(s_sc[s % 2], 32 * (r - SHARED_ROUNDS) + 16 * (s // 2))
                ve.tensor_copy(yb[s % 2], bank[4 + s % 2][:, :]).then_inc(s_y, 1)

            def take_inter(t, s):
                ve.wait_ge(s_I, t + 1)
                if not (isinstance(t, int) and t < 2):
                    ve.wait_ge(s_d, t - 1)
                ve.tensor_copy(iT[s % 2][:, :], bank[6 + s % 2][:, 0:P]).then_inc(s_iT, 1)

            def round_ve(r, shared, first=False):
                for s in range(ROUND):
                    t = r * ROUND + s
                    gated(t, r, s, shared)
                    if s:
                        take_y(t - 1, r, s - 1, shared)
                    elif not first:
                        take_y(t - 1, r - 1, ROUND - 1, shared or isinstance(r, int))
                    take_inter(t, s)

            round_ve(0, True, first=True)
            with ve.Fori(1, SHARED_ROUNDS) as r:
                round_ve(r, True)
            ve.wait_ge(s_tbl, 16)
            round_ve(SHARED_ROUNDS, False)
            with ve.Fori(SHARED_ROUNDS + 1, ROUNDS) as r:
                round_ve(r, False)
            take_y(FLAT - 1, ROUNDS - 1, ROUND - 1, False)

            for g in range(TILES):
                b, i = divmod(g, TPB)
                ve.wait_ge(s_fs, g + 1)
                ve.wait_ge(s_rows_g, 16 * BATCH)
                ve.tensor_tensor(fa[b % 2][:, i, :], fa[b % 2][:, i, :], rows_g[:, b, :], ALU.mult).then_inc(s_fm, 1)
                ve.wait_ge(s_fm, g + 1)
                ve.tensor_tensor(x_at(g), x_at(g), fa[b % 2][:, i, :], ALU.add).then_inc(s_fo, 1)

        @block.tensor
        def _(pe):
            pe.wait_ge(s_silu, 1)
            pe.wait_ge(s_wmod, 16 * NMOD)
            for n in range(MODC):
                for k in range(KC):
                    mm = pe.matmul(bank[0][:, n * BATCH:(n + 1) * BATCH], wmod[:, k, n * P:(n + 1) * P],
                                   silu_c[:, k * BATCH:(k + 1) * BATCH], start=(k == 0), stop=(k == KC - 1))
            mm.then_inc(s_mod, 1)
            pe.wait_ge(s_modv, 3)
            pe.wait_ge(s_const, 16)
            pe.transpose(bank[1][0:MODC * BATCH, 0:P], modf[:, :], ident).then_inc(s_modT, 1)
            pe.wait_ge(s_modr, 1)
            pe.wait_ge(s_win, 16)

            def attend(b):
                for c in range(KC):
                    if c == 0 and not (isinstance(b, int) and b == 0):
                        pe.wait_ge(s_hT, KC * b)
                        if not (isinstance(b, int) and b == 1):
                            pe.wait_ge(s_h2T, KC * (b - 1))
                    if c >= 2:
                        pe.wait_ge(s_hT, KC * b + c - 1)
                    for i in range(TPB):
                        if c == 0:
                            pe.wait_ge(s_xn, TPB * b + i + 1)
                        mm = pe.transpose(bank[c % 2][:, i * P:(i + 1) * P], xn[:, i, c * P:(c + 1) * P], ident)
                    mm.then_inc(s_tpA, 1)
                pe.wait_ge(s_hT, KC * (b + 1))
                for i in range(TPB):
                    for j in range(2):
                        if i or not (isinstance(b, int) and b == 0):
                            pe.wait_ge(s_kvr, 2 * TPB * b + 2 * (i - 1) + j + 1)
                        for k in range(KC):
                            mm = pe.matmul(bank[2 + j][:, :], hT[:, k, i * P:(i + 1) * P],
                                           win[:, k, (j + 1) * D:(j + 2) * D], start=(k == 0), stop=(k == KC - 1))
                        mm.then_inc(s_kv, 1)

                def queries(c):
                    if c < 2 and not (isinstance(b, int) and b == 0):
                        pe.wait_ge(s_or, TPB * b)
                    if c >= 2:
                        pe.wait_ge(s_qT, KC * b + c - 1)
                    for k in range(KC):
                        mm = pe.matmul(bank[4 + c % 2][:, :], win[:, k, c * P:(c + 1) * P], hT[:, k, :],
                                       start=(k == 0), stop=(k == KC - 1))
                    mm.then_inc(s_q, 1)

                queries(0)
                queries(1)
                pe.wait_ge(s_rn, b + 1)
                pe.wait_ge(s_kvp, TPB * (b + 1))
                if not (isinstance(b, int) and b == 0):
                    pe.wait_ge(s_woa, KC * b)
                if not (isinstance(b, int) and b <= 1):
                    pe.wait_ge(s_place, TPB * (b - 1))
                for c in range(KC):
                    for i in range(TPB):
                        mm = pe.matmul(bank[6][:, c:c + 1], kv[:, i, c * P:(c + 1) * P], krn[:, i:i + 1],
                                       start=(i == 0), stop=(i == TPB - 1))
                mm.then_inc(s_as, 1)
                queries(2)
                queries(3)

            def project(b):
                pe.wait_ge(s_qT, KC * (b + 1))
                pe.wait_ge(s_qro, 2 * (b + 1))
                pe.wait_ge(s_woa, KC * (b + 1))
                for i in range(TPB):
                    if i >= 2:
                        pe.wait_ge(s_or, TPB * b + i - 1)
                    for k in range(KC):
                        mm = pe.matmul(bank[4 + i % 2][:, :], qT[:, k, i * P:(i + 1) * P], woa[:, k, :],
                                       start=(k == 0), stop=(k == KC - 1))
                    mm.then_inc(s_o, 1)

            def route(b, hT_done):
                pe.wait_ge(s_h2, TPB * (b + 1))
                pe.wait_ge(s_hT, hT_done)
                if not (isinstance(b, int) and b == 0):
                    pe.wait_ge(s_top, TPB * b)
                    pe.wait_ge(s_place, TPB * b)
                for c in range(KC):
                    if c >= 2:
                        pe.wait_ge(s_h2T, KC * b + c - 1)
                    for i in range(TPB):
                        mm = pe.transpose(bank[c % 2][:, i * P:(i + 1) * P], h2[:, i, c * P:(c + 1) * P], ident)
                    mm.then_inc(s_tpC, 1)
                pe.wait_ge(s_h2T, KC * (b + 1))
                for i in range(TPB):
                    for k in range(KC):
                        mm = pe.matmul(bank[7][:, i * EV:(i + 1) * EV], h2T[:, k, i * P:(i + 1) * P], gate_w[:, k, :],
                                       start=(k == 0), stop=(k == KC - 1))
                    mm.then_inc(s_g, 1)
                for i in range(TPB):
                    pe.wait_ge(s_mask, TPB * b + i + 1)
                    o = bank[6][:, 8 + i * EV:8 + (i + 1) * EV]
                    pe.matmul(o, tri_bf[:, :], mask[:, i, :], start=True, stop=False)
                    pe.matmul(o, ones_bf[:, :], seen[:, i, :], start=False, stop=True).then_inc(s_rk, 1)

            pe.wait_ge(s_cst, 5)
            attend(0)
            pe.wait_ge(s_att, 16 * 7)
            project(0)
            attend(1)
            route(0, KC * 2)
            with pe.Fori(1, BATCH - 1) as b:
                project(b)
                attend(b + 1)
                route(b, KC * (b + 2))
            project(BATCH - 1)
            route(BATCH - 1, KC * BATCH)

            pe.wait_ge(s_place, TILES)
            pe.matmul(bank[6][0:EV, 0:1], seen[:, TPB, :], ones_bf[:, 0:1], start=True, stop=True).then_inc(s_cnt, 1)
            pe.wait_ge(s_ntile, 1)
            pe.matmul(bank[6][0:EV, 1:2], const[0:EV, C_TRI65:C_TRI65 + EV], tiles_f[:, :], start=True, stop=True)
            pe.matmul(bank[6][0:1, 8:8 + EV], tiles_f[:, :], const[0:EV, C_TRI65:C_TRI65 + EV],
                      start=True, stop=True).then_inc(s_cum, 1)
            pe.wait_ge(s_past, 1)
            pe.matmul(bank[7][0:1, 0:FLAT], col_step[:, :], past[:, :], start=True, stop=True)
            pe.matmul(bank[7][0:1, 256:256 + FLAT], ones1[0:EV, :], past[:, :], start=True, stop=True).then_inc(s_flat, 1)

            def turn(t, r, s, shared):
                if shared:
                    pe.wait_ge(s_xs[s], 16 * (r + 1))
                else:
                    pe.wait_ge(s_xg[s], 16 * (r - SHARED_ROUNDS + 1))
                if not (isinstance(t, int) and t < 2):
                    pe.wait_ge(s_xT, t - 1)
                for k in range(KC):
                    mm = pe.transpose(bank[s % 2][:, k * P:(k + 1) * P], xg[s][:, k * P:(k + 1) * P], ident)
                mm.then_inc(s_T, 1)

            def gate_up(t, s, w):
                pe.wait_ge(s_xT, t + 1)
                if not (isinstance(t, int) and t < 2):
                    pe.wait_ge(s_in, t - 1)
                for k in range(KC):
                    mm = pe.matmul(bank[2 + s % 2][:, 0:GU], xT[s % 2][:, k, :], wqkv[:, bass.ds(w + k * GU, GU)],
                                   start=(k == 0), stop=(k == KC - 1))
                mm.then_inc(s_G, 1)

            def down(t, s, w):
                pe.wait_ge(s_iT, t + 1)
                if not (isinstance(t, int) and t < 2):
                    pe.wait_ge(s_y, t - 1)
                pe.matmul(bank[4 + s % 2][:, :], iT[s % 2][:, :], wqkv[:, bass.ds(w + KC * GU, D)],
                          start=True, stop=True).then_inc(s_d, 1)

            def turn_inter(t, s):
                pe.wait_ge(s_in, t + 1)
                if not (isinstance(t, int) and t < 2):
                    pe.wait_ge(s_iT, t - 1)
                pe.transpose(bank[6 + s % 2][:, 0:P], inter[s % 2][:, :], ident).then_inc(s_I, 1)

            def round_pe(r, shared, first=False, last=False):
                before = 0
                if not shared:
                    before = pe.value_load(plan[0:1, 1, bass.ds(r * ROUND - 1, 1)], min_val=0, max_val=(WSLOTS - 1) * WROW)
                for s in range(ROUND):
                    t = r * ROUND + s
                    w = 0
                    if not shared:
                        w = pe.value_load(plan[0:1, 1, bass.ds(t, 1)], min_val=0, max_val=(WSLOTS - 1) * WROW)
                        need = pe.value_load(plan[0:1, 2, bass.ds(t, 1)], min_val=16, max_val=16 * EV)
                    if not (last and s == ROUND - 1):
                        turn(t + 1, r + (s + 1) // ROUND, (s + 1) % ROUND, shared and not (s == ROUND - 1 and isinstance(r, int) and r == SHARED_ROUNDS - 1))
                    if not shared:
                        pe.wait_ge(s_w, need)
                    gate_up(t, s, w)
                    if not (first and s == 0):
                        down(t - 1, (s - 1) % ROUND, before)
                    turn_inter(t, s)
                    before = w

            pe.wait_ge(s_w, 16)
            turn(0, 0, 0, True)
            round_pe(0, True, first=True)
            with pe.Fori(1, SHARED_ROUNDS - 1) as r:
                round_pe(r, True)
            round_pe(SHARED_ROUNDS - 1, True)
            pe.wait_ge(s_plan, 2)
            with pe.Fori(SHARED_ROUNDS, ROUNDS - 1) as r:
                round_pe(r, False)
            round_pe(ROUNDS - 1, False, last=True)
            w = pe.value_load(plan[0:1, 1, FLAT - 1:FLAT], min_val=0, max_val=(WSLOTS - 1) * WROW)
            down(FLAT - 1, ROUND - 1, w)


def _constants():
    c = np.zeros((P, CONSTS), np.float32)
    c[:, C_ID:C_ID + P] = np.eye(P)
    c[:, C_TRI:C_TRI + P] = np.triu(np.ones((P, P)), 1)
    c[:EV, C_TRI65:C_TRI65 + EV] = np.triu(np.ones((EV, EV)))
    c[:, C_IOTA:C_IOTA + EXPERTS] = np.arange(EXPERTS)
    c[:, C_FLAT:C_FLAT + FLAT] = np.arange(FLAT)
    c[:, C_TOK:C_TOK + TILES] = np.arange(TILES)[None, :] * P + np.arange(P)[:, None]
    inv = (1.0 / np.float32(10000.0) ** (np.arange(0, ROT, 2, dtype=np.float32) / np.float32(ROT))).astype(np.float32)
    freqs = np.arange(SEQ, dtype=np.float32)[:, None] * inv[None, :]
    cos = np.cos(freqs.astype(np.float64)).astype(np.float32)
    sin = np.sin(freqs.astype(np.float64)).astype(np.float32)
    by_row = lambda a: np.ascontiguousarray(a.reshape(TPB, P, ROT).transpose(1, 0, 2))
    rows = np.stack([by_row(np.concatenate([cos, cos], 1)), by_row(np.concatenate([-sin, sin], 1))])
    cols = np.ascontiguousarray(np.stack([cos.T, sin.T]))
    return c, rows, cols


def _layout(i):
    g = {n: np.asarray(a) for n, a in i.items()}
    order = np.concatenate([np.arange(0, ROT, 2), np.arange(1, ROT, 2), np.arange(ROT, D)])
    qkv = np.concatenate([order, D + order, 2 * D + order])
    chunks = lambda a: np.ascontiguousarray(a.reshape(KC, P, -1).transpose(1, 0, 2))
    w_in = chunks(g["L0_attn_W_in"][qkv].T)
    b_in = g["L0_attn_b_in"][qkv]
    w_out = chunks(g["L0_attn_W_out"].T[order])
    bout = np.ascontiguousarray(np.repeat(g["L0_attn_b_out"].reshape(KC, P).T[:, :, None], BATCH, 2).reshape(P, -1))
    gates = chunks(np.concatenate([g["L0_ffn_sh_gate1_w"], g["L0_ffn_gate_w"]]).T)
    gu = np.concatenate([np.concatenate([g["L0_ffn_sh_gate_w"], g["L0_ffn_sh_up_w"]])[None], g["L0_ffn_gu_w"]])
    gu = gu.transpose(0, 2, 1).reshape(EV, KC, P, GU).transpose(0, 2, 1, 3).reshape(EV, P, KC * GU)
    dp = np.concatenate([g["L0_ffn_sh_down_w"][None], g["L0_ffn_dp_w"]]).transpose(0, 2, 1)
    experts = np.ascontiguousarray(np.concatenate([gu, dp], 2))
    c_t = np.ascontiguousarray(g["L0_c"].reshape(BATCH, KC, P).transpose(2, 1, 0).reshape(P, -1))
    w_mod = chunks(g["L0_wmod"])
    c, rows, cols = _constants()
    return {
        "x": np.ascontiguousarray(g["L0_attn_X"].reshape(TOKENS, D)), "w_in": w_in,
        "b_col": np.ascontiguousarray(b_in[:D].reshape(KC, P).T), "b_row": np.ascontiguousarray(b_in[D:].reshape(2, D)),
        "w_out": w_out, "bout_col": bout, "gates": gates, "experts": experts, "c_t": c_t, "w_mod": w_mod,
        "tables": c, "rope_rows": rows, "rope_cols": cols,
    }


def kernel(**inputs):
    import concourse.bacc as _bacc
    from concourse.bass_utils import run_bass_kernel_spmd as _run

    nc = _bacc.Bacc("TRN2", target_bir_lowering=False, num_devices=1)
    arrays, args = {}, []
    for name, a in _layout(inputs).items():
        arrays[f"in_{name}"] = a
        args.append(nc.dram_tensor(f"in_{name}", a.shape, mybir.dt.from_np(a.dtype), kind="ExternalInput").ap())
    out = nc.dram_tensor("out_dram", (TOKENS, D), F32, kind="ExternalOutput").ap()
    build(nc, *args, out)
    r = _run(nc, [arrays], core_ids=[0])
    return r.results[0]["out_dram"].reshape(BATCH, SEQ, D)
```

```python
from contextlib import ExitStack

import numpy as np

import concourse.bass as bass
from concourse import mybir

ALU = mybir.AluOpType
ACT = mybir.ActivationFunctionType
F32 = mybir.dt.float32
BF16 = mybir.dt.bfloat16
I32 = mybir.dt.int32
U32 = mybir.dt.uint32

P = 128
BATCH = 4
SEQ = 512
D = 512
KC = D // P
TPB = SEQ // P
TOKENS = BATCH * SEQ
TILES = TOKENS // P
ROT = D // 2
HALF = ROT // 2
EXPERTS = 64
TOPK = 8
INNER = 128
EV = EXPERTS + 1
GU = 2 * INNER
WROW = KC * GU + D
WSLOTS = 4
SLOT_COLS = TOKENS // P
PAD_ID = TOKENS
ROWS = TOKENS + P
EXPERT_TILES = TOKENS * TOPK // P + EXPERTS
FLAT = TILES + EXPERT_TILES
PLAN = FLAT + 8
ROUND = 8
SHARED_ROUNDS = TILES // ROUND
AHEAD = 5
YBUFS = 4
ROUNDS = FLAT // ROUND
assert AHEAD <= ROUND == PLAN - FLAT
DUMMY_COL = EV * SLOT_COLS
NMOD = 6
MODC = NMOD * KC
LN_EPS = 1e-5
NEG = -3.0e38

C_ID, C_TRI, C_TRI65, C_IOTA, C_FLAT = 0, 128, 256, 256 + EV, 256 + EV + EXPERTS
C_TOK = C_FLAT + PLAN
CONSTS = C_TOK + TILES


class Tally:

    def __init__(self, sem, start=0):
        self.sem, self.start, self.n = sem, start, 0

    def mark(self, ins):
        ins.then_inc(self.sem, 1)
        self.n += 1
        return self.start + self.n


def build(nc, x_in, w_in, b_col, b_row, w_out, bout_col, gates, experts, c_t, w_mod, tables, rope_rows,
          rope_cols, out):
    slots = nc.dram_tensor("slot_table", [P * EXPERTS * SLOT_COLS, 2], I32)
    h2_rows = nc.dram_tensor("h2_rows", [ROWS, D], F32)
    acc = [nc.dram_tensor(f"ffn_sum{i}", [ROWS, D], F32) for i in range(2)]
    mod_rows = nc.dram_tensor("mod_rows", [MODC * BATCH, P], F32)

    ctx = ExitStack()
    with ctx:
        def sb(name, shape, dt=F32):
            return ctx.enter_context(nc.sbuf_tensor(name, shape, dt))

        def sem(name):
            return ctx.enter_context(nc.semaphore(name))

        x = sb("x", [P, TILES * D])
        front = sb("front", [P, KC * NMOD * D])
        wmod = front[:, :].rearrange("p (k m) -> p k m", k=KC)
        region = [front[:, i * 2048:(i + 1) * 2048] for i in range(6)]
        hT = region[0].rearrange("p (k s) -> p k s", k=KC)
        qT = region[1].rearrange("p (k s) -> p k s", k=KC)
        woa = region[2].rearrange("p (k s) -> p k s", k=KC)
        kv = region[3].rearrange("p (i d) -> p i d", i=TPB)
        kb, vb, rope_t, pool_t = (region[4][:, i * D:(i + 1) * D] for i in range(4))
        square_junk = region[5][:, 0:D]
        rope_q = [region[5][:, D:2 * D], region[5][:, 2 * D:3 * D]]
        h2_t = region[5][:, 3 * D:4 * D]
        wqkv = sb("wqkv", [P, KC * 3 * D])
        win = wqkv[:, :].rearrange("p (k e) -> p k e", k=KC)
        wo = sb("wo", [P, KC, D])
        kcos = sb("kcos", [P, TPB, ROT])
        ksin = sb("ksin", [P, TPB, ROT])
        qcos = sb("qcos", [P, SEQ])
        qsin = sb("qsin", [P, SEQ])
        bias_kv = sb("bias_kv", [P, 2, D])
        xn = sb("xn", [P, TPB, D])
        h2 = sb("h2", [P, TPB, D])
        h2T = sb("h2T", [P, KC, SEQ])
        rows_a = sb("rows_a", [P, 3, D])
        rows_b = sb("rows_b", [P, 2, D])
        rows_g = sb("rows_g", [P, BATCH, D])
        gate_w = sb("gate_w", [P, KC, EV])
        const = sb("const", [P, CONSTS])
        ident = const[:, C_ID:C_ID + P]
        tri_bf = sb("tri_bf", [P, P], BF16)
        ones_bf = sb("ones_bf", [P, P], BF16)
        ones1 = sb("ones1", [P, 1])
        tbl = sb("tbl", [P, DUMMY_COL + 1, 2], I32)
        bqc = sb("bqc", [P, KC])
        boc = sb("boc", [P, KC * BATCH])
        cT = sb("cT", [P, KC * BATCH])
        silu_c = sb("silu_c", [P, KC * BATCH])
        modc = sb("modc", [P, MODC * BATCH])
        modf = sb("modf", [P, MODC * BATCH])
        modr = sb("modr", [MODC * BATCH, P])
        scale_a = sb("scale_a", [P, KC * BATCH])
        mod_t = sb("mod_t", [P, 3, KC * BATCH])
        stats = sb("stats", [P, TPB, 6])
        mean_var = sb("mean_var", [P, TPB, 2])
        rstd = sb("rstd", [P, TPB])
        shift = sb("shift", [P, TPB])
        stats2 = sb("stats2", [P, TPB, 6])
        mean_var2 = sb("mean_var2", [P, TPB, 2])
        rstd2 = sb("rstd2", [P, TPB])
        shift2 = sb("shift2", [P, TPB])
        ksq = sb("ksq", [P, TPB])
        krn = sb("krn", [P, TPB])
        var = sb("var", [P, 3, TPB])
        root = sb("root", [P, 3, TPB])
        corr = sb("corr", [P, 3, TPB])
        asum = sb("asum", [P, KC])
        logit = sb("logit", [P, TPB, EV])
        topv = sb("topv", [P, TPB, TOPK])
        topi = sb("topi", [P, TPB, TOPK], U32)
        topif = sb("topif", [P, TPB, TOPK])
        ntop = sb("ntop", [P, TPB])
        replaced = sb("replaced", [P, TPB, EXPERTS])
        mask = sb("mask", [P, TPB, EV], BF16)
        seen = sb("seen", [P, TPB + 1, EV], BF16)
        etop = sb("etop", [P, TPB, TOPK])
        esum = sb("esum", [P, TPB])
        esh = sb("esh", [P, TPB])
        rsum = sb("rsum", [P, TPB])
        sh1 = sb("sh1", [P, TPB])
        gate_sh = sb("gate_sh", [P, TILES])
        rank_all = sb("rank_all", [P, TPB, EV])
        pick = sb("pick", [P, TOPK, EXPERTS])
        rank_f = sb("rank_f", [P, TPB, TOPK])
        rank_i = sb("rank_i", [P, TPB, TOPK], I32)
        idx_i = sb("idx_i", [P, TPB, TOPK], I32)
        place_r = sb("place_r", [P, TPB, TOPK], I32)
        place_q = sb("place_q", [P, TPB, TOPK], I32)
        place_e = sb("place_e", [P, TPB, TOPK], I32)
        place = sb("place", [P, TPB, TOPK], I32)
        pay = sb("pay", [P, TPB, TOPK, 2], I32)
        zero8 = sb("zero8", [P, TOPK])
        zrow = sb("zrow", [P, D])
        count_f = sb("count_f", [EV, 1])
        count_i = sb("count_i", [EV, 1], I32)
        tiles_i = sb("tiles_i", [EV, 1], I32)
        tiles_f = sb("tiles_f", [EV, 1])
        col_step = sb("col_step", [EV, 1])
        cum = sb("cum", [EV, 1])
        past = sb("past", [EV, PLAN])
        plan_f = sb("plan_f", [1, 2, PLAN])
        plan = sb("plan", [1, 2, PLAN], I32)
        cum_i = sb("cum_i", [1, EV], I32)
        rounds_f = sb("rounds_f", [1, 1])
        rounds_i = sb("rounds_i", [1, 1], I32)
        xg = [a[:, i, :] for a in (xn, h2) for i in range(TPB)]
        ids = [sb(f"ids{i}", [P, 2], I32) for i in range(ROUND)]
        xT = [h2T[:, i, :].rearrange("p (k t) -> p k t", k=KC) for i in range(4)]
        act = [sb(f"act{i}", [P, INNER]) for i in range(2)]
        inter = [sb(f"inter{i}", [P, INNER]) for i in range(2)]
        iT = [sb(f"iT{i}", [P, P]) for i in range(2)]
        yb = [region[5][:, i * D:(i + 1) * D] for i in range(YBUFS)]
        fa = [region[0].rearrange("p (i d) -> p i d", i=TPB), region[1].rearrange("p (i d) -> p i d", i=TPB)]
        fb = [region[2].rearrange("p (i d) -> p i d", i=TPB), region[3].rearrange("p (i d) -> p i d", i=TPB)]

        bank = [ctx.enter_context(nc.psum_tensor(f"bank{i}", [P, 512], F32)) for i in range(8)]

        s_const = sem("s_const")
        s_small = sem("s_small")
        s_wmod = sem("s_wmod")
        s_x0 = sem("s_x0")
        s_xrest = sem("s_xrest")
        s_win = sem("s_win")
        s_att = sem("s_att")
        s_modw = sem("s_modw")
        s_rows_a = sem("s_rows_a")
        s_rows_b = sem("s_rows_b")
        s_rows_g = sem("s_rows_g")
        s_zero = sem("s_zero")
        s_prefill = sem("s_prefill")
        s_h2w = sem("s_h2w")
        s_scat = sem("s_scat")
        s_tbl = sem("s_tbl")
        s_fill = sem("s_fill")
        s_silu = sem("s_silu")
        s_mod = sem("s_mod")
        s_modv = sem("s_modv")
        s_modT = sem("s_modT")
        s_modr = sem("s_modr")
        s_cst = sem("s_cst")
        s_v = sem("s_v")
        s_vl = sem("s_vl")
        s_va = sem("s_va")
        s_vb = sem("s_vb")
        s_vc = sem("s_vc")
        s_mv = sem("s_mv")
        s_var = [sem(f"s_var{i}") for i in range(3)]
        s_root = [sem(f"s_root{i}") for i in range(3)]
        s_xn = sem("s_xn")
        s_pres = sem("s_pres")
        s_res = sem("s_res")
        s_tpA = sem("s_tpA")
        s_hT = sem("s_hT")
        s_kv = sem("s_kv")
        s_kvr = sem("s_kvr")
        s_kro = sem("s_kro")
        s_ksq = sem("s_ksq")
        s_kvp = sem("s_kvp")
        s_rn = sem("s_rn")
        s_q = sem("s_q")
        s_qT = sem("s_qT")
        s_qro = sem("s_qro")
        s_as = sem("s_as")
        s_woa = sem("s_woa")
        s_o = sem("s_o")
        s_or = sem("s_or")
        s_mv2 = sem("s_mv2")
        s_xn2 = sem("s_xn2")
        s_h2m = sem("s_h2m")
        s_h2 = sem("s_h2")
        s_tpC = sem("s_tpC")
        s_h2T = sem("s_h2T")
        s_g = sem("s_g")
        s_gr = sem("s_gr")
        s_top = sem("s_top")
        s_ex = sem("s_ex")
        s_mask = sem("s_mask")
        s_rk = sem("s_rk")
        s_place = sem("s_place")
        s_cnt = sem("s_cnt")
        s_ntile = sem("s_ntile")
        s_cum = sem("s_cum")
        s_past = sem("s_past")
        s_flat = sem("s_flat")
        s_plan = sem("s_plan")
        s_w = sem("s_w")
        s_xs = [sem(f"s_xs{i}") for i in range(ROUND)]
        s_xg = [sem(f"s_xg{i}") for i in range(ROUND)]
        s_ids = sem("s_ids")
        s_T = sem("s_T")
        s_xT = sem("s_xT")
        s_G = sem("s_G")
        s_sl = sem("s_sl")
        s_in = sem("s_in")
        s_I = sem("s_I")
        s_iT = sem("s_iT")
        s_d = sem("s_d")
        s_y = sem("s_y")
        s_ss = [sem(f"s_ss{i}") for i in range(YBUFS)]
        s_sc = [sem("s_sc0"), sem("s_sc1")]
        s_fl = [sem("s_fl0"), sem("s_fl1")]
        s_fs = sem("s_fs")
        s_fm = sem("s_fm")
        s_fo = sem("s_fo")
        s_out = sem("s_out")

        x_view = x_in.rearrange("(b i p) d -> b p i d", i=TPB, p=P)
        out_view = out.rearrange("(b i p) d -> b p i d", i=TPB, p=P)
        x_tiles = x[:, :].rearrange("p (g d) -> p g d", g=TILES)
        h2_view = h2_rows[0:TOKENS, :].rearrange("(b i p) d -> b p i d", i=TPB, p=P)
        h2_tile = h2_rows[0:TOKENS, :].rearrange("(g p) d -> g p d", p=P)
        acc_tile = [a[0:TOKENS, :].rearrange("(g p) d -> g p d", p=P) for a in acc]
        acc_view = [a[0:TOKENS, :].rearrange("(b i p) d -> b p i d", i=TPB, p=P) for a in acc]
        mod_view = mod_rows[:, :].rearrange("(m c b) f -> m b c f", m=NMOD, b=BATCH)
        ex_view = experts

        def x_at(g):
            return x[:, bass.ds(g * D, D)]

        def mod_row(m, b):
            v = mod_view[m, bass.ds(b, 1), :, :].rearrange("o c f -> (o c) f")
            return v.unsqueeze(0).to_broadcast([P, KC, P])

        def apart(eng):
            eng.nop(nofuse=True)

        def rounds_used(eng):
            return eng.value_load(rounds_i[0:1, 0:1], min_val=0, max_val=ROUNDS - SHARED_ROUNDS - 1) + SHARED_ROUNDS + 1

        block = ctx.enter_context(nc.Block())

        @block.sync
        def _(sp):
            sp.dma_start(cT[:, :], c_t).then_inc(s_small, 16)
            sp.dma_start(bqc[:, :], b_col).then_inc(s_small, 16)
            sp.dma_start(boc[:, :], bout_col).then_inc(s_small, 16)
            for m in range(NMOD):
                sp.dma_start(wmod[:, :, m * D:(m + 1) * D], w_mod[:, :, m * D:(m + 1) * D]).then_inc(s_wmod, 16)
            sp.dma_start(x_tiles[:, 0:TPB, :], x_view[0]).then_inc(s_x0, 16)
            sp.dma_start(const[:, :], tables).then_inc(s_const, 16)
            sp.dma_start(win, w_in).then_inc(s_win, 16)
            sp.dma_start(bias_kv[:, :, :], b_row.unsqueeze(0).to_broadcast([P, 2, D])).then_inc(s_att, 16)
            sp.dma_start(kcos[:, :, :], rope_rows[0]).then_inc(s_att, 16)
            sp.dma_start(ksin[:, :, :], rope_rows[1]).then_inc(s_att, 16)
            sp.dma_start(qcos[:, :], rope_cols[0]).then_inc(s_att, 16)
            sp.dma_start(qsin[:, :], rope_cols[1]).then_inc(s_att, 16)
            sp.dma_start(wo[:, :, :], w_out).then_inc(s_att, 16)
            sp.dma_start(gate_w[:, :, :], gates).then_inc(s_att, 16)
            for b in range(1, BATCH):
                sp.dma_start(x_tiles[:, b * TPB:(b + 1) * TPB, :], x_view[b]).then_inc(s_xrest, 16)

            sp.wait_ge(s_modr, 1)
            sp.dma_start(mod_rows[:, :], modr[:, :]).then_inc(s_modw, 16)
            sp.wait_ge(s_modw, 16)

            def load_rows_a(b):
                for m in range(3):
                    sp.dma_start(rows_a[:, m, :].rearrange("p (c f) -> p c f", c=KC), mod_row(m, b)).then_inc(s_rows_a, 16)

            def load_rows_b(b):
                for m in range(2):
                    sp.dma_start(rows_b[:, m, :].rearrange("p (c f) -> p c f", c=KC), mod_row(3 + m, b)).then_inc(s_rows_b, 16)

            load_rows_a(0)
            load_rows_b(0)
            for b in range(BATCH):
                sp.dma_start(rows_g[:, b, :].rearrange("p (c f) -> p c f", c=KC), mod_row(5, b)).then_inc(s_rows_g, 16)
            sp.wait_ge(s_fill, 3)
            sp.dma_start(slots[:, :].rearrange("(p c) w -> p c w", p=P), tbl[:, 0:EXPERTS * SLOT_COLS, :]).then_inc(s_prefill, 16)
            sp.dma_start(h2_rows[TOKENS:ROWS, :], zrow[:, :]).then_inc(s_zero, 16)
            sp.dma_start(acc[0][TOKENS:ROWS, :], zrow[:, :]).then_inc(s_zero, 16)
            sp.dma_start(acc[1][:, :].rearrange("(g p) d -> p g d", p=P),
                         zrow[:, :].unsqueeze(1).to_broadcast([P, ROWS // P, D])).then_inc(s_zero, 16)
            sp.wait_ge(s_woa, KC)
            sp.wait_ge(s_res, TPB)
            load_rows_a(1)

            def round_sp(b, last):
                sp.wait_ge(s_h2, TPB * (b + 1))
                apart(sp)
                sp.dma_start(h2_view[bass.ds(b, 1)].rearrange("o p i d -> (o p) i d"), h2[:, :, :]).then_inc(s_h2w, 16)
                if not last:
                    load_rows_b(b + 1)

            for b in range(BATCH):
                round_sp(b, b == BATCH - 1)
                if b + 2 < BATCH:
                    sp.wait_ge(s_woa, KC * (b + 2))
                    sp.wait_ge(s_res, TPB * (b + 2))
                    load_rows_a(b + 2)

            def load_w(e):
                slot = wqkv[:, bass.ds((e & (WSLOTS - 1)) * WROW, WROW)] if not isinstance(e, int) else \
                    wqkv[:, (e % WSLOTS) * WROW:(e % WSLOTS + 1) * WROW]
                sp.dma_start(slot, ex_view[bass.ds(e, 1)].rearrange("o p w -> (o p) w")).then_inc(s_w, 16)

            sp.wait_ge(s_q, KC * BATCH)
            sp.wait_ge(s_kv, 2 * TPB * BATCH)
            for e in range(WSLOTS):
                if e:
                    sp.wait_ge(s_w, 16 * e)
                load_w(e)

            sp.wait_ge(s_h2w, 16 * BATCH)
            sp.wait_ge(s_zero, 48)

            sp.wait_ge(s_tpC, KC * BATCH)

            def load_shared(t):
                if t >= ROUND:
                    sp.wait_ge(s_T, t - ROUND + 1)
                sp.dma_start(xg[t % ROUND], h2_tile[t]).then_inc(s_xs[t % ROUND], 16)

            def store_shared(t):
                sp.wait_ge(s_y, t + 1)
                sp.dma_start(acc_tile[0][t], yb[t % YBUFS]).then_inc(s_ss[t % YBUFS], 16)

            for t in range(ROUND):
                load_shared(t)
            for t in range(TILES):
                store_shared(t)
                if t + ROUND < TILES:
                    load_shared(t + ROUND)

            sp.wait_ge(s_plan, 2)
            with sp.Fori(WSLOTS, EV) as e:
                done = sp.value_load(cum_i[0:1, bass.ds(e - WSLOTS, 1)], min_val=0, max_val=FLAT)
                sp.wait_ge(s_d, done)
                apart(sp)
                sp.wait_ge(s_w, 16 * e)
                apart(sp)
                load_w(e)

            def load_sums(b):
                if b >= 2:
                    sp.wait_ge(s_fo, TPB * (b - 1))
                sp.dma_start(fa[b % 2], acc_view[0][b]).then_inc(s_fl[b % 2], 16)
                sp.dma_start(fb[b % 2], acc_view[1][b]).then_inc(s_fl[b % 2], 16)

            used = rounds_used(sp)
            for added in s_sc:
                sp.wait_ge(added, (used - SHARED_ROUNDS) * (16 * ROUND // 2))
            apart(sp)
            load_sums(0)
            load_sums(1)
            for b in range(BATCH):
                sp.wait_ge(s_fo, TPB * (b + 1))
                sp.dma_start(out_view[b], x_tiles[:, b * TPB:(b + 1) * TPB, :]).then_inc(s_out, 16)
                if b + 2 < BATCH:
                    load_sums(b + 2)
            sp.wait_ge(s_out, 16 * BATCH)

        @block.gpsimd
        def _(pool):
            pool.memset(tbl[:, :, :], 0).then_inc(s_pres, 1)
            pool.memset(zrow[:, :], 0.0).then_inc(s_fill, 1)
            pool.memset(zero8[:, :], 0.0).then_inc(s_fill, 1)
            pool.wait_ge(s_pres, 1)
            pool.iota(tbl[:, :, 0], pattern=[[0, DUMMY_COL + 1]], base=PAD_ID, channel_multiplier=1).then_inc(s_fill, 1)

            PRES = 2 * TPB

            def residual(b):
                t = Tally(s_pres, PRES * b + 1)
                for i in range(TPB):
                    g = x_at(b * TPB + i)
                    pool.wait_ge(s_rows_a, 48 * (b + 1))
                    pool.wait_ge(s_xn, TPB * b + i + 1)
                    if i:
                        pool.wait_ge(s_res, TPB * b + i)
                    elif not (isinstance(b, int) and b == 0):
                        pool.wait_ge(s_res, TPB * b)
                    apart(pool)
                    a = t.mark(pool.tensor_tensor(pool_t, xn[:, i, :], rows_a[:, 1, :], ALU.mult))
                    c = t.mark(pool.tensor_tensor(g, g, rows_a[:, 2, :], ALU.add))
                    pool.wait_ge(s_pres, c)
                    apart(pool)
                    pool.tensor_tensor(g, g, pool_t, ALU.add).then_inc(s_res, 1)

            def finish_h2(b):
                for i in range(TPB):
                    pool.wait_ge(s_h2m, TPB * b + i + 1)
                    pool.tensor_tensor(h2[:, i, :], h2[:, i, :], rows_b[:, 1, :], ALU.add).then_inc(s_h2, 1)

            def scatter(b):
                for i in range(TPB):
                    pool.wait_ge(s_place, TPB * b + i + 1)
                    apart(pool)
                    for k in range(TOPK):
                        pool.indirect_dma_start(
                            out=slots[:, :], out_offset=bass.IndirectOffsetOnAxis(ap=place[:, i, k:k + 1], axis=0),
                            in_=pay[:, i, k, :], in_offset=None).then_inc(s_scat, 16)

            residual(0)
            pool.wait_ge(s_prefill, 16)
            residual(1)
            finish_h2(0)
            scatter(0)
            with pool.Fori(1, BATCH - 1) as b:
                residual(b + 1)
                finish_h2(b)
                scatter(b)
            finish_h2(BATCH - 1)
            scatter(BATCH - 1)
            pool.wait_ge(s_scat, 16 * TOPK * TILES)
            pool.dma_start(tbl[:, SLOT_COLS:EV * SLOT_COLS, :], slots[:, :].rearrange("(p c) w -> p c w", p=P)).then_inc(s_tbl, 16)
            pool.wait_ge(s_tbl, 16)
            pool.wait_ge(s_plan, 2)

            def added(r, s, back):
                return 16 * (ROUND // 2) * (r - SHARED_ROUNDS) + 16 * (s // 2 - back // 2 + 1)

            def gather(t, r, s):
                col = pool.value_load(plan[0:1, 0, bass.ds(t, 1)], min_val=0, max_val=DUMMY_COL)
                if not (isinstance(t, int) and t < TILES + ROUND):
                    pool.wait_ge(s_sc[s % 2], added(r, s, ROUND))
                pool.tensor_copy(ids[s][:, :], tbl[:, bass.ds(col, 1), :].rearrange("p o w -> p (o w)")).then_inc(s_ids, 1)
                pool.wait_ge(s_ids, t - TILES + 1)
                pool.wait_ge(s_T, t - ROUND + 1)
                apart(pool)
                pool.indirect_dma_start(
                    out=xg[s], out_offset=None, in_=h2_rows[:, :],
                    in_offset=bass.IndirectOffsetOnAxis(ap=ids[s][:, 0:1], axis=0)).then_inc(s_xg[s], 16)

            def add_rows(t, r, s):
                pool.wait_ge(s_y, t + 1)
                if not (isinstance(t, int) and t < TILES + 2):
                    pool.wait_ge(s_sc[s % 2], added(r, s, 2))
                apart(pool)
                pool.indirect_dma_start(
                    out=acc[s % 2][:, :], out_offset=bass.IndirectOffsetOnAxis(ap=ids[s][:, 0:1], axis=0),
                    in_=yb[s % YBUFS], in_offset=None, compute_op=ALU.add).then_inc(s_sc[s % 2], 16)

            for n in range(AHEAD):
                gather(TILES + n, SHARED_ROUNDS, n)
            for stored in s_ss:
                pool.wait_ge(stored, 16 * (TILES // YBUFS))

            def round_pool(r):
                for s in range(ROUND):
                    n = s + AHEAD
                    gather(r * ROUND + n, r + n // ROUND, n % ROUND)
                    add_rows(r * ROUND + s, r, s)

            round_pool(SHARED_ROUNDS)
            used = rounds_used(pool)
            with pool.Fori(SHARED_ROUNDS + 1, ROUNDS) as r:
                with pool.If(r < used):
                    round_pool(r)
            for n in range(AHEAD):
                pool.wait_ge(s_xg[n], (used - SHARED_ROUNDS) * 16 + 16)

            for g in range(TILES):
                b, i = divmod(g, TPB)
                pool.wait_ge(s_fl[b % 2], 32 * (b // 2 + 1))
                pool.tensor_tensor(fa[b % 2][:, i, :], fa[b % 2][:, i, :], fb[b % 2][:, i, :], ALU.add).then_inc(s_fs, 1)

        @block.scalar
        def _(sc):
            sc.wait_ge(s_small, 48)
            sc.activation(silu_c[:, :], cT[:, :], ACT.Silu).then_inc(s_silu, 1)

            def take_root(b, n):
                sc.wait_ge(s_var[n], b + 1)
                sc.activation(root[:, n, :], var[:, n, :], ACT.Sqrt).then_inc(s_root[n], 1)

            def norm1(b):
                take_root(b, 0)
                sc.wait_ge(s_mv, b + 1)
                if not (isinstance(b, int) and b == 0):
                    sc.wait_ge(s_tpA, KC * b)
                    sc.wait_ge(s_res, TPB * b)
                for i in range(TPB):
                    sc.activation(xn[:, i, :], x_at(b * TPB + i), ACT.Identity, bias=shift[:, i:i + 1],
                                  scale=rstd[:, i:i + 1]).then_inc(s_xn, 1)

            def attend(b):
                sc.wait_ge(s_modv, 3)
                if not (isinstance(b, int) and b == 0):
                    sc.wait_ge(s_q, KC * b)
                    sc.wait_ge(s_kv, 2 * TPB * b)
                for c in range(KC):
                    sc.wait_ge(s_tpA, KC * b + c + 1)
                    sc.activation(hT[:, c, :], bank[c % 2][:, :], ACT.Identity,
                                  bias=modc[:, bass.ds(c * BATCH + b, 1)],
                                  scale=scale_a[:, bass.ds(c * BATCH + b, 1)]).then_inc(s_hT, 1)
                for i in range(TPB):
                    sc.wait_ge(s_kro, TPB * b + i + 1)
                    if i == 0 and not (isinstance(b, int) and b == 0):
                        sc.wait_ge(s_rn, b)
                    if i or not (isinstance(b, int) and b == 0):
                        sc.wait_ge(s_ksq, TPB * b + i)
                    sc.activation(square_junk, kb, ACT.Square, accum_out=ksq[:, i:i + 1]).then_inc(s_ksq, 1)
                take_root(b, 2)
                if not (isinstance(b, int) and b == 0):
                    sc.wait_ge(s_o, TPB * b)
                for c in range(KC):
                    sc.wait_ge(s_q, KC * b + c + 1)
                    sc.activation(qT[:, c, :], bank[4 + c % 2][:, :], ACT.Identity,
                                  bias=bqc[:, c:c + 1]).then_inc(s_qT, 1)

            def norm2(b):
                if not (isinstance(b, int) and b == 0):
                    sc.wait_ge(s_tpC, KC * b)
                    sc.wait_ge(s_h2w, 16 * b)
                take_root(b, 1)
                sc.wait_ge(s_mv2, b + 1)
                for i in range(TPB):
                    sc.activation(h2[:, i, :], x_at(b * TPB + i), ACT.Identity, bias=shift2[:, i:i + 1],
                                  scale=rstd2[:, i:i + 1]).then_inc(s_xn2, 1)

            def route(b):
                if not (isinstance(b, int) and b == 0):
                    sc.wait_ge(s_g, TPB * b)
                for c in range(KC):
                    sc.wait_ge(s_tpC, KC * b + c + 1)
                    sc.activation(h2T[:, c, :], bank[c % 2][:, :], ACT.Copy).then_inc(s_h2T, 1)
                if not (isinstance(b, int) and b == 0):
                    sc.wait_ge(s_place, TPB * b)
                for i in range(TPB):
                    sc.wait_ge(s_top, TPB * b + i + 1)
                    sc.activation(etop[:, i, :], topv[:, i, :], ACT.Exp, bias=ntop[:, i:i + 1],
                                  accum_out=esum[:, i:i + 1]).then_inc(s_ex, 1)
                    sc.activation(esh[:, i:i + 1], logit[:, i, 0:1], ACT.Exp, scale=-1.0).then_inc(s_ex, 1)

            norm1(0)
            attend(0)
            norm1(1)
            norm2(0)
            attend(1)
            route(0)
            with sc.Fori(1, BATCH - 1) as b:
                norm1(b + 1)
                norm2(b)
                attend(b + 1)
                route(b)
            norm2(BATCH - 1)
            route(BATCH - 1)

            def take_x(t, s):
                sc.wait_ge(s_T, t + 1)
                if not (isinstance(t, int) and t < 4):
                    sc.wait_ge(s_G, t - 3)
                sc.activation(h2T[:, s % 4, :], bank[s % 2][:, :], ACT.Copy).then_inc(s_xT, 1)

            def silu(t, s):
                sc.wait_ge(s_G, t + 1)
                if not (isinstance(t, int) and t < 2):
                    sc.wait_ge(s_in, t - 1)
                sc.activation(act[s % 2][:, :], bank[2 + s % 2][:, 0:INNER], ACT.Silu).then_inc(s_sl, 1)

            def round_act(r):
                for s in range(ROUND):
                    take_x(r * ROUND + s + 1, s + 1)
                    silu(r * ROUND + s, s)

            take_x(0, 0)
            for r in range(SHARED_ROUNDS):
                round_act(r)
            sc.wait_ge(s_plan, 2)
            used = rounds_used(sc)
            with sc.Fori(SHARED_ROUNDS, ROUNDS) as r:
                with sc.If(r < used):
                    round_act(r)

        @block.vector
        def _(ve):
            def step(t, ins):
                ve.wait_ge(t.sem, t.mark(ins))

            t0 = Tally(s_v)
            ve.memset(ones_bf[:, :], 1.0).then_inc(s_cst, 1)
            ve.memset(ones1[:, :], 1.0).then_inc(s_cst, 1)
            ve.memset(mask[:, :, 0:1], 1.0).then_inc(s_cst, 1)
            ve.memset(seen[:, TPB, :], 0.0).then_inc(s_cst, 1)
            ve.wait_ge(s_const, 16)
            ve.tensor_copy(tri_bf[:, :], const[:, C_TRI:C_TRI + P]).then_inc(s_cst, 1)

            def one_over_root(t, n, to):
                step(t, ve.reciprocal(to, root[:, n, :]))
                step(t, ve.tensor_tensor(corr[:, n, :], to, to, ALU.mult))
                step(t, ve.tensor_tensor(corr[:, n, :], corr[:, n, :], var[:, n, :], ALU.mult))
                step(t, ve.tensor_scalar(corr[:, n, :], corr[:, n, :], -0.5, 1.5, ALU.mult, ALU.add))

            def stats1(b):
                t = Tally(s_vl, (2 * TPB + 5) * b)
                if not (isinstance(b, int) and b == 0):
                    ve.wait_ge(s_xn, TPB * b)
                    ve.wait_ge(s_mv, b)
                for i in range(TPB):
                    a = t.mark(ve.bn_stats(stats[:, i, :], x_at(b * TPB + i)))
                for i in range(TPB):
                    ve.wait_ge(s_vl, a - TPB + 1 + i)
                    apart(ve)
                    c = t.mark(ve.bn_aggr(mean_var[:, i, :], stats[:, i, :]))
                ve.wait_ge(s_vl, c)
                ve.tensor_scalar(var[:, 0, :], mean_var[:, :, 1], LN_EPS, None, ALU.add).then_inc(s_var[0], 1)
                ve.wait_ge(s_root[0], b + 1)
                one_over_root(t, 0, rstd[:, :])
                step(t, ve.tensor_tensor(rstd[:, :], rstd[:, :], corr[:, 0, :], ALU.mult))
                ve.scalar_tensor_tensor(out=shift[:, :], in0=mean_var[:, :, 0], scalar=-1.0, in1=rstd[:, :],
                                        op0=ALU.mult, op1=ALU.mult).then_inc(s_mv, 1)

            ve.wait_ge(s_x0, 16)
            stats1(0)

            ve.wait_ge(s_mod, 1)
            step(t0, ve.tensor_copy(modc[:, :], bank[0][:, 0:MODC * BATCH]))
            n = KC * BATCH
            sa, ca, ga, sbm, cb, gb = (modc[:, m * n:(m + 1) * n] for m in range(NMOD))
            row = [modf[:, m * n:(m + 1) * n] for m in range(NMOD)]
            for g, to in ((ga, row[0]), (gb, row[5])):
                t0.mark(ve.tensor_scalar(mod_t[:, 0, :], g, 0.0, 2.0, ALU.is_ge, ALU.mult))
                step(t0, ve.tensor_scalar(mod_t[:, 2, :], g, -1.0, 0.25, ALU.mult, ALU.max))
                step(t0, ve.tensor_tensor(mod_t[:, 1, :], g, mod_t[:, 2, :], ALU.max))
                step(t0, ve.tensor_scalar(mod_t[:, 2, :], mod_t[:, 0, :], -1.0, None, ALU.add))
                step(t0, ve.tensor_tensor(to, mod_t[:, 2, :], mod_t[:, 1, :], ALU.mult))
            ve.tensor_scalar(scale_a[:, :], ca, 1.0, None, ALU.add).then_inc(s_modv, 1)
            step(t0, ve.tensor_tensor(mod_t[:, 0, :], boc[:, :], sa, ALU.add))
            ve.wait_ge(s_modv, 1)
            t0.mark(ve.tensor_tensor(row[1], row[0], scale_a[:, :], ALU.mult))
            t0.mark(ve.tensor_tensor(row[2], row[0], mod_t[:, 0, :], ALU.mult))
            t0.mark(ve.tensor_scalar(row[3], cb, 1.0, None, ALU.add))
            step(t0, ve.tensor_copy(row[4], sbm))
            ve.tensor_copy(mod_t[:, 1, :], sbm).then_inc(s_modv, 1)
            ve.tensor_copy(mod_t[:, 2, :], sbm).then_inc(s_modv, 1)
            ve.wait_ge(s_modT, 1)
            ve.tensor_copy(modr[:, :], bank[1][0:MODC * BATCH, 0:P]).then_inc(s_modr, 1)

            VA = TPB * 6 + 4 + 5
            def attend(b):
                t = Tally(s_va, VA * b)
                for i in range(TPB):
                    ve.wait_ge(s_kv, 2 * TPB * b + 2 * i + 1)
                    if i or not (isinstance(b, int) and b == 0):
                        ve.wait_ge(s_ksq, TPB * b + i)
                        ve.wait_ge(s_kvp, TPB * b + i)
                    t.mark(ve.tensor_tensor(kb, bank[2][:, :], bias_kv[:, 0, :], ALU.add))
                    ve.wait_ge(s_va, t.start + t.n)
                    ve.nop().then_inc(s_kvr, 1)
                    t.mark(ve.tensor_tensor(rope_t[:, 0:HALF], kb[:, HALF:ROT], ksin[:, i, 0:HALF], ALU.mult))
                    c = t.mark(ve.tensor_tensor(rope_t[:, HALF:ROT], kb[:, 0:HALF], ksin[:, i, HALF:ROT], ALU.mult))
                    ve.wait_ge(s_va, c)
                    step(t, ve.tensor_tensor(kb[:, 0:ROT], kb[:, 0:ROT], kcos[:, i, :], ALU.mult))
                    step(t, ve.tensor_tensor(kb[:, 0:ROT], kb[:, 0:ROT], rope_t[:, 0:ROT], ALU.add))
                    ve.nop().then_inc(s_kro, 1)
                    ve.wait_ge(s_kv, 2 * TPB * b + 2 * i + 2)
                    step(t, ve.tensor_tensor(vb, bank[3][:, :], bias_kv[:, 1, :], ALU.add))
                    ve.nop().then_inc(s_kvr, 1)
                    if i == 0 and not (isinstance(b, int) and b == 0):
                        ve.wait_ge(s_as, b)
                    ve.tensor_tensor(kv[:, i, :], kb, vb, ALU.mult).then_inc(s_kvp, 1)
                ve.wait_ge(s_ksq, TPB * (b + 1))
                ve.tensor_scalar(var[:, 2, :], ksq[:, :], 1e-24, None, ALU.max).then_inc(s_var[2], 1)
                ve.wait_ge(s_root[2], b + 1)
                if not (isinstance(b, int) and b == 0):
                    ve.wait_ge(s_rn, b)
                    ve.wait_ge(s_as, b)
                one_over_root(t, 2, krn[:, :])
                ve.tensor_tensor(krn[:, :], krn[:, :], corr[:, 2, :], ALU.mult).then_inc(s_rn, 1)
                ve.wait_ge(s_qT, KC * b + 2)
                if not (isinstance(b, int) and b == 0):
                    ve.wait_ge(s_qro, 2 * b)
                t.mark(ve.tensor_tensor(rope_q[0], qT[:, 1, :], qsin[:, :], ALU.mult))
                c = t.mark(ve.tensor_tensor(rope_q[1], qT[:, 0, :], qsin[:, :], ALU.mult))
                ve.wait_ge(s_va, c)
                t.mark(ve.tensor_tensor(qT[:, 0, :], qT[:, 0, :], qcos[:, :], ALU.mult))
                c = t.mark(ve.tensor_tensor(qT[:, 1, :], qT[:, 1, :], qcos[:, :], ALU.mult))
                ve.wait_ge(s_va, c)
                ve.tensor_tensor(qT[:, 0, :], qT[:, 0, :], rope_q[0], ALU.subtract).then_inc(s_qro, 1)
                ve.tensor_tensor(qT[:, 1, :], qT[:, 1, :], rope_q[1], ALU.add).then_inc(s_qro, 1)
                ve.wait_ge(s_as, b + 1)
                ve.wait_ge(s_rows_a, 48 * (b + 1))
                if not (isinstance(b, int) and b == 0):
                    ve.wait_ge(s_woa, KC * b)
                step(t, ve.tensor_copy(asum[:, :], bank[6][:, 0:KC]))
                if not (isinstance(b, int) and b == 0):
                    ve.wait_ge(s_o, TPB * b)
                for k in range(KC):
                    ve.scalar_tensor_tensor(out=woa[:, k, :], in0=wo[:, k, :], scalar=asum[:, k:k + 1],
                                            in1=rows_a[:, 0, :], op0=ALU.mult, op1=ALU.mult).then_inc(s_woa, 1)
                assert t.n == VA, t.n

            VB = 3 * TPB + 5
            def finish(b):
                t = Tally(s_vb, VB * b)
                if not (isinstance(b, int) and b == 0):
                    ve.wait_ge(s_mv2, b)
                    ve.wait_ge(s_xn2, TPB * b)
                for i in range(TPB):
                    g = x_at(b * TPB + i)
                    ve.wait_ge(s_o, TPB * b + i + 1)
                    ve.wait_ge(s_res, TPB * b + i + 1)
                    step(t, ve.tensor_tensor(g, bank[4 + i % 2][:, :], g, ALU.add))
                    ve.nop().then_inc(s_or, 1)
                    step(t, ve.bn_stats(stats2[:, i, :], g))
                    apart(ve)
                    step(t, ve.bn_aggr(mean_var2[:, i, :], stats2[:, i, :]))
                ve.tensor_scalar(var[:, 1, :], mean_var2[:, :, 1], LN_EPS, None, ALU.add).then_inc(s_var[1], 1)
                ve.wait_ge(s_root[1], b + 1)
                one_over_root(t, 1, rstd2[:, :])
                step(t, ve.tensor_tensor(rstd2[:, :], rstd2[:, :], corr[:, 1, :], ALU.mult))
                ve.scalar_tensor_tensor(out=shift2[:, :], in0=mean_var2[:, :, 0], scalar=-1.0,
                                        in1=rstd2[:, :], op0=ALU.mult, op1=ALU.mult).then_inc(s_mv2, 1)
                for i in range(TPB):
                    ve.wait_ge(s_rows_b, 32 * (b + 1))
                    ve.wait_ge(s_xn2, TPB * b + i + 1)
                    ve.tensor_tensor(h2[:, i, :], h2[:, i, :], rows_b[:, 0, :], ALU.mult).then_inc(s_h2m, 1)
                assert t.n == VB

            VC = 7 * TPB + 17 * TPB + 2
            def route(b):
                t = Tally(s_vc, (VC + 1) * b)
                if not (isinstance(b, int) and b == 0):
                    ve.wait_ge(s_rk, TPB * b)
                step(t, ve.tensor_copy(seen[:, 0, :], seen[:, TPB, :]))
                if not (isinstance(b, int) and b == 0):
                    ve.wait_ge(s_scat, 16 * TOPK * TPB * b)
                ve.wait_ge(s_g, TPB * (b + 1))
                c = t.mark(ve.tensor_copy(logit[:, :, :].rearrange("p i e -> p (i e)"), bank[7][:, 0:TPB * EV]))
                ve.wait_ge(s_vc, c)
                for i in range(TPB):
                    apart(ve)
                    step(t, ve.max(topv[:, i, :], logit[:, i, 1:EV]))
                    ve.tensor_scalar(ntop[:, i:i + 1], topv[:, i, 0:1], -1.0, None, ALU.mult).then_inc(s_top, 1)
                    t.mark(ve.max_index(topi[:, i, :], topv[:, i, :], logit[:, i, 1:EV]))
                    step(t, ve.match_replace(replaced[:, i, :], topv[:, i, :], logit[:, i, 1:EV], NEG))
                    step(t, ve.tensor_tensor(mask[:, i, 1:EV], replaced[:, i, :], logit[:, i, 1:EV], ALU.not_equal))
                    step(t, ve.tensor_tensor(seen[:, i + 1, :], seen[:, i, :], mask[:, i, :], ALU.add))
                    ve.nop().then_inc(s_mask, 1)
                    t.mark(ve.tensor_copy(topif[:, i, :], topi[:, i, :]))
                    step(t, ve.tensor_copy(idx_i[:, i, :], topi[:, i, :]))
                ve.wait_ge(s_rk, TPB * (b + 1))
                step(t, ve.tensor_copy(rank_all[:, :, :].rearrange("p i e -> p (i e)"), bank[6][:, 8:8 + TPB * EV]))
                for i in range(TPB):
                    g = b * TPB + i
                    for k in range(TOPK):
                        c = t.mark(ve.scalar_tensor_tensor(
                            out=pick[:, k, :], in0=const[:, C_IOTA:C_IOTA + EXPERTS], scalar=topif[:, i, k:k + 1],
                            in1=rank_all[:, i, 1:EV], op0=ALU.is_equal, op1=ALU.mult,
                            accum_out=rank_f[:, i, k:k + 1]))
                    ve.wait_ge(s_vc, c)
                    step(t, ve.tensor_copy(rank_i[:, i, :], rank_f[:, i, :]))
                    t.mark(ve.tensor_scalar(place_r[:, i, :], rank_i[:, i, :], P - 1, 10, ALU.bitwise_and, ALU.logical_shift_left))
                    t.mark(ve.tensor_scalar(place_q[:, i, :], rank_i[:, i, :], 7, None, ALU.logical_shift_right))
                    step(t, ve.tensor_scalar(place_e[:, i, :], idx_i[:, i, :], 4, None, ALU.logical_shift_left))
                    step(t, ve.tensor_tensor(place_q[:, i, :], place_q[:, i, :], place_e[:, i, :], ALU.bitwise_or))
                    t.mark(ve.tensor_tensor(place[:, i, :], place_q[:, i, :], place_r[:, i, :], ALU.bitwise_or))
                    ve.wait_ge(s_ex, 2 * TPB * b + 2 * i + 2)
                    t.mark(ve.tensor_scalar(sh1[:, i:i + 1], esh[:, i:i + 1], 1.0, None, ALU.add))
                    step(t, ve.reciprocal(rsum[:, i:i + 1], esum[:, i:i + 1]))
                    t.mark(ve.tensor_scalar(pay[:, i, :, 0], zero8[:, :], const[:, bass.ds(C_TOK + g, 1)], None, ALU.add))
                    ve.tensor_scalar(pay[:, i, :, 1].bitcast(F32), etop[:, i, :], rsum[:, i:i + 1], None, ALU.mult).then_inc(s_gr, 1)
                    ve.wait_ge(s_gr, TPB * b + i + 1)
                    ve.reciprocal(gate_sh[:, bass.ds(g, 1)], sh1[:, i:i + 1]).then_inc(s_place, 1)
                assert t.n == VC + 1, t.n

            ve.wait_ge(s_att, 16 * 7)
            ve.wait_ge(s_fill, 3)
            attend(0)
            ve.wait_ge(s_xrest, 16 * (BATCH - 1))
            stats1(1)
            finish(0)
            attend(1)
            route(0)
            with ve.Fori(1, BATCH - 1) as b:
                stats1(b + 1)
                finish(b)
                attend(b + 1)
                route(b)
            finish(BATCH - 1)
            route(BATCH - 1)

            ve.wait_ge(s_cnt, 1)
            step(t0, ve.tensor_copy(count_i[:, :], bank[6][0:EV, 0:1]))
            step(t0, ve.tensor_scalar(count_f[:, :], count_i[:, :], float(P - 1), None, ALU.add))
            step(t0, ve.tensor_copy(count_i[:, :], count_f[:, :]))
            step(t0, ve.tensor_scalar(tiles_i[:, :], count_i[:, :], 7, None, ALU.logical_shift_right))
            step(t0, ve.tensor_copy(tiles_f[:, :], tiles_i[:, :]))
            step(t0, ve.tensor_scalar(tiles_f[:, :], tiles_f[:, :], 1.0, None, ALU.max))
            step(t0, ve.tensor_scalar(col_step[:, :], tiles_f[:, :], -1.0, float(SLOT_COLS), ALU.mult, ALU.add))
            ve.tensor_copy(tiles_f[:, :], tiles_f[:, :]).then_inc(s_ntile, 1)
            ve.wait_ge(s_cum, 1)
            step(t0, ve.tensor_copy(cum[:, :], bank[6][0:EV, 1:2]))
            t0.mark(ve.tensor_copy(cum_i[:, :], bank[6][0:1, 8:8 + EV]))
            step(t0, ve.tensor_scalar(rounds_f[:, :], bank[6][0:1, 8 + EV - 1:8 + EV], float(ROUND - 1 - ROUND * (SHARED_ROUNDS + 1)), None, ALU.add))
            step(t0, ve.tensor_copy(rounds_i[:, :], rounds_f[:, :]))
            step(t0, ve.tensor_scalar(rounds_i[:, :], rounds_i[:, :], ROUND.bit_length() - 1, None, ALU.logical_shift_right))
            ve.tensor_scalar(past[:, :], const[0:EV, C_FLAT:C_FLAT + PLAN], cum[:, 0:1], None, ALU.is_ge).then_inc(s_past, 1)
            ve.wait_ge(s_flat, 1)
            t0.mark(ve.tensor_tensor(plan_f[:, 0, :], bank[7][0:1, 0:PLAN], const[0:1, C_FLAT:C_FLAT + PLAN], ALU.add))
            step(t0, ve.tensor_scalar(plan_f[:, 1, :], bank[7][0:1, 256:256 + PLAN], float(EV - 1), None, ALU.min))
            step(t0, ve.tensor_scalar(plan_f[:, 0, :], plan_f[:, 0, :], float(DUMMY_COL), None, ALU.min))
            ve.tensor_copy(plan[:, 0, :], plan_f[:, 0, :]).then_inc(s_plan, 1)
            ve.tensor_copy(plan[:, 1, :], plan_f[:, 1, :]).then_inc(s_plan, 1)

            def gated(t, r, s, shared):
                ve.wait_ge(s_sl, t + 1)
                if not (isinstance(t, int) and t < 2):
                    ve.wait_ge(s_I, t - 1)
                w = gate_sh[:, bass.ds(t, 1)] if shared else ids[s][:, 1:2].bitcast(F32)
                ve.scalar_tensor_tensor(out=inter[s % 2][:, :], in0=bank[2 + s % 2][:, INNER:GU], scalar=w,
                                        in1=act[s % 2][:, :], op0=ALU.mult, op1=ALU.mult).then_inc(s_in, 1)

            def take_y(t, r, s):
                ve.wait_ge(s_d, t + 1)
                if not isinstance(t, int) or t >= TILES + YBUFS:
                    ve.wait_ge(s_sc[s % 2], 16 * (ROUND // 2) * (r - SHARED_ROUNDS) + 16 * (s // 2 - YBUFS // 2 + 1))
                elif t >= YBUFS:
                    ve.wait_ge(s_ss[t % YBUFS], 16 * (t // YBUFS if t < TILES else TILES // YBUFS))
                ve.tensor_copy(yb[s % YBUFS], bank[4 + s % 2][:, :]).then_inc(s_y, 1)

            def take_inter(t, s):
                ve.wait_ge(s_I, t + 1)
                if not (isinstance(t, int) and t < 2):
                    ve.wait_ge(s_d, t - 1)
                ve.tensor_copy(iT[s % 2][:, :], bank[6 + s % 2][:, 0:P]).then_inc(s_iT, 1)

            def round_ve(r, shared, first=False):
                for s in range(ROUND):
                    t = r * ROUND + s
                    before = (t - 1, r, s - 1) if s else (t - 1, r - 1, ROUND - 1)
                    if not (first and s == 0):
                        take_inter(t - 1, (s - 1) % ROUND)
                    gated(t, r, s, shared)
                    if not (first and s == 0):
                        take_y(*before)

            for r in range(SHARED_ROUNDS):
                round_ve(r, True, first=(r == 0))
            ve.wait_ge(s_tbl, 16)
            round_ve(SHARED_ROUNDS, False)
            ve.wait_ge(s_plan, 2)
            used = rounds_used(ve)
            with ve.Fori(SHARED_ROUNDS + 1, ROUNDS) as r:
                with ve.If(r < used):
                    round_ve(r, False)
            take_inter(used * ROUND - 1, ROUND - 1)
            take_y(used * ROUND - 1, used - 1, ROUND - 1)

            for g in range(TILES):
                b, i = divmod(g, TPB)
                ve.wait_ge(s_fs, g + 1)
                ve.wait_ge(s_rows_g, 16 * BATCH)
                ve.tensor_tensor(fa[b % 2][:, i, :], fa[b % 2][:, i, :], rows_g[:, b, :], ALU.mult).then_inc(s_fm, 1)
                ve.wait_ge(s_fm, g + 1)
                ve.tensor_tensor(x_at(g), x_at(g), fa[b % 2][:, i, :], ALU.add).then_inc(s_fo, 1)

        @block.tensor
        def _(pe):
            pe.wait_ge(s_silu, 1)
            pe.wait_ge(s_wmod, 16 * NMOD)
            for n in range(MODC):
                for k in range(KC):
                    mm = pe.matmul(bank[0][:, n * BATCH:(n + 1) * BATCH], wmod[:, k, n * P:(n + 1) * P],
                                   silu_c[:, k * BATCH:(k + 1) * BATCH], start=(k == 0), stop=(k == KC - 1))
            mm.then_inc(s_mod, 1)
            pe.wait_ge(s_modv, 3)
            pe.wait_ge(s_const, 16)
            pe.transpose(bank[1][0:MODC * BATCH, 0:P], modf[:, :], ident).then_inc(s_modT, 1)
            pe.wait_ge(s_modr, 1)
            pe.wait_ge(s_win, 16)

            def attend(b):
                for c in range(KC):
                    if c == 0 and not (isinstance(b, int) and b == 0):
                        pe.wait_ge(s_hT, KC * b)
                        if not (isinstance(b, int) and b == 1):
                            pe.wait_ge(s_h2T, KC * (b - 1))
                    if c >= 2:
                        pe.wait_ge(s_hT, KC * b + c - 1)
                    for i in range(TPB):
                        if c == 0:
                            pe.wait_ge(s_xn, TPB * b + i + 1)
                        mm = pe.transpose(bank[c % 2][:, i * P:(i + 1) * P], xn[:, i, c * P:(c + 1) * P], ident)
                    mm.then_inc(s_tpA, 1)
                pe.wait_ge(s_hT, KC * (b + 1))
                for i in range(TPB):
                    for j in range(2):
                        if i or not (isinstance(b, int) and b == 0):
                            pe.wait_ge(s_kvr, 2 * TPB * b + 2 * (i - 1) + j + 1)
                        for k in range(KC):
                            mm = pe.matmul(bank[2 + j][:, :], hT[:, k, i * P:(i + 1) * P],
                                           win[:, k, (j + 1) * D:(j + 2) * D], start=(k == 0), stop=(k == KC - 1))
                        mm.then_inc(s_kv, 1)

                def queries(c):
                    if c < 2 and not (isinstance(b, int) and b == 0):
                        pe.wait_ge(s_or, TPB * b)
                    if c >= 2:
                        pe.wait_ge(s_qT, KC * b + c - 1)
                    for k in range(KC):
                        mm = pe.matmul(bank[4 + c % 2][:, :], win[:, k, c * P:(c + 1) * P], hT[:, k, :],
                                       start=(k == 0), stop=(k == KC - 1))
                    mm.then_inc(s_q, 1)

                queries(0)
                queries(1)
                pe.wait_ge(s_rn, b + 1)
                pe.wait_ge(s_kvp, TPB * (b + 1))
                if not (isinstance(b, int) and b == 0):
                    pe.wait_ge(s_woa, KC * b)
                if not (isinstance(b, int) and b <= 1):
                    pe.wait_ge(s_place, TPB * (b - 1))
                for c in range(KC):
                    for i in range(TPB):
                        mm = pe.matmul(bank[6][:, c:c + 1], kv[:, i, c * P:(c + 1) * P], krn[:, i:i + 1],
                                       start=(i == 0), stop=(i == TPB - 1))
                mm.then_inc(s_as, 1)
                queries(2)
                queries(3)

            def project(b):
                pe.wait_ge(s_qT, KC * (b + 1))
                pe.wait_ge(s_qro, 2 * (b + 1))
                pe.wait_ge(s_woa, KC * (b + 1))
                for i in range(TPB):
                    if i >= 2:
                        pe.wait_ge(s_or, TPB * b + i - 1)
                    for k in range(KC):
                        mm = pe.matmul(bank[4 + i % 2][:, :], qT[:, k, i * P:(i + 1) * P], woa[:, k, :],
                                       start=(k == 0), stop=(k == KC - 1))
                    mm.then_inc(s_o, 1)

            def route(b, hT_done):
                pe.wait_ge(s_h2, TPB * (b + 1))
                pe.wait_ge(s_hT, hT_done)
                if not (isinstance(b, int) and b == 0):
                    pe.wait_ge(s_top, TPB * b)
                    pe.wait_ge(s_place, TPB * b)
                for c in range(KC):
                    if c >= 2:
                        pe.wait_ge(s_h2T, KC * b + c - 1)
                    for i in range(TPB):
                        mm = pe.transpose(bank[c % 2][:, i * P:(i + 1) * P], h2[:, i, c * P:(c + 1) * P], ident)
                    mm.then_inc(s_tpC, 1)
                pe.wait_ge(s_h2T, KC * (b + 1))
                for i in range(TPB):
                    for k in range(KC):
                        mm = pe.matmul(bank[7][:, i * EV:(i + 1) * EV], h2T[:, k, i * P:(i + 1) * P], gate_w[:, k, :],
                                       start=(k == 0), stop=(k == KC - 1))
                    mm.then_inc(s_g, 1)
                for i in range(TPB):
                    pe.wait_ge(s_mask, TPB * b + i + 1)
                    o = bank[6][:, 8 + i * EV:8 + (i + 1) * EV]
                    pe.matmul(o, tri_bf[:, :], mask[:, i, :], start=True, stop=False)
                    pe.matmul(o, ones_bf[:, :], seen[:, i, :], start=False, stop=True).then_inc(s_rk, 1)

            pe.wait_ge(s_cst, 5)
            attend(0)
            pe.wait_ge(s_att, 16 * 7)
            project(0)
            attend(1)
            route(0, KC * 2)
            with pe.Fori(1, BATCH - 1) as b:
                project(b)
                attend(b + 1)
                route(b, KC * (b + 2))
            project(BATCH - 1)
            route(BATCH - 1, KC * BATCH)

            pe.wait_ge(s_place, TILES)
            pe.matmul(bank[6][0:EV, 0:1], seen[:, TPB, :], ones_bf[:, 0:1], start=True, stop=True).then_inc(s_cnt, 1)
            pe.wait_ge(s_ntile, 1)
            pe.matmul(bank[6][0:EV, 1:2], const[0:EV, C_TRI65:C_TRI65 + EV], tiles_f[:, :], start=True, stop=True)
            pe.matmul(bank[6][0:1, 8:8 + EV], tiles_f[:, :], const[0:EV, C_TRI65:C_TRI65 + EV],
                      start=True, stop=True).then_inc(s_cum, 1)
            pe.wait_ge(s_past, 1)
            pe.matmul(bank[7][0:1, 0:PLAN], col_step[:, :], past[:, :], start=True, stop=True)
            pe.matmul(bank[7][0:1, 256:256 + PLAN], ones1[0:EV, :], past[:, :], start=True, stop=True).then_inc(s_flat, 1)

            def turn(t, r, s):
                if isinstance(t, int) and t < TILES:
                    pe.wait_ge(s_xs[s], 16 * (r + 1))
                else:
                    pe.wait_ge(s_xg[s], 16 * (r - SHARED_ROUNDS + 1))
                if not (isinstance(t, int) and t < 2):
                    pe.wait_ge(s_xT, t - 1)
                for k in range(KC):
                    mm = pe.transpose(bank[s % 2][:, k * P:(k + 1) * P], xg[s][:, k * P:(k + 1) * P], ident)
                mm.then_inc(s_T, 1)

            def gate_up(t, s, w):
                pe.wait_ge(s_xT, t + 1)
                if not (isinstance(t, int) and t < 2):
                    pe.wait_ge(s_in, t - 1)
                for k in range(KC):
                    mm = pe.matmul(bank[2 + s % 2][:, 0:GU], xT[s % 4][:, k, :], wqkv[:, bass.ds(w + k * GU, GU)],
                                   start=(k == 0), stop=(k == KC - 1))
                mm.then_inc(s_G, 1)

            def down(t, s, w):
                pe.wait_ge(s_iT, t + 1)
                if not (isinstance(t, int) and t < 2):
                    pe.wait_ge(s_y, t - 1)
                pe.matmul(bank[4 + s % 2][:, :], iT[s % 2][:, :], wqkv[:, bass.ds(w + KC * GU, D)],
                          start=True, stop=True).then_inc(s_d, 1)

            def turn_inter(t, s):
                pe.wait_ge(s_in, t + 1)
                if not (isinstance(t, int) and t < 2):
                    pe.wait_ge(s_iT, t - 1)
                pe.transpose(bank[6 + s % 2][:, 0:P], inter[s % 2][:, :], ident).then_inc(s_I, 1)

            def expert_of(t):
                e = pe.value_load(plan[0:1, 1, bass.ds(t, 1)], min_val=0, max_val=EXPERTS)
                return (e & (WSLOTS - 1)) * WROW, e * 16 + 16

            def round_pe(r, shared):
                w = [0] * (ROUND + 2)
                for s in range(ROUND):
                    t = r * ROUND + s
                    old = not (isinstance(t, int) and t < 2)
                    if old:
                        turn_inter(t - 2, s % 2)
                    turn(t + 1, r + (s + 1) // ROUND, (s + 1) % ROUND)
                    if not shared:
                        if s == 0 and not (isinstance(r, int) and r == SHARED_ROUNDS):
                            w[0], w[1] = expert_of(t - 2)[0], expert_of(t - 1)[0]
                        w[s + 2], loaded = expert_of(t)
                    if old:
                        down(t - 2, s % 2, w[s])
                    if not shared:
                        pe.wait_ge(s_w, loaded)
                    gate_up(t, s, w[s + 2])

            pe.wait_ge(s_w, 16)
            turn(0, 0, 0)
            for r in range(SHARED_ROUNDS):
                round_pe(r, True)
            pe.wait_ge(s_plan, 2)
            round_pe(SHARED_ROUNDS, False)
            used = rounds_used(pe)
            with pe.Fori(SHARED_ROUNDS + 1, ROUNDS) as r:
                with pe.If(r < used):
                    round_pe(r, False)
            for n in range(2):
                t = used * ROUND - 2 + n
                turn_inter(t, n)
                down(t, n, expert_of(t)[0])


def _constants():
    c = np.zeros((P, CONSTS), np.float32)
    c[:, C_ID:C_ID + P] = np.eye(P)
    c[:, C_TRI:C_TRI + P] = np.triu(np.ones((P, P)), 1)
    c[:EV, C_TRI65:C_TRI65 + EV] = np.triu(np.ones((EV, EV)))
    c[:, C_IOTA:C_IOTA + EXPERTS] = np.arange(EXPERTS)
    c[:, C_FLAT:C_FLAT + PLAN] = np.arange(PLAN)
    c[:, C_TOK:C_TOK + TILES] = np.arange(TILES)[None, :] * P + np.arange(P)[:, None]
    inv = (1.0 / np.float32(10000.0) ** (np.arange(0, ROT, 2, dtype=np.float32) / np.float32(ROT))).astype(np.float32)
    freqs = np.arange(SEQ, dtype=np.float32)[:, None] * inv[None, :]
    cos = np.cos(freqs.astype(np.float64)).astype(np.float32)
    sin = np.sin(freqs.astype(np.float64)).astype(np.float32)
    by_row = lambda a: np.ascontiguousarray(a.reshape(TPB, P, ROT).transpose(1, 0, 2))
    rows = np.stack([by_row(np.concatenate([cos, cos], 1)), by_row(np.concatenate([-sin, sin], 1))])
    cols = np.ascontiguousarray(np.stack([cos.T, sin.T]))
    return c, rows, cols


def _layout(i):
    g = {n: np.asarray(a) for n, a in i.items()}
    order = np.concatenate([np.arange(0, ROT, 2), np.arange(1, ROT, 2), np.arange(ROT, D)])
    qkv = np.concatenate([order, D + order, 2 * D + order])
    chunks = lambda a: np.ascontiguousarray(a.reshape(KC, P, -1).transpose(1, 0, 2))
    w_in = chunks(g["L0_attn_W_in"][qkv].T)
    b_in = g["L0_attn_b_in"][qkv]
    w_out = chunks(g["L0_attn_W_out"].T[order])
    bout = np.ascontiguousarray(np.repeat(g["L0_attn_b_out"].reshape(KC, P).T[:, :, None], BATCH, 2).reshape(P, -1))
    gates = chunks(np.concatenate([g["L0_ffn_sh_gate1_w"], g["L0_ffn_gate_w"]]).T)
    gu = np.concatenate([np.concatenate([g["L0_ffn_sh_gate_w"], g["L0_ffn_sh_up_w"]])[None], g["L0_ffn_gu_w"]])
    gu = gu.transpose(0, 2, 1).reshape(EV, KC, P, GU).transpose(0, 2, 1, 3).reshape(EV, P, KC * GU)
    dp = np.concatenate([g["L0_ffn_sh_down_w"][None], g["L0_ffn_dp_w"]]).transpose(0, 2, 1)
    experts = np.ascontiguousarray(np.concatenate([gu, dp], 2))
    c_t = np.ascontiguousarray(g["L0_c"].reshape(BATCH, KC, P).transpose(2, 1, 0).reshape(P, -1))
    w_mod = chunks(g["L0_wmod"])
    c, rows, cols = _constants()
    return {
        "x": np.ascontiguousarray(g["L0_attn_X"].reshape(TOKENS, D)), "w_in": w_in,
        "b_col": np.ascontiguousarray(b_in[:D].reshape(KC, P).T), "b_row": np.ascontiguousarray(b_in[D:].reshape(2, D)),
        "w_out": w_out, "bout_col": bout, "gates": gates, "experts": experts, "c_t": c_t, "w_mod": w_mod,
        "tables": c, "rope_rows": rows, "rope_cols": cols,
    }


def kernel(**inputs):
    import concourse.bacc as _bacc
    from concourse.bass_utils import run_bass_kernel_spmd as _run

    nc = _bacc.Bacc("TRN2", target_bir_lowering=False, num_devices=1)
    arrays, args = {}, []
    for name, a in _layout(inputs).items():
        arrays[f"in_{name}"] = a
        args.append(nc.dram_tensor(f"in_{name}", a.shape, mybir.dt.from_np(a.dtype), kind="ExternalInput").ap())
    out = nc.dram_tensor("out_dram", (TOKENS, D), F32, kind="ExternalOutput").ap()
    build(nc, *args, out)
    r = _run(nc, [arrays], core_ids=[0])
    return r.results[0]["out_dram"].reshape(BATCH, SEQ, D)
```

```python
from contextlib import ExitStack

import numpy as np

import concourse.bass as bass
from concourse import mybir

ALU = mybir.AluOpType
ACT = mybir.ActivationFunctionType
F32 = mybir.dt.float32
BF16 = mybir.dt.bfloat16
I32 = mybir.dt.int32
U32 = mybir.dt.uint32

P = 128
BATCH = 4
SEQ = 512
D = 512
KC = D // P
TPB = SEQ // P
TOKENS = BATCH * SEQ
TILES = TOKENS // P
ROT = D // 2
HALF = ROT // 2
EXPERTS = 64
TOPK = 8
INNER = 128
EV = EXPERTS + 1
GU = 2 * INNER
WROW = KC * GU + D
WSLOTS = 4
SLOT_COLS = TOKENS // P
PAD_ID = TOKENS
ROWS = TOKENS + P
EXPERT_TILES = TOKENS * TOPK // P + EXPERTS
PLAN = EXPERT_TILES + 8
ROUND = 8
AHEAD = 5
YBUFS = 4
ROUNDS = EXPERT_TILES // ROUND
assert AHEAD <= ROUND == PLAN - EXPERT_TILES
DUMMY_COL = EV * SLOT_COLS
NMOD = 6
LN_EPS = 1e-5
NEG = -3.0e38

C_ID, C_TRI, C_TRI65, C_IOTA, C_FLAT = 0, 128, 256, 256 + EV, 256 + EV + EXPERTS
C_TOK = C_FLAT + PLAN
CONSTS = C_TOK + TILES


class Tally:

    def __init__(self, sem, start=0):
        self.sem, self.start, self.n = sem, start, 0

    def mark(self, ins):
        ins.then_inc(self.sem, 1)
        self.n += 1
        return self.start + self.n


def build(nc, x_in, w_in, b_col, b_row, w_out, b_out, gates, experts, c_t, w_mod, tables, rope_rows,
          rope_cols, out):
    slots = nc.dram_tensor("slot_table", [P * EXPERTS * SLOT_COLS, 2], I32)
    h2_rows = nc.dram_tensor("h2_rows", [ROWS, D], F32)
    acc = [nc.dram_tensor(f"ffn_sum{i}", [ROWS, D], F32) for i in range(2)]
    mod_rows = nc.dram_tensor("mod_rows", [BATCH, NMOD * D], F32)

    ctx = ExitStack()
    with ctx:
        def sb(name, shape, dt=F32):
            return ctx.enter_context(nc.sbuf_tensor(name, shape, dt))

        def sem(name):
            return ctx.enter_context(nc.semaphore(name))

        x = sb("x", [P, TILES * D])
        front = sb("front", [P, KC * NMOD * D])
        region = [front[:, i * KC * D:(i + 1) * KC * D] for i in range(NMOD)]
        wmod = [region[i].rearrange("p (k d) -> p k d", k=KC) for i in (0, 3, 4, 1, 2, 5)]
        hT = region[0].rearrange("p (k s) -> p k s", k=KC)
        qT = region[1].rearrange("p (k s) -> p k s", k=KC)
        woa = region[2].rearrange("p (k s) -> p k s", k=KC)
        kv = region[3].rearrange("p (i d) -> p i d", i=TPB)
        kb, vb, rope_t, pool_t = (region[4][:, i * D:(i + 1) * D] for i in range(4))
        rope_q = [region[5][:, D:2 * D], region[5][:, 2 * D:3 * D]]
        shared_out = region[5][:, 3 * D:4 * D]
        shared_w = sb("shared_w", [P, WROW])
        shared_act = sb("shared_act", [P, SEQ])
        shared_inter = sb("shared_inter", [P, SEQ])
        square_junk = shared_act[:, :]
        wqkv = sb("wqkv", [P, KC * 3 * D])
        win = wqkv[:, :].rearrange("p (k e) -> p k e", k=KC)
        wo = sb("wo", [P, KC, D])
        kcos = sb("kcos", [P, TPB, ROT])
        ksin = sb("ksin", [P, TPB, ROT])
        qcos = sb("qcos", [P, SEQ])
        qsin = sb("qsin", [P, SEQ])
        bias_kv = sb("bias_kv", [P, 2, D])
        xn = sb("xn", [P, TPB, D])
        h2 = sb("h2", [P, TPB, D])
        h2T = sb("h2T", [P, KC, SEQ])
        rows_a = sb("rows_a", [P, 3, D])
        rows_b = sb("rows_b", [P, 2, D])
        rows_g = sb("rows_g", [P, BATCH, D])
        gate_w = sb("gate_w", [P, KC, EV])
        const = sb("const", [P, CONSTS])
        ident = const[:, C_ID:C_ID + P]
        tri_bf = sb("tri_bf", [P, P], BF16)
        ones_bf = sb("ones_bf", [P, P], BF16)
        ones1 = sb("ones1", [P, 1])
        tbl = sb("tbl", [P, DUMMY_COL + 1, 2], I32)
        bqc = sb("bqc", [P, KC])
        cT = sb("cT", [P, KC * BATCH])
        silu_c = sb("silu_c", [P, KC * BATCH])
        firstc = sb("firstc", [P, 2 * KC * BATCH])
        secondc = sb("secondc", [P, 2 * KC * BATCH])
        stats = sb("stats", [P, TPB, 6])
        mean_var = sb("mean_var", [P, TPB, 2])
        rstd = sb("rstd", [P, TPB])
        shift = sb("shift", [P, TPB])
        stats2 = sb("stats2", [P, TPB, 6])
        mean_var2 = sb("mean_var2", [P, TPB, 2])
        rstd2 = sb("rstd2", [P, TPB])
        shift2 = sb("shift2", [P, TPB])
        ksq = sb("ksq", [P, TPB])
        krn = sb("krn", [P, TPB])
        var = sb("var", [P, 3, TPB])
        root = sb("root", [P, 3, TPB])
        corr = sb("corr", [P, 3, TPB])
        asum = sb("asum", [P, KC])
        logit = sb("logit", [P, TPB, EV])
        topv = sb("topv", [P, TPB, TOPK])
        topi = sb("topi", [P, TPB, TOPK], U32)
        topif = sb("topif", [P, TPB, TOPK])
        ntop = sb("ntop", [P, TPB])
        replaced = sb("replaced", [P, TPB, EXPERTS])
        mask = sb("mask", [P, TPB, EV], BF16)
        seen = sb("seen", [P, TPB + 1, EV], BF16)
        etop = sb("etop", [P, TPB, TOPK])
        esum = sb("esum", [P, TPB])
        esh = sb("esh", [P, TPB])
        rsum = sb("rsum", [P, TPB])
        sh1 = sb("sh1", [P, TPB])
        gate_sh = sb("gate_sh", [P, TILES])
        rank_all = sb("rank_all", [P, TPB, EV])
        pick = region[5][:, 0:D].rearrange("p (k e) -> p k e", k=TOPK)
        rank_f = sb("rank_f", [P, TPB, TOPK])
        rank_i = sb("rank_i", [P, TPB, TOPK], I32)
        idx_i = sb("idx_i", [P, TPB, TOPK], I32)
        place_r = sb("place_r", [P, TPB, TOPK], I32)
        place_q = sb("place_q", [P, TPB, TOPK], I32)
        place_e = sb("place_e", [P, TPB, TOPK], I32)
        place = [sb(f"place{i}", [P, TPB, TOPK], I32) for i in range(2)]
        pay = [sb(f"pay{i}", [P, TPB, TOPK, 2], I32) for i in range(2)]
        zrow = sb("zrow", [P, D])
        count_f = sb("count_f", [EV, 1])
        count_i = sb("count_i", [EV, 1], I32)
        tiles_i = sb("tiles_i", [EV, 1], I32)
        tiles_f = sb("tiles_f", [EV, 1])
        col_step = sb("col_step", [EV, 1])
        cum = sb("cum", [EV, 1])
        past = sb("past", [EV, PLAN])
        plan_f = sb("plan_f", [1, 2, PLAN])
        plan = sb("plan", [1, 2, PLAN], I32)
        cum_i = sb("cum_i", [1, EV], I32)
        rounds_f = sb("rounds_f", [1, 1])
        rounds_i = sb("rounds_i", [1, 1], I32)
        xg = [a[:, i, :] for a in (xn, h2) for i in range(TPB)]
        ids = [sb(f"ids{i}", [P, 2], I32) for i in range(ROUND)]
        xT = [h2T[:, i, :].rearrange("p (k t) -> p k t", k=KC) for i in range(4)]
        act, inter, iT = ([region[5][:, (2 * j + i) * P:(2 * j + i + 1) * P] for i in range(2)] for j in range(3))
        yb = [region[4][:, i * D:(i + 1) * D] for i in range(YBUFS)]
        sum_a = front[:, 0:TILES * D].rearrange("p (g d) -> p g d", g=TILES)
        b_front = (KC * NMOD - TILES)
        sum_b = [front[:, TILES * D:].rearrange("p (g d) -> p g d", g=b_front)[:, g, :] if g < b_front else
                 wqkv[:, (g - b_front) * D:(g - b_front + 1) * D] for g in range(TILES)]

        modr = [h2[0:BATCH, 0:3, :], h2T[0:BATCH, 0:3, :]]
        bout_r = h2[0:BATCH, 3, :]
        first = [h2T[0:BATCH, 3, :], shared_inter[0:BATCH, :]]
        mod_t = [shared_w[0:BATCH, i * D:(i + 1) * D] for i in range(3)]

        bank = [ctx.enter_context(nc.psum_tensor(f"bank{i}", [P, 512], F32)) for i in range(8)]

        mod_bank = [bank[m][0:BATCH, :] for m in (0, 1, 4, 6, 7, 0)]

        s_const = sem("s_const")
        s_small = sem("s_small")
        s_wmod = [sem(f"s_wmod{i}") for i in range(NMOD)]
        s_x0 = sem("s_x0")
        s_x1 = sem("s_x1")
        s_xrest = sem("s_xrest")
        s_win = [sem("s_win_q"), sem("s_win_kv")]
        s_att = sem("s_att")
        s_late = sem("s_late")
        s_modw = sem("s_modw")
        s_rows_a = sem("s_rows_a")
        s_rows_b = sem("s_rows_b")
        s_rows_g = sem("s_rows_g")
        s_zero = sem("s_zero")
        s_prefill = sem("s_prefill")
        s_h2w = sem("s_h2w")
        s_scat = [sem("s_scat0"), sem("s_scat1")]
        s_tbl = [sem(f"s_tbl{i}") for i in range(4)]
        s_fill = sem("s_fill")
        s_silu = sem("s_silu")
        s_mod = sem("s_mod")
        s_modv = sem("s_modv")
        s_modT = sem("s_modT")
        s_modr = sem("s_modr")
        s_first = sem("s_first")
        s_cst = sem("s_cst")
        s_v = sem("s_v")
        s_vl = sem("s_vl")
        s_va = sem("s_va")
        s_vb = sem("s_vb")
        s_vq = sem("s_vq")
        s_vc = sem("s_vc")
        s_vd = sem("s_vd")
        s_mv = sem("s_mv")
        s_var = [sem(f"s_var{i}") for i in range(3)]
        s_root = [sem(f"s_root{i}") for i in range(3)]
        s_xn = sem("s_xn")
        s_pres = sem("s_pres")
        s_res = sem("s_res")
        s_tpA = sem("s_tpA")
        s_hT = sem("s_hT")
        s_kv = sem("s_kv")
        s_kvr = sem("s_kvr")
        s_kro = sem("s_kro")
        s_ksq = sem("s_ksq")
        s_kvp = sem("s_kvp")
        s_rn = sem("s_rn")
        s_q = sem("s_q")
        s_qT = sem("s_qT")
        s_qro = sem("s_qro")
        s_as = sem("s_as")
        s_woa = sem("s_woa")
        s_o = sem("s_o")
        s_or = sem("s_or")
        s_mv2 = sem("s_mv2")
        s_xn2 = sem("s_xn2")
        s_h2m = sem("s_h2m")
        s_shw = sem("s_shw")
        s_shg = sem("s_shg")
        s_shs = sem("s_shs")
        s_shi = sem("s_shi")
        s_shd = sem("s_shd")
        s_sht = sem("s_sht")
        s_shx = sem("s_shx")
        s_h2 = sem("s_h2")
        s_tpC = sem("s_tpC")
        s_h2T = sem("s_h2T")
        s_g = sem("s_g")
        s_gate = sem("s_gate")
        s_top = sem("s_top")
        s_ex = sem("s_ex")
        s_mask = sem("s_mask")
        s_rk = sem("s_rk")
        s_rd = sem("s_rd")
        s_pay = sem("s_pay")
        s_place = sem("s_place")
        s_cnt = sem("s_cnt")
        s_ntile = sem("s_ntile")
        s_cum = sem("s_cum")
        s_past = sem("s_past")
        s_flat = sem("s_flat")
        s_plan = sem("s_plan")
        s_w = sem("s_w")
        s_xg = [sem(f"s_xg{i}") for i in range(ROUND)]
        s_ids = sem("s_ids")
        s_T = sem("s_T")
        s_xT = sem("s_xT")
        s_G = sem("s_G")
        s_sl = sem("s_sl")
        s_in = sem("s_in")
        s_I = sem("s_I")
        s_iT = sem("s_iT")
        s_d = sem("s_d")
        s_y = sem("s_y")
        s_sc = [sem("s_sc0"), sem("s_sc1")]
        s_fl = [sem(f"s_fl{i}") for i in range(TILES // 2)]
        s_fs = sem("s_fs")
        s_fm = sem("s_fm")
        s_fo = sem("s_fo")
        s_out = sem("s_out")

        x_view = x_in.rearrange("(b i p) d -> b p i d", i=TPB, p=P)
        out_view = out.rearrange("(g p) d -> p g d", p=P)
        x_tiles = x[:, :].rearrange("p (g d) -> p g d", g=TILES)
        h2_view = h2_rows[0:TOKENS, :].rearrange("(b i p) d -> b p i d", i=TPB, p=P)
        acc_view = [a[0:TOKENS, :].rearrange("(g p) d -> p g d", p=P) for a in acc]

        def x_at(g):
            return x[:, bass.ds(g * D, D)]

        def mod_row(m, b):
            return mod_rows[b, m * D:(m + 1) * D].unsqueeze(0).to_broadcast([P, D])

        def apart(eng):
            eng.nop(nofuse=True)

        def finish_h2(eng, b):
            eng.wait_ge(s_rows_b, 32 * (b + 1))
            eng.wait_ge(s_tpC, KC * (b + 1))
            for i in range(TPB):
                eng.tensor_tensor(h2[:, i, :], h2[:, i, :], rows_b[:, 0, :], ALU.mult).then_inc(s_h2m, 1)
                eng.wait_ge(s_h2m, TPB * b + i + 1)
                eng.tensor_tensor(h2[:, i, :], h2[:, i, :], rows_b[:, 1, :], ALU.add).then_inc(s_h2, 1)

        def rounds_used(eng):
            return eng.value_load(rounds_i[0:1, 0:1], min_val=0, max_val=ROUNDS - 1) + 1

        block = ctx.enter_context(nc.Block())

        @block.sync
        def _(sp):
            sp.dma_start(cT[:, :], c_t).then_inc(s_small, 16)
            sp.dma_start(bqc[:, :], b_col).then_inc(s_small, 16)
            sp.dma_start(bout_r, b_out.to_broadcast([BATCH, D])).then_inc(s_small, 16)
            def load_wmod(m):
                sp.dma_start(wmod[m], w_mod[:, :, m * D:(m + 1) * D]).then_inc(s_wmod[m], 16)

            load_wmod(0)
            sp.dma_start(x_tiles[:, 0:TPB, :], x_view[0]).then_inc(s_x0, 16)
            load_wmod(1)
            sp.dma_start(const[:, :], tables).then_inc(s_const, 16)
            load_wmod(2)
            sp.dma_start(win[:, :, D:3 * D], w_in[:, :, D:3 * D]).then_inc(s_win[1], 16)
            sp.dma_start(bias_kv[:, :, :], b_row.unsqueeze(0).to_broadcast([P, 2, D])).then_inc(s_att, 16)
            sp.dma_start(kcos[:, :, :], rope_rows[0]).then_inc(s_att, 16)
            sp.dma_start(ksin[:, :, :], rope_rows[1]).then_inc(s_att, 16)
            sp.dma_start(win[:, :, 0:D], w_in[:, :, 0:D]).then_inc(s_win[0], 16)
            sp.dma_start(qcos[:, :], rope_cols[0]).then_inc(s_late, 16)
            sp.dma_start(qsin[:, :], rope_cols[1]).then_inc(s_late, 16)
            sp.dma_start(wo[:, :, :], w_out).then_inc(s_late, 16)
            sp.dma_start(gate_w[:, :, :], gates).then_inc(s_late, 16)

            def load_rows_a(b):
                for m in range(3):
                    sp.dma_start(rows_a[:, m, :], mod_row(m, b)).then_inc(s_rows_a, 16)

            def load_rows_b(b):
                for m in range(2):
                    sp.dma_start(rows_b[:, m, :], mod_row(3 + m, b)).then_inc(s_rows_b, 16)

            def store_rows(half):
                sp.wait_ge(s_modr, half + 1)
                sp.dma_start(mod_rows[:, :].rearrange("b (m d) -> b m d", m=NMOD)[:, 3 * half:3 * half + 3, :],
                             modr[half]).then_inc(s_modw, 16)
                sp.wait_ge(s_modw, 16 * (half + 1))

            store_rows(0)
            load_rows_a(0)
            sp.dma_start(x_tiles[:, TPB:2 * TPB, :], x_view[1]).then_inc(s_x1, 16)
            for m in range(3, NMOD):
                load_wmod(m)
            for b in range(2, BATCH):
                sp.dma_start(x_tiles[:, b * TPB:(b + 1) * TPB, :], x_view[b]).then_inc(s_xrest, 16)
            store_rows(1)
            load_rows_b(0)
            for b in range(BATCH):
                sp.dma_start(rows_g[:, b, :], mod_row(5, b)).then_inc(s_rows_g, 16)
            sp.dma_start(shared_w[:, :], experts[0]).then_inc(s_shw, 16)
            sp.wait_ge(s_fill, 2)
            sp.dma_start(slots[:, :].rearrange("(p c) w -> p c w", p=P), tbl[:, 0:EXPERTS * SLOT_COLS, :]).then_inc(s_prefill, 16)
            sp.dma_start(h2_rows[TOKENS:ROWS, :], zrow[:, :]).then_inc(s_zero, 16)
            for a in acc:
                sp.dma_start(a[:, :].rearrange("(g p) d -> p g d", p=P),
                             zrow[:, :].unsqueeze(1).to_broadcast([P, ROWS // P, D])).then_inc(s_zero, 16)

            def next_rows_a(b):
                sp.wait_ge(s_woa, KC * b)
                sp.wait_ge(s_res, TPB * b)
                load_rows_a(b)

            next_rows_a(1)
            for b in range(BATCH):
                if b + 2 < BATCH:
                    next_rows_a(b + 2)
                sp.wait_ge(s_h2, TPB * (b + 1))
                sp.dma_start(h2_view[b], h2[:, :, :]).then_inc(s_h2w, 16)
                if b + 1 < BATCH:
                    load_rows_b(b + 1)

            def load_w(e):
                slot = (e & (WSLOTS - 1)) * WROW
                sp.dma_start(wqkv[:, bass.ds(slot, WROW)], experts[bass.ds(e, 1)].rearrange("o p w -> (o p) w")).then_inc(s_w, 16)

            for e in range(1, WSLOTS + 1):
                if e > 1:
                    sp.wait_ge(s_w, 16 * (e - 1))
                load_w(e)

            for done in s_scat:
                sp.wait_ge(done, 16 * TOPK * TILES // 2)
            for i in range(4):
                n = EXPERTS * SLOT_COLS // 4
                sp.dma_start(tbl[:, SLOT_COLS + i * n:SLOT_COLS + (i + 1) * n, :],
                             slots[:, :].rearrange("(p c) w -> p c w", p=P)[:, i * n:(i + 1) * n, :]).then_inc(s_tbl[i], 16)

            sp.wait_ge(s_plan, 2)
            with sp.Fori(WSLOTS + 1, EV) as e:
                done = sp.value_load(cum_i[0:1, bass.ds(e - WSLOTS, 1)], min_val=1, max_val=EXPERT_TILES)
                sp.wait_ge(s_d, done)
                apart(sp)
                sp.wait_ge(s_w, 16 * e - 16)
                apart(sp)
                load_w(e)

            sp.wait_ge(s_w, 16 * EXPERTS)
            used = rounds_used(sp)
            for added in s_sc:
                sp.wait_ge(added, used * (16 * ROUND // 2))
            apart(sp)
            for g in range(0, TILES, 2):
                sp.dma_start(sum_a[:, g:g + 2, :], acc_view[0][:, g:g + 2, :]).then_inc(s_fl[g // 2], 16)
                base, at = (front, TILES + g) if g < b_front else (wqkv, g - b_front)
                sp.dma_start(base[:, at * D:(at + 2) * D].rearrange("p (g d) -> p g d", g=2),
                             acc_view[1][:, g:g + 2, :]).then_inc(s_fl[g // 2], 16)
            for g in range(0, TILES, 2):
                sp.wait_ge(s_fo, g + 2)
                sp.dma_start(out_view[:, g:g + 2, :], x_tiles[:, g:g + 2, :]).then_inc(s_out, 16)
            sp.wait_ge(s_out, 16 * TILES // 2)

        @block.gpsimd
        def _(pool):
            pool.memset(tbl[:, :, :], 0).then_inc(s_pres, 1)
            pool.memset(zrow[:, :], 0.0).then_inc(s_fill, 1)
            pool.wait_ge(s_pres, 1)
            pool.iota(tbl[:, :, 0], pattern=[[0, DUMMY_COL + 1]], base=PAD_ID, channel_multiplier=1).then_inc(s_fill, 1)

            PRES = 2 * TPB

            def residual(b):
                t = Tally(s_pres, PRES * b + 1)
                for i in range(TPB):
                    g = x_at(b * TPB + i)
                    pool.wait_ge(s_rows_a, 48 * (b + 1))
                    pool.wait_ge(s_xn, TPB * b + i + 1)
                    if i:
                        pool.wait_ge(s_res, TPB * b + i)
                    elif b:
                        pool.wait_ge(s_res, TPB * b)
                    apart(pool)
                    a = t.mark(pool.tensor_tensor(pool_t, xn[:, i, :], rows_a[:, 1, :], ALU.mult))
                    c = t.mark(pool.tensor_tensor(g, g, rows_a[:, 2, :], ALU.add))
                    pool.wait_ge(s_pres, c)
                    apart(pool)
                    pool.tensor_tensor(g, g, pool_t, ALU.add).then_inc(s_res, 1)

            def scatter(b):
                for i in range(TPB):
                    pool.wait_ge(s_place, 2 * (b + 1 + (i if b == BATCH - 1 else 0)))
                    for k in range(TOPK):
                        pool.indirect_dma_start(
                            out=slots[:, :], out_offset=bass.IndirectOffsetOnAxis(ap=place[b % 2][:, i, k:k + 1], axis=0),
                            in_=pay[b % 2][:, i, k, :], in_offset=None).then_inc(s_scat[b % 2], 16)

            residual(0)
            residual(1)
            residual(2)
            finish_h2(pool, 0)
            pool.wait_ge(s_prefill, 16)
            scatter(0)
            finish_h2(pool, 1)
            residual(3)
            scatter(1)
            finish_h2(pool, 2)
            scatter(2)
            scatter(3)
            pool.wait_ge(s_tbl[0], 16)
            pool.wait_ge(s_plan, 2)
            pool.wait_ge(s_h2w, 16 * BATCH)
            pool.wait_ge(s_tpC, KC * BATCH)
            pool.wait_ge(s_zero, 48)

            def added(r, s, back):
                return 16 * (ROUND // 2) * r + 16 * (s // 2 - back // 2 + 1)

            def gather(t, r, s):
                col = pool.value_load(plan[0:1, 0, bass.ds(t, 1)], min_val=0, max_val=DUMMY_COL)
                if not (isinstance(t, int) and t < ROUND):
                    pool.wait_ge(s_sc[s % 2], added(r, s, ROUND))
                pool.tensor_copy(ids[s][:, :], tbl[:, bass.ds(col, 1), :].rearrange("p o w -> p (o w)")).then_inc(s_ids, 1)
                pool.wait_ge(s_ids, t + 1)
                if not (isinstance(t, int) and t < ROUND):
                    pool.wait_ge(s_T, t - ROUND + 1)
                apart(pool)
                pool.indirect_dma_start(
                    out=xg[s], out_offset=None, in_=h2_rows[:, :],
                    in_offset=bass.IndirectOffsetOnAxis(ap=ids[s][:, 0:1], axis=0)).then_inc(s_xg[s], 16)

            def add_rows(t, r, s):
                pool.wait_ge(s_y, t + 1)
                if not (isinstance(t, int) and t < 2):
                    pool.wait_ge(s_sc[s % 2], added(r, s, 2))
                apart(pool)
                pool.indirect_dma_start(
                    out=acc[s % 2][:, :], out_offset=bass.IndirectOffsetOnAxis(ap=ids[s][:, 0:1], axis=0),
                    in_=yb[s % YBUFS], in_offset=None, compute_op=ALU.add).then_inc(s_sc[s % 2], 16)

            for n in range(AHEAD):
                gather(n, 0, n)
            for i in range(1, 4):
                pool.wait_ge(s_tbl[i], 16)

            def round_pool(r):
                for s in range(ROUND):
                    n = s + AHEAD
                    gather(r * ROUND + n, r + n // ROUND, n % ROUND)
                    add_rows(r * ROUND + s, r, s)

            round_pool(0)
            used = rounds_used(pool)
            with pool.Fori(1, ROUNDS) as r:
                with pool.If(r < used):
                    round_pool(r)
            for n in range(AHEAD):
                pool.wait_ge(s_xg[n], used * 16 + 16)

            for g in range(TILES):
                pool.wait_ge(s_fl[g // 2], 32)
                pool.tensor_tensor(sum_a[:, g, :], sum_a[:, g, :], sum_b[g], ALU.add).then_inc(s_fs, 1)

        @block.scalar
        def _(sc):
            sc.wait_ge(s_small, 48)
            sc.activation(silu_c[:, :], cT[:, :], ACT.Silu).then_inc(s_silu, 1)

            def take_root(b, n):
                sc.wait_ge(s_var[n], b + 1)
                sc.activation(root[:, n, :], var[:, n, :], ACT.Sqrt).then_inc(s_root[n], 1)

            def norm1(b):
                take_root(b, 0)
                sc.wait_ge(s_mv, b + 1)
                if b:
                    sc.wait_ge(s_tpA, KC * b)
                    sc.wait_ge(s_res, TPB * b)
                for i in range(TPB):
                    sc.activation(xn[:, i, :], x_at(b * TPB + i), ACT.Identity, bias=shift[:, i:i + 1],
                                  scale=rstd[:, i:i + 1]).then_inc(s_xn, 1)

            def turned_h(b):
                sc.wait_ge(s_modv, 1)
                if b:
                    sc.wait_ge(s_q, KC * b)
                for c in range(KC):
                    sc.wait_ge(s_tpA, KC * b + c + 1)
                    at = c * BATCH + b
                    sc.activation(hT[:, c, :], bank[c % 2][:, :], ACT.Identity, bias=firstc[:, at:at + 1],
                                  scale=firstc[:, KC * BATCH + at:KC * BATCH + at + 1]).then_inc(s_hT, 1)

            def key_norms(b):
                for i in range(TPB):
                    sc.wait_ge(s_kro, TPB * b + i + 1)
                    if i == 0 and b:
                        sc.wait_ge(s_rn, b)
                    if i == 0 and b >= 3:
                        sc.wait_ge(s_shi, b - 2)
                    if i or b:
                        sc.wait_ge(s_ksq, TPB * b + i)
                    sc.activation(square_junk, kb, ACT.Square, accum_out=ksq[:, i:i + 1]).then_inc(s_ksq, 1)
                take_root(b, 2)

            def take_q(b):
                if b:
                    sc.wait_ge(s_o, TPB * b)
                for c in range(KC):
                    sc.wait_ge(s_q, KC * b + c + 1)
                    sc.activation(qT[:, c, :], bank[4 + c % 2][:, :], ACT.Identity,
                                  bias=bqc[:, c:c + 1]).then_inc(s_qT, 1)

            def norm2(b):
                if b:
                    sc.wait_ge(s_h2w, 16 * b)
                take_root(b, 1)
                sc.wait_ge(s_mv2, b + 1)
                for i in range(TPB):
                    sc.activation(h2[:, i, :], x_at(b * TPB + i), ACT.Identity, bias=shift2[:, i:i + 1],
                                  scale=rstd2[:, i:i + 1]).then_inc(s_xn2, 1)

            def turned_h2(b):
                if b:
                    sc.wait_ge(s_shg, b)
                for c in range(KC):
                    sc.wait_ge(s_tpC, KC * b + c + 1)
                    at = c * BATCH + b
                    sc.activation(h2T[:, c, :], bank[c % 2][:, :], ACT.Identity, scale=secondc[:, at:at + 1],
                                  bias=secondc[:, KC * BATCH + at:KC * BATCH + at + 1]).then_inc(s_h2T, 1)

            def exponents(b):
                if b:
                    sc.wait_ge(s_place, 2 * b)
                sc.wait_ge(s_top, b + 1)
                for i in range(TPB):
                    sc.activation(etop[:, i, :], topv[:, i, :], ACT.Exp, bias=ntop[:, i:i + 1],
                                  accum_out=esum[:, i:i + 1]).then_inc(s_ex, 1)
                if b:
                    sc.wait_ge(s_gate, b)
                sc.activation(esh[:, :], logit[:, :, 0], ACT.Exp, scale=-1.0).then_inc(s_ex, 1)

            def shared_silu(b):
                sc.wait_ge(s_shg, b + 1)
                if b:
                    sc.wait_ge(s_shi, b)
                sc.wait_ge(s_ksq, TPB * min(b + 3, BATCH))
                sc.activation(shared_act[:, :], bank[2][:, :], ACT.Silu).then_inc(s_shs, 1)

            norm1(0)
            turned_h(0)
            key_norms(0)
            norm1(1)
            take_q(0)
            turned_h(1)
            key_norms(1)
            for b in range(BATCH):
                if b + 2 < BATCH:
                    norm1(b + 2)
                norm2(b)
                if b + 1 < BATCH:
                    take_q(b + 1)
                if b + 2 < BATCH:
                    turned_h(b + 2)
                    key_norms(b + 2)
                if b == BATCH - 1:
                    shared_silu(b - 1)
                turned_h2(b)
                exponents(b)
                if b != BATCH - 2:
                    shared_silu(b)

            def take_x(t, s):
                sc.wait_ge(s_T, t + 1)
                if not (isinstance(t, int) and t < 4):
                    sc.wait_ge(s_G, t - 3)
                sc.activation(h2T[:, s % 4, :], bank[s % 2][:, :], ACT.Copy).then_inc(s_xT, 1)

            def silu(t, s):
                sc.wait_ge(s_G, t + 1)
                if not (isinstance(t, int) and t < 2):
                    sc.wait_ge(s_in, t - 1)
                sc.activation(act[s % 2], bank[2 + s % 2][:, 0:INNER], ACT.Silu).then_inc(s_sl, 1)

            def round_act(r):
                for s in range(ROUND):
                    take_x(r * ROUND + s + 1, s + 1)
                    silu(r * ROUND + s, s)

            take_x(0, 0)
            round_act(0)
            sc.wait_ge(s_plan, 2)
            used = rounds_used(sc)
            with sc.Fori(1, ROUNDS) as r:
                with sc.If(r < used):
                    round_act(r)

        @block.vector
        def _(ve):
            def step(t, ins):
                ve.wait_ge(t.sem, t.mark(ins))

            t0 = Tally(s_v)
            ve.memset(ones_bf[:, :], 1.0).then_inc(s_cst, 1)
            ve.memset(ones1[:, :], 1.0).then_inc(s_cst, 1)
            ve.memset(mask[:, :, 0:1], 1.0).then_inc(s_cst, 1)
            ve.memset(seen[:, TPB, :], 0.0).then_inc(s_cst, 1)

            def one_over_root(t, n, to):
                step(t, ve.reciprocal(to, root[:, n, :]))
                step(t, ve.tensor_tensor(corr[:, n, :], to, to, ALU.mult))
                step(t, ve.tensor_tensor(corr[:, n, :], corr[:, n, :], var[:, n, :], ALU.mult))
                step(t, ve.tensor_scalar(corr[:, n, :], corr[:, n, :], -0.5, 1.5, ALU.mult, ALU.add))

            def stats1(b):
                t = Tally(s_vl, (2 * TPB + 5) * b)
                if b:
                    ve.wait_ge(s_xn, TPB * b)
                    ve.wait_ge(s_mv, b)
                for i in range(TPB):
                    a = t.mark(ve.bn_stats(stats[:, i, :], x_at(b * TPB + i)))
                for i in range(TPB):
                    ve.wait_ge(s_vl, a - TPB + 1 + i)
                    apart(ve)
                    c = t.mark(ve.bn_aggr(mean_var[:, i, :], stats[:, i, :]))
                ve.wait_ge(s_vl, c)
                ve.tensor_scalar(var[:, 0, :], mean_var[:, :, 1], LN_EPS, None, ALU.add).then_inc(s_var[0], 1)
                ve.wait_ge(s_root[0], b + 1)
                one_over_root(t, 0, rstd[:, :])
                step(t, ve.tensor_tensor(rstd[:, :], rstd[:, :], corr[:, 0, :], ALU.mult))
                ve.scalar_tensor_tensor(out=shift[:, :], in0=mean_var[:, :, 0], scalar=-1.0, in1=rstd[:, :],
                                        op0=ALU.mult, op1=ALU.mult).then_inc(s_mv, 1)

            ve.wait_ge(s_x0, 16)
            stats1(0)
            ve.wait_ge(s_const, 16)
            ve.tensor_copy(tri_bf[:, :], const[:, C_TRI:C_TRI + P]).then_inc(s_cst, 1)

            ve.wait_ge(s_mod, 2)
            t0.mark(ve.tensor_copy(first[0], mod_bank[0]))
            step(t0, ve.tensor_scalar(first[1], mod_bank[1], 1.0, None, ALU.add))
            ve.nop().then_inc(s_first, 1)
            ve.wait_ge(s_modT, 1)
            ve.tensor_copy(firstc[:, :], bank[2][:, 0:2 * KC * BATCH]).then_inc(s_modv, 1)

            def away_from_zero(m, to):
                g = mod_bank[m]
                ve.wait_ge(s_mod, m + 1)
                t0.mark(ve.tensor_scalar(mod_t[0], g, 0.0, 2.0, ALU.is_ge, ALU.mult))
                step(t0, ve.tensor_scalar(mod_t[2], g, -1.0, 0.25, ALU.mult, ALU.max))
                step(t0, ve.tensor_tensor(mod_t[1], g, mod_t[2], ALU.max))
                step(t0, ve.tensor_scalar(mod_t[2], mod_t[0], -1.0, None, ALU.add))
                step(t0, ve.tensor_tensor(to, mod_t[2], mod_t[1], ALU.mult))

            away_from_zero(2, modr[0][:, 0, :])
            step(t0, ve.tensor_tensor(mod_t[0], bout_r, first[0], ALU.add))
            t0.mark(ve.tensor_tensor(modr[0][:, 1, :], modr[0][:, 0, :], first[1], ALU.mult))
            step(t0, ve.tensor_tensor(modr[0][:, 2, :], modr[0][:, 0, :], mod_t[0], ALU.mult))
            ve.nop().then_inc(s_modr, 1)

            VA = TPB * 6 + 4
            VQ = 4 + 1
            def keys_values(b):
                t = Tally(s_va, VA * b)
                for i in range(TPB):
                    ve.wait_ge(s_kv, 2 * TPB * b + 2 * i + 1)
                    if i or b:
                        ve.wait_ge(s_ksq, TPB * b + i)
                        ve.wait_ge(s_kvp, TPB * b + i)
                    t.mark(ve.tensor_tensor(kb, bank[2][:, :], bias_kv[:, 0, :], ALU.add))
                    ve.wait_ge(s_va, t.start + t.n)
                    ve.nop().then_inc(s_kvr, 1)
                    t.mark(ve.tensor_tensor(rope_t[:, 0:HALF], kb[:, HALF:ROT], ksin[:, i, 0:HALF], ALU.mult))
                    c = t.mark(ve.tensor_tensor(rope_t[:, HALF:ROT], kb[:, 0:HALF], ksin[:, i, HALF:ROT], ALU.mult))
                    ve.wait_ge(s_va, c)
                    step(t, ve.tensor_tensor(kb[:, 0:ROT], kb[:, 0:ROT], kcos[:, i, :], ALU.mult))
                    step(t, ve.tensor_tensor(kb[:, 0:ROT], kb[:, 0:ROT], rope_t[:, 0:ROT], ALU.add))
                    ve.nop().then_inc(s_kro, 1)
                    ve.wait_ge(s_kv, 2 * TPB * b + 2 * i + 2)
                    step(t, ve.tensor_tensor(vb, bank[3][:, :], bias_kv[:, 1, :], ALU.add))
                    ve.nop().then_inc(s_kvr, 1)
                    if i == 0 and b:
                        ve.wait_ge(s_as, b)
                    ve.tensor_tensor(kv[:, i, :], kb, vb, ALU.mult).then_inc(s_kvp, 1)
                ve.wait_ge(s_ksq, TPB * (b + 1))
                ve.tensor_scalar(var[:, 2, :], ksq[:, :], 1e-24, None, ALU.max).then_inc(s_var[2], 1)
                ve.wait_ge(s_root[2], b + 1)
                if b:
                    ve.wait_ge(s_rn, b)
                    ve.wait_ge(s_as, b)
                one_over_root(t, 2, krn[:, :])
                ve.tensor_tensor(krn[:, :], krn[:, :], corr[:, 2, :], ALU.mult).then_inc(s_rn, 1)
                assert t.n == VA, t.n

            def rope_queries(b):
                t = Tally(s_vq, VQ * b)
                ve.wait_ge(s_qT, KC * b + 2)
                if b:
                    ve.wait_ge(s_qro, 2 * b)
                t.mark(ve.tensor_tensor(rope_q[0], qT[:, 1, :], qsin[:, :], ALU.mult))
                c = t.mark(ve.tensor_tensor(rope_q[1], qT[:, 0, :], qsin[:, :], ALU.mult))
                ve.wait_ge(s_vq, c)
                t.mark(ve.tensor_tensor(qT[:, 0, :], qT[:, 0, :], qcos[:, :], ALU.mult))
                c = t.mark(ve.tensor_tensor(qT[:, 1, :], qT[:, 1, :], qcos[:, :], ALU.mult))
                ve.wait_ge(s_vq, c)
                ve.tensor_tensor(qT[:, 0, :], qT[:, 0, :], rope_q[0], ALU.subtract).then_inc(s_qro, 1)
                ve.tensor_tensor(qT[:, 1, :], qT[:, 1, :], rope_q[1], ALU.add).then_inc(s_qro, 1)
                assert t.n == VQ - 1, t.n

            def weigh_w_out(b):
                t = Tally(s_vq, VQ * b + VQ - 1)
                ve.wait_ge(s_as, b + 1)
                ve.wait_ge(s_rows_a, 48 * (b + 1))
                if b:
                    ve.wait_ge(s_woa, KC * b)
                step(t, ve.tensor_copy(asum[:, :], bank[6][:, 0:KC]))
                if b:
                    ve.wait_ge(s_o, TPB * b)
                for k in range(KC):
                    ve.scalar_tensor_tensor(out=woa[:, k, :], in0=wo[:, k, :], scalar=asum[:, k:k + 1],
                                            in1=rows_a[:, 0, :], op0=ALU.mult, op1=ALU.mult).then_inc(s_woa, 1)

            VD = 1 + TPB * TOPK + 6
            def read_ranks(b):
                t = Tally(s_vd, VD * b)
                if b >= 2:
                    ve.wait_ge(s_scat[b % 2], 16 * TOPK * TPB * (b // 2))
                ve.wait_ge(s_rk, TPB * (b + 1))
                step(t, ve.tensor_copy(rank_all[:, :, :].rearrange("p i e -> p (i e)"), bank[6][:, 8:8 + TPB * EV]))
                ve.nop().then_inc(s_rd, 1)
                return t

            def pick_ranks(t, i):
                for k in range(TOPK):
                    c = t.mark(ve.scalar_tensor_tensor(
                        out=pick[:, k, :], in0=const[:, C_IOTA:C_IOTA + EXPERTS], scalar=topif[:, i, k:k + 1],
                        in1=rank_all[:, i, 1:EV], op0=ALU.is_equal, op1=ALU.mult,
                        accum_out=rank_f[:, i, k:k + 1]))
                ve.wait_ge(s_vd, c)

            def make_pairs(t, b, i=None):
                at, n = (slice(None), TPB) if i is None else (slice(i, i + 1), 1)
                if i is None or i == 0:
                    t.mark(ve.reciprocal(rsum[:, :], esum[:, :]))
                step(t, ve.tensor_copy(rank_i[:, at, :], rank_f[:, at, :]))
                t.mark(ve.tensor_scalar(place_r[:, at, :], rank_i[:, at, :], P - 1, 10, ALU.bitwise_and, ALU.logical_shift_left))
                t.mark(ve.tensor_scalar(place_q[:, at, :], rank_i[:, at, :], 7, None, ALU.logical_shift_right))
                step(t, ve.tensor_scalar(place_e[:, at, :], idx_i[:, at, :], 4, None, ALU.logical_shift_left))
                step(t, ve.tensor_tensor(place_q[:, at, :], place_q[:, at, :], place_e[:, at, :], ALU.bitwise_or))
                ve.tensor_tensor(place[b % 2][:, at, :], place_q[:, at, :], place_r[:, at, :], ALU.bitwise_or).then_inc(s_place, 1)
                ids_at = C_TOK + b * TPB + (i or 0)
                t_ids = const[:, ids_at:ids_at + n].unsqueeze(2).to_broadcast([P, n, TOPK])
                ve.tensor_copy(pay[b % 2][:, at, :, 0], t_ids).then_inc(s_pay, 1)
                ve.wait_ge(s_pay, b + 1 + (i or 0))
                ve.tensor_tensor(pay[b % 2][:, at, :, 1].bitcast(F32), etop[:, at, :],
                                 rsum[:, at].unsqueeze(2).to_broadcast([P, n, TOPK]), ALU.mult).then_inc(s_place, 1)
                assert t.n == VD or i is not None, t.n

            VB = 3 * TPB + 5
            def add_x(b):
                t = Tally(s_vb, VB * b)
                early = b and b < BATCH - 1
                if early:
                    find = read_ranks(b - 1)
                    pick_ranks(find, 0)
                if b:
                    ve.wait_ge(s_mv2, b)
                    ve.wait_ge(s_xn2, TPB * b)
                for i in range(TPB):
                    g = x_at(b * TPB + i)
                    if early and i + 1 < TPB:
                        pick_ranks(find, i + 1)
                    elif early:
                        make_pairs(find, b - 1)
                    ve.wait_ge(s_o, TPB * b + i + 1)
                    ve.wait_ge(s_res, TPB * b + i + 1)
                    step(t, ve.tensor_tensor(g, bank[4 + i % 2][:, :], g, ALU.add))
                    ve.nop().then_inc(s_or, 1)
                    step(t, ve.bn_stats(stats2[:, i, :], g))
                    apart(ve)
                    step(t, ve.bn_aggr(mean_var2[:, i, :], stats2[:, i, :]))
                ve.tensor_scalar(var[:, 1, :], mean_var2[:, :, 1], LN_EPS, None, ALU.add).then_inc(s_var[1], 1)
                ve.wait_ge(s_root[1], b + 1)
                one_over_root(t, 1, rstd2[:, :])
                step(t, ve.tensor_tensor(rstd2[:, :], rstd2[:, :], corr[:, 1, :], ALU.mult))
                ve.scalar_tensor_tensor(out=shift2[:, :], in0=mean_var2[:, :, 0], scalar=-1.0,
                                        in1=rstd2[:, :], op0=ALU.mult, op1=ALU.mult).then_inc(s_mv2, 1)
                assert t.n == VB

            VC = 2 + 4 * TPB + 4
            def choose(b):
                t = Tally(s_vc, VC * b)
                if b:
                    ve.wait_ge(s_rk, TPB * b)
                    ve.wait_ge(s_ex, (TPB + 1) * b)
                step(t, ve.tensor_copy(seen[:, 0, :], seen[:, TPB, :]))
                ve.wait_ge(s_g, TPB * (b + 1))
                step(t, ve.tensor_copy(logit[:, :, :].rearrange("p i e -> p (i e)"), bank[7][:, 0:TPB * EV]))
                apart(ve)
                for i in range(TPB):
                    c = t.mark(ve.max(topv[:, i, :], logit[:, i, 1:EV]))
                ve.wait_ge(s_vc, c)
                ve.tensor_scalar(ntop[:, :], topv[:, :, 0], -1.0, None, ALU.mult).then_inc(s_top, 1)
                for i in range(TPB):
                    t.mark(ve.match_replace(replaced[:, i, :], topv[:, i, :], logit[:, i, 1:EV], NEG))
                ve.wait_ge(s_vc, t.start + t.n)
                step(t, ve.tensor_tensor(mask[:, :, 1:EV], replaced[:, :, :], logit[:, :, 1:EV], ALU.not_equal))
                for i in range(TPB):
                    step(t, ve.tensor_tensor(seen[:, i + 1, :], seen[:, i, :], mask[:, i, :], ALU.add))
                    ve.nop().then_inc(s_mask, 1)
                for i in range(TPB):
                    c = t.mark(ve.max_index(topi[:, i, :], topv[:, i, :], logit[:, i, 1:EV]))
                ve.wait_ge(s_vc, c)
                t.mark(ve.tensor_copy(topif[:, :, :], topi[:, :, :]))
                t.mark(ve.tensor_copy(idx_i[:, :, :], topi[:, :, :]))
                ve.wait_ge(s_ex, (TPB + 1) * (b + 1))
                step(t, ve.tensor_scalar(sh1[:, :], esh[:, :], 1.0, None, ALU.add))
                ve.reciprocal(gate_sh[:, b * TPB:(b + 1) * TPB], sh1[:, :]).then_inc(s_gate, 1)
                assert t.n == VC, t.n

            def shared_inner(b):
                ve.wait_ge(s_shs, b + 1)
                if b:
                    ve.wait_ge(s_shd, TPB * b)
                ve.tensor_tensor(shared_inter[:, :], bank[3][:, :], shared_act[:, :], ALU.mult).then_inc(s_shi, 1)

            def shared_sum(b, tiles=range(TPB)):
                ve.wait_ge(s_rows_g, 16 * BATCH)
                for i in tiles:
                    g = b * TPB + i
                    ve.wait_ge(s_shd, g + 1)
                    if g:
                        ve.wait_ge(s_shx, g)
                    ve.scalar_tensor_tensor(out=shared_out, in0=bank[2 + i % 2][:, :], scalar=gate_sh[:, g:g + 1],
                                            in1=rows_g[:, b, :], op0=ALU.mult, op1=ALU.mult).then_inc(s_sht, 1)
                    ve.wait_ge(s_sht, g + 1)
                    ve.tensor_tensor(x_at(g), x_at(g), shared_out, ALU.add).then_inc(s_shx, 1)

            ve.wait_ge(s_att, 16 * 3)
            keys_values(0)
            ve.wait_ge(s_x1, 16)
            stats1(1)
            away_from_zero(5, modr[1][:, 2, :])
            t0.mark(ve.tensor_scalar(modr[1][:, 0, :], mod_bank[4], 1.0, None, ALU.add))
            step(t0, ve.tensor_copy(modr[1][:, 1, :], mod_bank[3]))
            ve.nop().then_inc(s_modr, 1)
            ve.wait_ge(s_late, 16 * 4)
            rope_queries(0)
            ve.wait_ge(s_modT, 2)
            ve.tensor_copy(secondc[:, :], bank[0][:, 0:2 * KC * BATCH]).then_inc(s_modv, 1)
            weigh_w_out(0)
            keys_values(1)
            ve.wait_ge(s_xrest, 16 * (BATCH - 2))
            for b in range(BATCH):
                if b + 2 < BATCH:
                    stats1(b + 2)
                add_x(b)
                if b == BATCH - 1:
                    shared_inner(b - 1)
                if b + 1 < BATCH:
                    rope_queries(b + 1)
                if b == BATCH - 2:
                    shared_sum(b - 1, range(0, 2))
                    choose(b)
                    shared_sum(b - 1, range(2, TPB))
                elif b and b < BATCH - 1:
                    shared_sum(b - 1)
                if b + 1 < BATCH:
                    weigh_w_out(b + 1)
                if b + 2 < BATCH:
                    keys_values(b + 2)
                if b != BATCH - 2:
                    choose(b)
                if b >= BATCH - 2:
                    find = read_ranks(b)
                    for i in range(TPB):
                        pick_ranks(find, i)
                        if b == BATCH - 1:
                            make_pairs(find, b, i)
                    if b < BATCH - 1:
                        make_pairs(find, b)
                if b == BATCH - 1:
                    finish_h2(ve, b)
                    shared_sum(b - 1)
                if b != BATCH - 2:
                    shared_inner(b)

            ve.wait_ge(s_cnt, 1)
            step(t0, ve.tensor_copy(count_i[:, :], bank[6][0:EV, 0:1]))
            step(t0, ve.tensor_scalar(count_f[:, :], count_i[:, :], float(P - 1), None, ALU.add))
            step(t0, ve.tensor_copy(count_i[:, :], count_f[:, :]))
            step(t0, ve.tensor_scalar(tiles_i[:, :], count_i[:, :], 7, None, ALU.logical_shift_right))
            step(t0, ve.tensor_copy(tiles_f[:, :], tiles_i[:, :]))
            step(t0, ve.tensor_scalar(tiles_f[:, :], tiles_f[:, :], 1.0, None, ALU.max))
            step(t0, ve.memset(tiles_f[0:1, :], 0.0))
            step(t0, ve.tensor_scalar(col_step[:, :], tiles_f[:, :], -1.0, float(SLOT_COLS), ALU.mult, ALU.add))
            ve.tensor_copy(tiles_f[:, :], tiles_f[:, :]).then_inc(s_ntile, 1)
            ve.wait_ge(s_cum, 1)
            step(t0, ve.tensor_copy(cum[:, :], bank[6][0:EV, 1:2]))
            t0.mark(ve.tensor_copy(cum_i[:, :], bank[6][0:1, 8:8 + EV]))
            step(t0, ve.tensor_scalar(rounds_f[:, :], bank[6][0:1, 8 + EV - 1:8 + EV], -1.0, None, ALU.add))
            step(t0, ve.tensor_copy(rounds_i[:, :], rounds_f[:, :]))
            step(t0, ve.tensor_scalar(rounds_i[:, :], rounds_i[:, :], ROUND.bit_length() - 1, None, ALU.logical_shift_right))
            ve.tensor_scalar(past[:, :], const[0:EV, C_FLAT:C_FLAT + PLAN], cum[:, 0:1], None, ALU.is_ge).then_inc(s_past, 1)
            ve.wait_ge(s_flat, 1)
            t0.mark(ve.tensor_tensor(plan_f[:, 0, :], bank[7][0:1, 0:PLAN], const[0:1, C_FLAT:C_FLAT + PLAN], ALU.add))
            step(t0, ve.tensor_scalar(plan_f[:, 1, :], bank[7][0:1, 256:256 + PLAN], float(EV - 1), None, ALU.min))
            step(t0, ve.tensor_scalar(plan_f[:, 0, :], plan_f[:, 0, :], float(DUMMY_COL), None, ALU.min))
            ve.tensor_copy(plan[:, 0, :], plan_f[:, 0, :]).then_inc(s_plan, 1)
            ve.tensor_copy(plan[:, 1, :], plan_f[:, 1, :]).then_inc(s_plan, 1)

            shared_sum(BATCH - 1)

            def gated(t, s):
                ve.wait_ge(s_sl, t + 1)
                if not (isinstance(t, int) and t < 2):
                    ve.wait_ge(s_I, t - 1)
                ve.scalar_tensor_tensor(out=inter[s % 2], in0=bank[2 + s % 2][:, INNER:GU],
                                        scalar=ids[s][:, 1:2].bitcast(F32), in1=act[s % 2],
                                        op0=ALU.mult, op1=ALU.mult).then_inc(s_in, 1)

            def take_y(t, r, s):
                ve.wait_ge(s_d, t + 1)
                if not (isinstance(t, int) and t < YBUFS):
                    ve.wait_ge(s_sc[s % 2], 16 * (ROUND // 2) * r + 16 * (s // 2 - YBUFS // 2 + 1))
                ve.tensor_copy(yb[s % YBUFS], bank[4 + s % 2][:, :]).then_inc(s_y, 1)

            def take_inter(t, s):
                ve.wait_ge(s_I, t + 1)
                if not (isinstance(t, int) and t < 2):
                    ve.wait_ge(s_d, t - 1)
                ve.tensor_copy(iT[s % 2], bank[6 + s % 2][:, 0:P]).then_inc(s_iT, 1)

            def round_ve(r):
                for s in range(ROUND):
                    t = r * ROUND + s
                    if not (isinstance(t, int) and t < 2):
                        take_y(t - 2, r if s >= 2 else r - 1, (s - 2) % ROUND)
                    if not (isinstance(t, int) and t < 1):
                        take_inter(t - 1, (s - 1) % 2)
                    gated(t, s)

            round_ve(0)
            ve.wait_ge(s_plan, 2)
            used = rounds_used(ve)
            with ve.Fori(1, ROUNDS) as r:
                with ve.If(r < used):
                    round_ve(r)
            take_y(used * ROUND - 2, used - 1, ROUND - 2)
            take_inter(used * ROUND - 1, ROUND - 1)
            take_y(used * ROUND - 1, used - 1, ROUND - 1)

            for g in range(TILES):
                ve.wait_ge(s_fs, g + 1)
                ve.tensor_tensor(sum_a[:, g, :], sum_a[:, g, :], rows_g[:, g // TPB, :], ALU.mult).then_inc(s_fm, 1)
                ve.wait_ge(s_fm, g + 1)
                ve.tensor_tensor(x_at(g), x_at(g), sum_a[:, g, :], ALU.add).then_inc(s_fo, 1)

        @block.tensor
        def _(pe):
            pe.wait_ge(s_silu, 1)

            def modulate(m):
                pe.wait_ge(s_wmod[m], 16)
                for k in range(KC):
                    mm = pe.matmul(mod_bank[m], silu_c[:, k * BATCH:(k + 1) * BATCH], wmod[m][:, k, :],
                                   start=(k == 0), stop=(k == KC - 1))
                mm.then_inc(s_mod, 1)

            modulate(0)
            modulate(1)
            pe.wait_ge(s_first, 1)
            pe.wait_ge(s_const, 16)
            for m in range(2):
                for c in range(KC):
                    at = (m * KC + c) * BATCH
                    mm = pe.transpose(bank[2][:, at:at + BATCH], first[m][:, c * P:(c + 1) * P], ident[0:BATCH, 0:BATCH])
            mm.then_inc(s_modT, 1)

            def turn_h(b):
                for c in range(KC):
                    if c < 2 and b >= 3:
                        pe.wait_ge(s_h2T, KC * (b - 2))
                    if c < 2 and b:
                        pe.wait_ge(s_hT, KC * b)
                    if c >= 2:
                        pe.wait_ge(s_hT, KC * b + c - 1)
                    for i in range(TPB):
                        if c == 0:
                            pe.wait_ge(s_xn, TPB * b + i + 1)
                        mm = pe.transpose(bank[c % 2][:, i * P:(i + 1) * P], xn[:, i, c * P:(c + 1) * P], ident)
                    mm.then_inc(s_tpA, 1)

            def keys_values(b):
                pe.wait_ge(s_hT, KC * (b + 1))
                if b >= 3:
                    pe.wait_ge(s_sht, TPB * (b - 2))
                for i in range(TPB):
                    for j in range(2):
                        if i or b:
                            pe.wait_ge(s_kvr, 2 * TPB * b + 2 * (i - 1) + j + 1)
                        for k in range(KC):
                            mm = pe.matmul(bank[2 + j][:, :], hT[:, k, i * P:(i + 1) * P],
                                           win[:, k, (j + 1) * D:(j + 2) * D], start=(k == 0), stop=(k == KC - 1))
                        mm.then_inc(s_kv, 1)

            def queries(b):
                for c in range(KC):
                    if c < 2 and b:
                        pe.wait_ge(s_or, TPB * b)
                    if c >= 2:
                        pe.wait_ge(s_qT, KC * b + c - 1)
                    for k in range(KC):
                        mm = pe.matmul(bank[4 + c % 2][:, :], win[:, k, c * P:(c + 1) * P], hT[:, k, :],
                                       start=(k == 0), stop=(k == KC - 1))
                    mm.then_inc(s_q, 1)

            def sum_keys(b):
                pe.wait_ge(s_rn, b + 1)
                pe.wait_ge(s_kvp, TPB * (b + 1))
                if b:
                    pe.wait_ge(s_woa, KC * b)
                if b >= 2:
                    pe.wait_ge(s_rd, b - 1)
                for c in range(KC):
                    for i in range(TPB):
                        mm = pe.matmul(bank[6][:, c:c + 1], kv[:, i, c * P:(c + 1) * P], krn[:, i:i + 1],
                                       start=(i == 0), stop=(i == TPB - 1))
                mm.then_inc(s_as, 1)

            def project(b):
                pe.wait_ge(s_qT, KC * (b + 1))
                pe.wait_ge(s_qro, 2 * (b + 1))
                pe.wait_ge(s_woa, KC * (b + 1))
                for i in range(TPB):
                    if i >= 2:
                        pe.wait_ge(s_or, TPB * b + i - 1)
                    for k in range(KC):
                        mm = pe.matmul(bank[4 + i % 2][:, :], qT[:, k, i * P:(i + 1) * P], woa[:, k, :],
                                       start=(k == 0), stop=(k == KC - 1))
                    mm.then_inc(s_o, 1)

            def turn_h2(b):
                pe.wait_ge(s_xn2, TPB * (b + 1))
                pe.wait_ge(s_hT, KC * min(b + 3, BATCH))
                if b:
                    pe.wait_ge(s_h2T, KC * b)
                for c in range(KC):
                    if c >= 2:
                        pe.wait_ge(s_h2T, KC * b + c - 1)
                    for i in range(TPB):
                        mm = pe.transpose(bank[c % 2][:, i * P:(i + 1) * P], h2[:, i, c * P:(c + 1) * P], ident)
                    mm.then_inc(s_tpC, 1)

            def score(b):
                pe.wait_ge(s_h2T, KC * (b + 1))
                if b:
                    pe.wait_ge(s_top, b)
                for i in range(TPB):
                    for k in range(KC):
                        mm = pe.matmul(bank[7][:, i * EV:(i + 1) * EV], h2T[:, k, i * P:(i + 1) * P], gate_w[:, k, :],
                                       start=(k == 0), stop=(k == KC - 1))
                    mm.then_inc(s_g, 1)

            def shared_gate_up(b):
                pe.wait_ge(s_shw, 16)
                pe.wait_ge(s_kvr, 2 * TPB * min(b + 3, BATCH))
                if b:
                    pe.wait_ge(s_sht, TPB * b)
                for j in range(2):
                    for k in range(KC):
                        at = k * GU + j * INNER
                        mm = pe.matmul(bank[2 + j][:, :], shared_w[:, at:at + INNER], h2T[:, k, :],
                                       start=(k == 0), stop=(k == KC - 1))
                mm.then_inc(s_shg, 1)

            def shared_down(b, tiles=range(TPB)):
                pe.wait_ge(s_shi, b + 1)
                for i in tiles:
                    if i >= 2:
                        pe.wait_ge(s_sht, TPB * b + i - 1)
                    pe.matmul(bank[2 + i % 2][:, :], shared_inter[:, i * P:(i + 1) * P], shared_w[:, KC * GU:WROW],
                              start=True, stop=True).then_inc(s_shd, 1)

            def rank(b):
                pe.wait_ge(s_woa, KC * min(b + 2, BATCH))
                if b:
                    pe.wait_ge(s_rd, b)
                for i in range(TPB):
                    pe.wait_ge(s_mask, TPB * b + i + 1)
                    o = bank[6][:, 8 + i * EV:8 + (i + 1) * EV]
                    pe.matmul(o, tri_bf[:, :], mask[:, i, :], start=True, stop=False)
                    pe.matmul(o, ones_bf[:, :], seen[:, i, :], start=False, stop=True).then_inc(s_rk, 1)

            turn_h(0)
            modulate(2)
            pe.wait_ge(s_win[1], 16)
            keys_values(0)
            for m in range(3, NMOD):
                modulate(m)
            pe.wait_ge(s_modr, 1)
            pe.wait_ge(s_win[0], 16)
            queries(0)
            pe.wait_ge(s_modr, 2)
            for m in range(2):
                for c in range(KC):
                    at = (m * KC + c) * BATCH
                    mm = pe.transpose(bank[0][:, at:at + BATCH], modr[1][:, m, c * P:(c + 1) * P], ident[0:BATCH, 0:BATCH])
            mm.then_inc(s_modT, 1)
            sum_keys(0)
            pe.wait_ge(s_modv, 2)
            turn_h(1)
            keys_values(1)
            pe.wait_ge(s_late, 16 * 4)
            pe.wait_ge(s_cst, 5)
            for b in range(BATCH):
                project(b)
                if b == BATCH - 1:
                    shared_gate_up(b - 1)
                if b + 1 < BATCH:
                    queries(b + 1)
                if b == BATCH - 2:
                    shared_down(b - 1, range(0, 2))
                    turn_h2(b)
                    score(b)
                    shared_down(b - 1, range(2, TPB))
                elif b and b < BATCH - 1:
                    shared_down(b - 1)
                if b + 1 < BATCH:
                    sum_keys(b + 1)
                if b + 2 < BATCH:
                    turn_h(b + 2)
                    keys_values(b + 2)
                if b != BATCH - 2:
                    turn_h2(b)
                    score(b)
                if b >= BATCH - 2:
                    rank(b)
                if b == BATCH - 1:
                    shared_down(b - 1)
                if b != BATCH - 2:
                    shared_gate_up(b)
                if b < BATCH - 2:
                    rank(b)

            pe.wait_ge(s_rd, BATCH)
            pe.matmul(bank[6][0:EV, 0:1], seen[:, TPB, :], ones_bf[:, 0:1], start=True, stop=True).then_inc(s_cnt, 1)
            pe.wait_ge(s_ntile, 1)
            pe.matmul(bank[6][0:EV, 1:2], const[0:EV, C_TRI65:C_TRI65 + EV], tiles_f[:, :], start=True, stop=True)
            pe.matmul(bank[6][0:1, 8:8 + EV], tiles_f[:, :], const[0:EV, C_TRI65:C_TRI65 + EV],
                      start=True, stop=True).then_inc(s_cum, 1)
            pe.wait_ge(s_past, 1)
            pe.matmul(bank[7][0:1, 0:PLAN], col_step[:, :], past[:, :], start=True, stop=True)
            pe.matmul(bank[7][0:1, 256:256 + PLAN], ones1[0:EV, :], past[:, :], start=True, stop=True).then_inc(s_flat, 1)
            shared_down(BATCH - 1)

            def turn(t, r, s):
                pe.wait_ge(s_xg[s], 16 * (r + 1))
                if not (isinstance(t, int) and t < 2):
                    pe.wait_ge(s_xT, t - 1)
                for k in range(KC):
                    mm = pe.transpose(bank[s % 2][:, k * P:(k + 1) * P], xg[s][:, k * P:(k + 1) * P], ident)
                mm.then_inc(s_T, 1)

            def gate_up(t, s, w):
                for k in range(KC):
                    mm = pe.matmul(bank[2 + s % 2][:, 0:GU], xT[s % 4][:, k, :], wqkv[:, bass.ds(w + k * GU, GU)],
                                   start=(k == 0), stop=(k == KC - 1))
                mm.then_inc(s_G, 1)

            def down(t, s, w):
                pe.wait_ge(s_iT, t + 1)
                if not (isinstance(t, int) and t < 2):
                    pe.wait_ge(s_y, t - 1)
                pe.matmul(bank[4 + s % 2][:, :], iT[s % 2], wqkv[:, bass.ds(w + KC * GU, D)],
                          start=True, stop=True).then_inc(s_d, 1)

            def turn_inter(t, s):
                pe.wait_ge(s_in, t + 1)
                if not (isinstance(t, int) and t < 2):
                    pe.wait_ge(s_iT, t - 1)
                pe.transpose(bank[6 + s % 2][:, 0:P], inter[s % 2], ident).then_inc(s_I, 1)

            def expert_of(t):
                e = pe.value_load(plan[0:1, 1, bass.ds(t, 1)], min_val=1, max_val=EXPERTS)
                return (e & (WSLOTS - 1)) * WROW, e * 16

            def round_pe(r):
                again = not isinstance(r, int)
                w, loaded = {}, {}
                w[0], loaded[0] = expert_of(r * ROUND)
                for s in range(ROUND):
                    t = r * ROUND + s
                    turn(t + 1, r + (s + 1) // ROUND, (s + 1) % ROUND)
                    pe.wait_ge(s_w, loaded[s])
                    pe.wait_ge(s_xT, t + 1)
                    if again or t >= 1:
                        turn_inter(t - 1, (s - 1) % 2)
                    gate_up(t, s, w[s])
                    if again and s == 0:
                        w[-1] = expert_of(t - 1)[0]
                    if s + 1 < ROUND:
                        w[s + 1], loaded[s + 1] = expert_of(t + 1)
                    if again or t >= 1:
                        down(t - 1, (s - 1) % 2, w[s - 1])

            pe.wait_ge(s_plan, 2)
            pe.wait_ge(s_shx, TILES)
            turn(0, 0, 0)
            round_pe(0)
            used = rounds_used(pe)
            with pe.Fori(1, ROUNDS) as r:
                with pe.If(r < used):
                    round_pe(r)
            end = used * ROUND
            turn_inter(end - 1, 1)
            down(end - 1, 1, expert_of(end - 1)[0])


def _constants():
    c = np.zeros((P, CONSTS), np.float32)
    c[:, C_ID:C_ID + P] = np.eye(P)
    c[:, C_TRI:C_TRI + P] = np.triu(np.ones((P, P)), 1)
    c[:EV, C_TRI65:C_TRI65 + EV] = np.triu(np.ones((EV, EV)))
    c[:, C_IOTA:C_IOTA + EXPERTS] = np.arange(EXPERTS)
    c[:, C_FLAT:C_FLAT + PLAN] = np.arange(PLAN)
    c[:, C_TOK:C_TOK + TILES] = np.arange(TILES)[None, :] * P + np.arange(P)[:, None]
    inv = (1.0 / np.float32(10000.0) ** (np.arange(0, ROT, 2, dtype=np.float32) / np.float32(ROT))).astype(np.float32)
    freqs = np.arange(SEQ, dtype=np.float32)[:, None] * inv[None, :]
    cos = np.cos(freqs.astype(np.float64)).astype(np.float32)
    sin = np.sin(freqs.astype(np.float64)).astype(np.float32)
    by_row = lambda a: np.ascontiguousarray(a.reshape(TPB, P, ROT).transpose(1, 0, 2))
    rows = np.stack([by_row(np.concatenate([cos, cos], 1)), by_row(np.concatenate([-sin, sin], 1))])
    cols = np.ascontiguousarray(np.stack([cos.T, sin.T]))
    return c, rows, cols


def _layout(i):
    g = {n: np.asarray(a) for n, a in i.items()}
    order = np.concatenate([np.arange(0, ROT, 2), np.arange(1, ROT, 2), np.arange(ROT, D)])
    qkv = np.concatenate([order, D + order, 2 * D + order])
    chunks = lambda a: np.ascontiguousarray(a.reshape(KC, P, -1).transpose(1, 0, 2))
    w_in = chunks(g["L0_attn_W_in"][qkv].T)
    b_in = g["L0_attn_b_in"][qkv]
    w_out = chunks(g["L0_attn_W_out"].T[order])
    gates = chunks(np.concatenate([g["L0_ffn_sh_gate1_w"], g["L0_ffn_gate_w"]]).T)
    gu = np.concatenate([np.concatenate([g["L0_ffn_sh_gate_w"], g["L0_ffn_sh_up_w"]])[None], g["L0_ffn_gu_w"]])
    gu = gu.transpose(0, 2, 1).reshape(EV, KC, P, GU).transpose(0, 2, 1, 3).reshape(EV, P, KC * GU)
    dp = np.concatenate([g["L0_ffn_sh_down_w"][None], g["L0_ffn_dp_w"]]).transpose(0, 2, 1)
    experts = np.ascontiguousarray(np.concatenate([gu, dp], 2))
    c_t = np.ascontiguousarray(g["L0_c"].reshape(BATCH, KC, P).transpose(2, 1, 0).reshape(P, -1))
    w_mod = chunks(g["L0_wmod"])
    c, rows, cols = _constants()
    return {
        "x": np.ascontiguousarray(g["L0_attn_X"].reshape(TOKENS, D)), "w_in": w_in,
        "b_col": np.ascontiguousarray(b_in[:D].reshape(KC, P).T), "b_row": np.ascontiguousarray(b_in[D:].reshape(2, D)),
        "w_out": w_out, "b_out": g["L0_attn_b_out"].reshape(1, D), "gates": gates, "experts": experts, "c_t": c_t, "w_mod": w_mod,
        "tables": c, "rope_rows": rows, "rope_cols": cols,
    }


def kernel(**inputs):
    import concourse.bacc as _bacc
    from concourse.bass_utils import run_bass_kernel_spmd as _run

    nc = _bacc.Bacc("TRN2", target_bir_lowering=False, num_devices=1)
    arrays, args = {}, []
    for name, a in _layout(inputs).items():
        arrays[f"in_{name}"] = a
        args.append(nc.dram_tensor(f"in_{name}", a.shape, mybir.dt.from_np(a.dtype), kind="ExternalInput").ap())
    out = nc.dram_tensor("out_dram", (TOKENS, D), F32, kind="ExternalOutput").ap()
    build(nc, *args, out)
    r = _run(nc, [arrays], core_ids=[0])
    return r.results[0]["out_dram"].reshape(BATCH, SEQ, D)
```
